# Optimizing a Trainium2 kernel written in Bass

```python
import numpy as np
import jax
import jax.numpy as jnp

def _softmax(x, axis=-1):
    return jax.nn.softmax(x, axis=axis)

def _gelu(x):
    return jax.nn.gelu(x, approximate=True)

def _silu(x):
    return jax.nn.silu(x)

def _sigmoid(x):
    return jax.nn.sigmoid(x)

def _layernorm(x, axis=-1, eps=1e-05):
    m = jnp.mean(x, axis=axis, keepdims=True)
    v = jnp.var(x, axis=axis, keepdims=True)
    return (x - m) / jnp.sqrt(v + eps)

def _scatter_add(tgt, idx, src, axis=0):
    return tgt.at[idx].add(src)

def _segment_sum(src, seg, n):
    return jax.ops.segment_sum(src, seg, n)
kernel_name = 'mk_adj_resnorm_d4_adj_r2_69b877'

def setup_inputs(seed: int=0):
    np.random.seed(seed)
    _w = jnp.asarray

    def _rec_inputs():
        import jax
        import jax.numpy as jnp
        _gk = jax.random.key(seed)
        x = -0.0005207 + 1.001 * jax.random.normal(jax.random.fold_in(_gk, 1), (16, 512, 128), jnp.float32)
        _a = jax.random.bernoulli(jax.random.fold_in(_gk, 2), 0.015625, (16, 512, 512))
        _a = jnp.logical_or(_a, jnp.swapaxes(_a, -1, -2))
        _a = jnp.logical_or(_a, jnp.eye(512, dtype=bool))
        _af = _a.astype(jnp.float32)
        _af = _af * jax.random.uniform(jax.random.fold_in(_gk, 3), (16, 512, 512), jnp.float32, 0.05, 1)
        adj = _af
        return (x, adj)
    x, adj = _rec_inputs()

    def _L0_gnn_setup():
        import jax, jax.numpy as jnp
        import numpy as np
        B, N, F = (8, 512, 128)
        OUT, REL = (128, 16)
        NADJ = 7
        key = jax.random.key(seed)
        k0, k1, k2, k3, k4 = jax.random.split(key, 5)
        features = jax.random.normal(k0, (B, N, F), dtype=jnp.float32)
        A1 = jax.random.uniform(k1, (B, N, N), dtype=jnp.float32)
        A2 = jax.random.uniform(k2, (B, N, N), dtype=jnp.float32)
        W = jax.random.normal(k3, (NADJ, F + REL, OUT), dtype=jnp.float32) * 0.05
        W_edges = jnp.ones((NADJ, REL), dtype=jnp.float32)
        b = jax.random.uniform(k4, (N, OUT), dtype=jnp.float32, minval=-0.05, maxval=0.05)
        return {'features': features, 'A1': A1, 'A2': A2, 'W': W, 'W_edges': W_edges, 'b': b}
    _L0_gnn_all = _L0_gnn_setup()
    _L0_gnn_in = {k: v for k, v in _L0_gnn_all.items() if k in ('W', 'W_edges', 'b')}
    del _L0_gnn_all

    def _L1_gnn_setup():
        import jax, jax.numpy as jnp
        import numpy as np
        BN_EPS = 0.001
        LRELU_ALPHA = 0.3

        def _bn(x, gamma, beta, mean, var):
            return gamma * (x - mean) * jax.lax.rsqrt(var + BN_EPS) + beta

        def _gcn(x, adj, w, b):
            xw = jnp.einsum('bnf,fc->bnc', x, w)
            return jnp.einsum('bnm,bmc->bnc', adj, xw) + b

        def _lrelu(x):
            return jnp.where(x >= 0, x, LRELU_ALPHA * x)
        key = jax.random.key(seed)
        ks = jax.random.split(key, 12)
        B, N, C = (16, 512, 128)
        x = jax.random.normal(ks[0], (B, N, C), dtype=jnp.float32)
        adj = jax.random.uniform(ks[1], (B, N, N), dtype=jnp.float32) / N
        s = 1.0 / np.sqrt(C)
        return {'x': x, 'adj': adj, 'bn1_gamma': jnp.ones((C,), jnp.float32), 'bn1_beta': jnp.zeros((C,), jnp.float32), 'bn1_mean': jax.random.normal(ks[2], (C,), jnp.float32) * 0.1, 'bn1_var': jax.random.uniform(ks[3], (C,), jnp.float32) + 0.5, 'w1': jax.random.normal(ks[4], (C, C), jnp.float32) * s, 'b1': jnp.zeros((C,), jnp.float32), 'bn2_gamma': jnp.ones((C,), jnp.float32), 'bn2_beta': jnp.zeros((C,), jnp.float32), 'bn2_mean': jax.random.normal(ks[5], (C,), jnp.float32) * 0.1, 'bn2_var': jax.random.uniform(ks[6], (C,), jnp.float32) + 0.5, 'w2': jax.random.normal(ks[7], (C, C), jnp.float32) * s, 'b2': jnp.zeros((C,), jnp.float32), 'w_skip': jax.random.normal(ks[8], (C, C), jnp.float32) * s, 'b_skip': jnp.zeros((C,), jnp.float32)}
    _L1_gnn_all = _L1_gnn_setup()
    _L1_gnn_in = {k: v for k, v in _L1_gnn_all.items() if k in ('bn1_gamma', 'bn1_beta', 'bn1_mean', 'bn1_var', 'w1', 'b1', 'bn2_gamma', 'bn2_beta', 'bn2_mean', 'bn2_var', 'w2', 'b2', 'w_skip', 'b_skip')}
    del _L1_gnn_all

    def _L2_gnn_setup():
        import jax, jax.numpy as jnp
        import numpy as np
        D_IN = 128
        D_HID = 256
        key = jax.random.key(seed)
        k1, k2, k3, k4, k5, k6 = jax.random.split(key, 6)
        x = jax.random.normal(k1, (8, 2048, D_IN), dtype=jnp.float32)
        adj = jax.random.uniform(k2, (8, 2048, 2048), dtype=jnp.float32)
        s1 = 1.0 / np.sqrt(D_IN)
        s2 = 1.0 / np.sqrt(D_HID)
        W1 = jax.random.uniform(k3, (D_IN, D_HID), dtype=jnp.float32, minval=-s1, maxval=s1)
        b1 = jax.random.uniform(k4, (D_HID,), dtype=jnp.float32, minval=-s1, maxval=s1)
        W2 = jax.random.uniform(k5, (D_HID, D_IN), dtype=jnp.float32, minval=-s2, maxval=s2)
        b2 = jax.random.uniform(k6, (D_IN,), dtype=jnp.float32, minval=-s2, maxval=s2)
        eps = jnp.zeros((1,), dtype=jnp.float32)
        return {'x': x, 'adj': adj, 'eps': eps, 'W1': W1, 'b1': b1, 'W2': W2, 'b2': b2}
    _L2_gnn_all = _L2_gnn_setup()
    _L2_gnn_in = {k: v for k, v in _L2_gnn_all.items() if k in ('eps', 'W1', 'b1', 'W2', 'b2')}
    del _L2_gnn_all

    def _L3_gnn_setup():
        import jax, jax.numpy as jnp
        import numpy as np
        from jax import lax
        DIM = 128
        EPS = 1e-05

        def _bn(h, g, b, m, v):
            scale = g / jnp.sqrt(v + EPS)
            return h * scale[None, :, None] + (b - m * scale)[None, :, None]

        def _conv1d(h, w, pad):
            return lax.conv_general_dilated(h, w, window_strides=(1,), padding=[(pad, pad)], dimension_numbers=('NCH', 'OIH', 'NCH'))
        key = jax.random.key(seed)
        ks = jax.random.split(key, 16)
        bs, n, d = (16, 1024, DIM)
        s = 0.05
        return {'x': jax.random.normal(ks[0], (bs, n, d), jnp.float32), 'mask': jnp.ones((bs, n, n), jnp.float32), 'w_se': jax.random.normal(ks[1], (3, d), jnp.float32) * s, 'b_se': jnp.zeros((3,), jnp.float32), 'conv1_w': jax.random.normal(ks[2], (d, d, 1), jnp.float32) * s, 'bn1_g': jnp.ones((d,), jnp.float32), 'bn1_b': jnp.zeros((d,), jnp.float32), 'bn1_m': jnp.zeros((d,), jnp.float32), 'bn1_v': jnp.ones((d,), jnp.float32), 'conv2_w': jax.random.normal(ks[3], (d, d, 17), jnp.float32) * s, 'bn2_g': jnp.ones((d,), jnp.float32), 'bn2_b': jnp.zeros((d,), jnp.float32), 'bn2_m': jnp.zeros((d,), jnp.float32), 'bn2_v': jnp.ones((d,), jnp.float32), 'w_msg': jax.random.normal(ks[4], (d, d), jnp.float32) * s, 'b_msg': jnp.zeros((d,), jnp.float32), 'w_ih': jax.random.normal(ks[5], (3 * d, 2 * d), jnp.float32) * s, 'b_ih': jnp.zeros((3 * d,), jnp.float32), 'w_hh': jax.random.normal(ks[6], (3 * d, d), jnp.float32) * s, 'b_hh': jnp.zeros((3 * d,), jnp.float32)}
    _L3_gnn_all = _L3_gnn_setup()
    _L3_gnn_in = {k: v for k, v in _L3_gnn_all.items() if k in ('w_se', 'b_se', 'conv1_w', 'bn1_g', 'bn1_b', 'bn1_m', 'bn1_v', 'conv2_w', 'bn2_g', 'bn2_b', 'bn2_m', 'bn2_v', 'w_msg', 'b_msg', 'w_ih', 'b_ih', 'w_hh', 'b_hh')}
    del _L3_gnn_all
    return {'x': x, 'adj': adj, 'L0_gnn_W': _L0_gnn_in['W'], 'L0_gnn_W_edges': _L0_gnn_in['W_edges'], 'L0_gnn_b': _L0_gnn_in['b'], 'L1_gnn_bn1_gamma': _L1_gnn_in['bn1_gamma'], 'L1_gnn_bn1_beta': _L1_gnn_in['bn1_beta'], 'L1_gnn_bn1_mean': _L1_gnn_in['bn1_mean'], 'L1_gnn_bn1_var': _L1_gnn_in['bn1_var'], 'L1_gnn_w1': _L1_gnn_in['w1'], 'L1_gnn_b1': _L1_gnn_in['b1'], 'L1_gnn_bn2_gamma': _L1_gnn_in['bn2_gamma'], 'L1_gnn_bn2_beta': _L1_gnn_in['bn2_beta'], 'L1_gnn_bn2_mean': _L1_gnn_in['bn2_mean'], 'L1_gnn_bn2_var': _L1_gnn_in['bn2_var'], 'L1_gnn_w2': _L1_gnn_in['w2'], 'L1_gnn_b2': _L1_gnn_in['b2'], 'L1_gnn_w_skip': _L1_gnn_in['w_skip'], 'L1_gnn_b_skip': _L1_gnn_in['b_skip'], 'L2_gnn_eps': _L2_gnn_in['eps'], 'L2_gnn_W1': _L2_gnn_in['W1'], 'L2_gnn_b1': _L2_gnn_in['b1'], 'L2_gnn_W2': _L2_gnn_in['W2'], 'L2_gnn_b2': _L2_gnn_in['b2'], 'L3_gnn_w_se': _L3_gnn_in['w_se'], 'L3_gnn_b_se': _L3_gnn_in['b_se'], 'L3_gnn_conv1_w': _L3_gnn_in['conv1_w'], 'L3_gnn_bn1_g': _L3_gnn_in['bn1_g'], 'L3_gnn_bn1_b': _L3_gnn_in['bn1_b'], 'L3_gnn_bn1_m': _L3_gnn_in['bn1_m'], 'L3_gnn_bn1_v': _L3_gnn_in['bn1_v'], 'L3_gnn_conv2_w': _L3_gnn_in['conv2_w'], 'L3_gnn_bn2_g': _L3_gnn_in['bn2_g'], 'L3_gnn_bn2_b': _L3_gnn_in['bn2_b'], 'L3_gnn_bn2_m': _L3_gnn_in['bn2_m'], 'L3_gnn_bn2_v': _L3_gnn_in['bn2_v'], 'L3_gnn_w_msg': _L3_gnn_in['w_msg'], 'L3_gnn_b_msg': _L3_gnn_in['b_msg'], 'L3_gnn_w_ih': _L3_gnn_in['w_ih'], 'L3_gnn_b_ih': _L3_gnn_in['b_ih'], 'L3_gnn_w_hh': _L3_gnn_in['w_hh'], 'L3_gnn_b_hh': _L3_gnn_in['b_hh']}

def reference(x, adj, L0_gnn_W, L0_gnn_W_edges, L0_gnn_b, L1_gnn_bn1_gamma, L1_gnn_bn1_beta, L1_gnn_bn1_mean, L1_gnn_bn1_var, L1_gnn_w1, L1_gnn_b1, L1_gnn_bn2_gamma, L1_gnn_bn2_beta, L1_gnn_bn2_mean, L1_gnn_bn2_var, L1_gnn_w2, L1_gnn_b2, L1_gnn_w_skip, L1_gnn_b_skip, L2_gnn_eps, L2_gnn_W1, L2_gnn_b1, L2_gnn_W2, L2_gnn_b2, L3_gnn_w_se, L3_gnn_b_se, L3_gnn_conv1_w, L3_gnn_bn1_g, L3_gnn_bn1_b, L3_gnn_bn1_m, L3_gnn_bn1_v, L3_gnn_conv2_w, L3_gnn_bn2_g, L3_gnn_bn2_b, L3_gnn_bn2_m, L3_gnn_bn2_v, L3_gnn_w_msg, L3_gnn_b_msg, L3_gnn_w_ih, L3_gnn_b_ih, L3_gnn_w_hh, L3_gnn_b_hh):
    import jax
    import jax.numpy as jnp

    def _L0_gnn_ref(features, A1, A2, W, W_edges, b):
        import jax, jax.numpy as jnp
        import numpy as np
        B, N, F = (8, 512, 128)
        OUT, REL = (128, 16)
        NADJ = 7
        eye = jnp.zeros_like(A1) + jnp.eye(N, dtype=A1.dtype)
        shifted = jnp.roll(eye, 1, axis=0)
        A_fwd = [A1, A2, shifted]
        A_list = A_fwd + [jnp.swapaxes(a, 1, 2) for a in A_fwd]
        A_list.append(eye)
        A = jnp.stack(A_list, axis=0)
        HW = jnp.einsum('bnf,rfo->rbno', features, W[:, :F]) + jnp.einsum('rd,rdo->ro', W_edges, W[:, F:])[:, None, None, :]
        AHW = jnp.einsum('rbnm,rbmo->rbno', A, HW)
        out = jnp.max(AHW, axis=0) + b
        return out

    def _L1_gnn_ref(x, adj, bn1_gamma, bn1_beta, bn1_mean, bn1_var, w1, b1, bn2_gamma, bn2_beta, bn2_mean, bn2_var, w2, b2, w_skip, b_skip):
        import jax, jax.numpy as jnp
        import numpy as np
        BN_EPS = 0.001
        LRELU_ALPHA = 0.3

        def _bn(x, gamma, beta, mean, var):
            return gamma * (x - mean) * jax.lax.rsqrt(var + BN_EPS) + beta

        def _gcn(x, adj, w, b):
            xw = jnp.einsum('bnf,fc->bnc', x, w)
            return jnp.einsum('bnm,bmc->bnc', adj, xw) + b

        def _lrelu(x):
            return jnp.where(x >= 0, x, LRELU_ALPHA * x)
        h = _bn(x, bn1_gamma, bn1_beta, bn1_mean, bn1_var)
        out = _lrelu(_gcn(h, adj, w1, b1))
        out = _bn(out, bn2_gamma, bn2_beta, bn2_mean, bn2_var)
        out = _lrelu(_gcn(out, adj, w2, b2))
        skip = _gcn(h, adj, w_skip, b_skip)
        return out + skip

    def _L2_gnn_ref(x, adj, eps, W1, b1, W2, b2):
        import jax, jax.numpy as jnp
        import numpy as np
        D_IN = 128
        D_HID = 256
        aggregated = jnp.einsum('bnm,bmd->bnd', adj, x)
        h = (1.0 + eps) * x + aggregated
        h = jax.nn.relu(h @ W1 + b1)
        return h @ W2 + b2

    def _L3_gnn_ref(x, mask, w_se, b_se, conv1_w, bn1_g, bn1_b, bn1_m, bn1_v, conv2_w, bn2_g, bn2_b, bn2_m, bn2_v, w_msg, b_msg, w_ih, b_ih, w_hh, b_hh):
        import jax, jax.numpy as jnp
        import numpy as np
        from jax import lax
        DIM = 128
        EPS = 1e-05

        def _bn(h, g, b, m, v):
            scale = g / jnp.sqrt(v + EPS)
            return h * scale[None, :, None] + (b - m * scale)[None, :, None]

        def _conv1d(h, w, pad):
            return lax.conv_general_dilated(h, w, window_strides=(1,), padding=[(pad, pad)], dimension_numbers=('NCH', 'OIH', 'NCH'))
        d = x.shape[-1]
        xc = jnp.transpose(x, (0, 2, 1))
        h = _bn(_conv1d(xc, conv1_w, 0), bn1_g, bn1_b, bn1_m, bn1_v)
        h = jax.nn.relu(h)
        h = _bn(_conv1d(h, conv2_w, 8), bn2_g, bn2_b, bn2_m, bn2_v)
        x_conv = jnp.transpose(jax.nn.relu(h + xc), (0, 2, 1))
        s = x @ w_se.T + b_se
        sq = jnp.sum(s * s, axis=-1)
        dist = sq[:, :, None] + sq[:, None, :] - 2.0 * jnp.einsum('bnd,bmd->bnm', s, s)
        A = jnp.exp(-dist) * mask
        msg = jax.nn.relu(x @ w_msg.T + b_msg)
        x_nmp = jnp.einsum('bnm,bmd->bnd', A, msg)
        x_in = jnp.concatenate([x_conv, x_nmp], axis=-1)
        gi = x_in @ w_ih.T + b_ih
        gh = x @ w_hh.T + b_hh
        gi_r, gi_z, gi_n = (gi[..., :d], gi[..., d:2 * d], gi[..., 2 * d:])
        gh_r, gh_z, gh_n = (gh[..., :d], gh[..., d:2 * d], gh[..., 2 * d:])
        r = jax.nn.sigmoid(gi_r + gh_r)
        z = jax.nn.sigmoid(gi_z + gh_z)
        nn_ = jnp.tanh(gi_n + r * gh_n)
        return (1.0 - z) * nn_ + z * x
    x = _layernorm(x + _L0_gnn_ref(x, adj, adj, L0_gnn_W, L0_gnn_W_edges, L0_gnn_b), axis=-1)
    x = _layernorm(x + _L1_gnn_ref(x, adj, L1_gnn_bn1_gamma, L1_gnn_bn1_beta, L1_gnn_bn1_mean, L1_gnn_bn1_var, L1_gnn_w1, L1_gnn_b1, L1_gnn_bn2_gamma, L1_gnn_bn2_beta, L1_gnn_bn2_mean, L1_gnn_bn2_var, L1_gnn_w2, L1_gnn_b2, L1_gnn_w_skip, L1_gnn_b_skip), axis=-1)
    x = _layernorm(x + _L2_gnn_ref(x, adj, L2_gnn_eps, L2_gnn_W1, L2_gnn_b1, L2_gnn_W2, L2_gnn_b2), axis=-1)
    x = _layernorm(x + _L3_gnn_ref(x, adj, L3_gnn_w_se, L3_gnn_b_se, L3_gnn_conv1_w, L3_gnn_bn1_g, L3_gnn_bn1_b, L3_gnn_bn1_m, L3_gnn_bn1_v, L3_gnn_conv2_w, L3_gnn_bn2_g, L3_gnn_bn2_b, L3_gnn_bn2_m, L3_gnn_bn2_v, L3_gnn_w_msg, L3_gnn_b_msg, L3_gnn_w_ih, L3_gnn_b_ih, L3_gnn_w_hh, L3_gnn_b_hh), axis=-1)
    return x

_drawn_inputs = setup_inputs


def setup_inputs(seed=0):
    import zlib

    import numpy as np

    out = dict(_drawn_inputs(seed))
    spreads = {'L0_gnn_W_edges': (1.0, 0.2),
     'L1_gnn_bn1_gamma': (1.0, 0.2),
     'L1_gnn_bn1_beta': (0.0, 0.1),
     'L1_gnn_b1': (0.0, 0.367),
     'L1_gnn_bn2_gamma': (1.0, 0.2),
     'L1_gnn_bn2_beta': (0.0, 0.275),
     'L1_gnn_b2': (0.0, 0.8),
     'L1_gnn_b_skip': (0.0, 0.8),
     'L3_gnn_b_se': (0.0, 2.0),
     'L3_gnn_bn1_g': (1.0, 0.6),
     'L3_gnn_bn1_b': (0.0, 0.575),
     'L3_gnn_bn1_m': (0.0, 0.56),
     'L3_gnn_bn1_v': (1.0, 0.6),
     'L3_gnn_bn2_g': (1.0, 0.6),
     'L3_gnn_bn2_b': (0.0, 0.8),
     'L3_gnn_bn2_m': (0.0, 0.8),
     'L3_gnn_bn2_v': (1.0, 0.6),
     'L3_gnn_b_msg': (0.0, 0.283),
     'L3_gnn_b_ih': (0.0, 0.433),
     'L3_gnn_b_hh': (0.0, 0.446)}
    factors = {'L0_gnn_b': 8.0, 'L2_gnn_b1': 5.719, 'L2_gnn_b2': 3.348, 'L3_gnn_w_se': 8.0}
    for name, (base, spread) in spreads.items():
        noise = np.random.default_rng([zlib.crc32(name.encode()), seed]).standard_normal(out[name].shape)
        drawn = base * np.exp(spread * noise) if base else spread * noise
        out[name] = jnp.asarray(drawn.astype(out[name].dtype))
    for name, factor in factors.items():
        out[name] = (out[name] * factor).astype(out[name].dtype)
    return out
```

```python
from contextlib import ExitStack

import numpy as np

import concourse.bass as bass
from concourse import mybir

F32 = mybir.dt.float32
F16 = mybir.dt.float16
BF16 = mybir.dt.bfloat16
I32 = mybir.dt.int32
ALU = mybir.AluOpType
ACT = mybir.ActivationFunctionType
AX_X = mybir.AxisListType.X

P = 128
B, N, C = 16, 512, 128
T = N // P
NREL = 7
REL = 16
TAPS, PAD = 17, 8
SX = 16.0
SW = 256.0
SE = 1024.0
DOWN = 1.0 / SW
LRELU = 0.3
LN_EPS = 1e-5
RSQRT_SEED = 1597463007.0

NROW = 2 * 4 * T + 2
BLOCKS = [0, 1, 3, 4, 2, 5, 6]

WCOLS = {}
_at = 0
for _n, _w in (("rel", NREL * C), ("gcn1", 2 * C), ("gcn2", C), ("gin1", 2 * C), ("gin2", 2 * C),
               ("conv1", C), ("conv2", TAPS * C), ("msg", C), ("se", 4), ("ih_conv", 3 * C),
               ("ih_nmp", 3 * C), ("hh", 3 * C), ("eye", C)):
    WCOLS[_n] = (_at, _at + _w)
    _at += _w
NW = _at
BCOLS = {"gcn1": (0, 2 * C), "gcn2": (2 * C, 3 * C), "ih": (3 * C, 6 * C), "hh": (6 * C, 9 * C),
         "msg": (9 * C, 10 * C), "se": (10 * C, 10 * C + 4)}
NB = 10 * C + 4
VEC_VAR, VEC_GAMMA, VEC_BETA, VEC_MEAN, VEC_B1, VEC_EPS = 0, 4, 8, 12, 16, 18
NV = 19
MASK_HI_ROW, MASK_LO_ROW, MASK_HI_COL, MASK_LO_COL = 0, T, 2 * T, 3 * T
MASK_HI_ONE, MASK_LO_ONE, MASK_ROW, MASK_ONE, MASK_FIRST, MASK_SECOND = range(4 * T, 4 * T + 6)
NM = 4 * T + 6

KD = 36
KD_RIGHT = 64


def row_masks():
    m = np.zeros((NROW, NM), np.float32)
    for t in range(T):
        for j in range(4):
            m[4 * t + j, (MASK_LO_ROW if j % 2 else MASK_HI_ROW) + t] = 1.0
            m[4 * T + 4 * t + j, (MASK_LO_COL if j % 2 else MASK_HI_COL) + t] = 1.0
    m[NROW - 2, MASK_HI_ONE] = 1.0
    m[NROW - 1, MASK_LO_ONE] = 1.0
    m[0:4 * T, MASK_ROW] = 1.0
    m[NROW - 2:, MASK_ONE] = 1.0
    m[0, MASK_FIRST] = 1.0
    m[1, MASK_SECOND] = 1.0
    return m


def adj_resnorm(nc, x, xT, adj, adjT, weights, edge_w, edge_f, bias_rows, vecs, gin_b2, rel_b, ident, masks,
                bn_eps, out):
    ctx = ExitStack()
    with ctx:
        def sb(name, shape, dt=F32):
            return ctx.enter_context(nc.sbuf_tensor(name, shape, dt))

        def sem(name):
            return ctx.enter_context(nc.semaphore(name))

        shared = sb("shared", [P, 2 * T * N + 3 * N])
        w_raw = shared[:, 0:NW]
        w_hi = sb("w_hi", [P, NW], F16)
        w_lo = sb("w_lo", [P, NW], F16)
        at_keep = sb("at_keep", [P, T, N])
        setup_view = at_keep[:].rearrange("p t n -> p (t n)")
        rows_f = setup_view[0:NROW, 0:NREL * C]
        rows_b = setup_view[0:NROW, NREL * C:NREL * C + 4 * C]
        edge_f_sb = setup_view[0:REL, (NREL + 4) * C:(NREL + 4) * C + NREL * NROW]\
            .rearrange("p (r k) -> p r k", r=NREL)
        hid = sb("hid", [P, 2, N])
        edge_w_sb = hid[0:REL].rearrange("p k n -> p (k n)")[:, 0:NREL * C].rearrange("p (r c) -> p r c", r=NREL)
        gru_sums = sb("gru_sums", [P, 3, T * C])
        bias_sb = gru_sums[0:NROW].rearrange("p k n -> p (k n)")[:, 0:NB]
        vec = sb("vec", [P, NV])
        bn_eps_sb = sb("bn_eps_sb", [P, 4])
        bn_scale = sb("bn_scale", [P, 4])
        bn_shift = sb("bn_shift", [P, 4])
        bn_tmp = sb("bn_tmp", [P, 4])
        gin_b1 = sb("gin_b1", [P, 2])
        conv1_scale = sb("conv1_scale", [P, 1])
        conv1_shift = sb("conv1_shift", [P, 1])
        conv2_scale = sb("conv2_scale", [P, 1])
        conv2_shift = sb("conv2_shift", [P, 1])
        gin_b2_sb = sb("gin_b2_sb", [P, C])
        rel_b_sb = sb("rel_b_sb", [P, T, C])
        ident_f = sb("ident_f", [P, P])
        ident_h = sb("ident_h", [P, P], F16)
        ident_b = sb("ident_b", [P, P], BF16)
        mask_sb = sb("mask_sb", [NROW, NM])
        shift_bc = sb("shift_bc", [P, 2, NROW])
        rows_hi = sb("rows_hi", [NROW, NREL * C], F16)
        rows_lo = sb("rows_lo", [NROW, NREL * C], F16)
        rank_rel = sb("rank_rel", [NROW, T, NREL * C], F16)
        rank_gcn1 = sb("rank_gcn1", [NROW, T, 2 * C], F16)
        rank_gcn2 = sb("rank_gcn2", [NROW, T, C], F16)
        rank_gru = sb("rank_gru", [2, 4 * C], F16)
        rank_msg = sb("rank_msg", [2, C + 4], F16)
        ones2 = sb("ones2", [2, P], F16)

        a_in = sb("a_in", [P, T, N])
        at_in = sb("at_in", [P, T, N])
        x_in = sb("x_in", [P, T, C])
        xT_in = sb("xT_in", [P, N])
        a_hi, a_lo = sb("a_hi", [P, T, N], F16), sb("a_lo", [P, T, N], F16)
        at_hi, at_lo = sb("at_hi", [P, T, N], F16), sb("at_lo", [P, T, N], F16)
        x_hi, x_lo = sb("x_hi", [P, T, C], F16), sb("x_lo", [P, T, C], F16)
        xT_hi, xT_lo = sb("xT_hi", [P, N], F16), sb("xT_lo", [P, N], F16)
        sums = sb("sums", [P, 2 * T])
        sum_cols = sb("sum_cols", [P, NROW], F16)
        sum_rows = sb("sum_rows", [NROW, P], F16)
        x_bias = sb("x_bias", [P, T, C])
        ax_hi, ax_lo = sb("ax_hi", [P, N], F16), sb("ax_lo", [P, N], F16)
        atx_hi, atx_lo = sb("atx_hi", [P, N], F16), sb("atx_lo", [P, N], F16)
        rel_max = sb("rel_max", [P, T, C])
        y = sb("y", [P, T, C])
        x1 = sb("x1", [P, T, C])
        x1_hi, x1_lo = sb("x1_hi", [P, T, C], F16), sb("x1_lo", [P, T, C], F16)
        p1_hi, p1_lo = sb("p1_hi", [P, N], F16), sb("p1_lo", [P, N], F16)
        relu_part = sb("relu_part", [P, T, C])
        g1 = sb("g1", [P, T, C])
        g1_hi, g1_lo = sb("g1_hi", [P, T, C], F16), sb("g1_lo", [P, T, C], F16)
        x1_skip = sb("x1_skip", [P, T, C])
        p2_hi, p2_lo = sb("p2_hi", [P, N], F16), sb("p2_lo", [P, N], F16)
        gcn2_out = sb("gcn2_out", [P, T, C])
        x2 = sb("x2", [P, T, C])
        x2_hi, x2_lo = sb("x2_hi", [P, T, C], F16), sb("x2_lo", [P, T, C], F16)
        x2_bias = sb("x2_bias", [P, T, C])
        agg_hi, agg_lo = sb("agg_hi", [P, N], F16), sb("agg_lo", [P, N], F16)
        hid_hi, hid_lo = sb("hid_hi", [P, 2, N], F16), sb("hid_lo", [P, 2, N], F16)
        x3 = sb("x3", [P, T, C])
        x3T = sb("x3T", [P, N])
        x3T_hi, x3T_lo = sb("x3T_hi", [P, N], F16), sb("x3T_lo", [P, N], F16)
        feat = sb("feat", [P, T, 4])
        feat_rest = sb("feat_rest", [P, T, 4])
        feat_sq = sb("feat_sq", [P, T, 3])
        feat_parts = sb("feat_parts", [P, T, 3, 4], BF16)
        feat_cols = sb("feat_cols", [P, T, P], BF16)
        left_rows = sb("left_rows", [KD, N], BF16)
        right_rows = sb("right_rows", [KD, N], BF16)
        expd = shared[:, 0:T * N].rearrange("p (t n) -> p t n", t=T)
        kern = shared[:, T * N:2 * T * N].rearrange("p (t n) -> p t n", t=T)
        h1, conv_sum, xc = (shared[:, 2 * T * N + k * N:2 * T * N + (k + 1) * N] for k in range(3))
        kern_hi, kern_lo = sb("kern_hi", [P, T, N], F16), sb("kern_lo", [P, T, N], F16)
        stats = sb("stats", [P, T, 6])
        mean_var = sb("mean_var", [P, T, 2])
        var_eps = sb("var_eps", [P, T])
        rstd = sb("rstd", [P, T])
        newton = sb("newton", [P, T])

        msg = sb("msg", [P, T, C])
        msg_hi, msg_lo = sb("msg_hi", [P, T, C], F16), sb("msg_lo", [P, T, C], F16)
        h1_hi, h1_lo = sb("h1_hi", [P, N + 2 * PAD], F16), sb("h1_lo", [P, N + 2 * PAD], F16)
        nmp_hi, nmp_lo = sb("nmp_hi", [P, N], F16), sb("nmp_lo", [P, N], F16)
        xc_hi, xc_lo = sb("xc_hi", [P, N], F16), sb("xc_lo", [P, N], F16)
        gates = sb("gates", [P, T, 2 * C])
        reset_n = sb("reset_n", [P, 2, C])
        n_pre = sb("n_pre", [P, 2, C])
        cand = sb("cand", [P, T, C])
        x_minus, x_plus, y4 = (gru_sums[:, k].rearrange("p (t c) -> p t c", t=T) for k in range(3))
        result = sb("result", [P, T, C])

        front = ctx.enter_context(nc.psum_tensor("front", [P, 4, N], F32))
        back = ctx.enter_context(nc.psum_tensor("back", [P, 4, N], F32))

        def tiles(bank):
            return bank.rearrange("p (t c) -> p t c", t=T)

        names = """consts vectors_done weights_folded consts_set w_hi_done w_lo_done rank_psum rank_evac ranks_done
            a_loaded at_loaded x_loaded xT_loaded stored
            a_hi_done a_lo_done at_hi_done at_lo_done at_kept x_hi_done x_lo_done xT_hi_done xT_lo_done
            sum_cols_done sum_psum sum_rows_done
            ax_psum ax_hi_done ax_lo_done atx_psum atx_hi_done atx_lo_done
            x1_done x1_hi_done x1_lo_done p1_psum p1_hi_done p1_lo_done
            g1_done g1_hi_done g1_lo_done gcn1_free p2_psum p2_hi_done p2_lo_done
            gcn2_psum relu2_done gcn2_done y2_done x2_done x2_hi_done x2_lo_done x2_bias_done
            agg_psum agg_hi_done agg_lo_done hid_lo_done gin_psum y3_done x3_done
            x3T_psum x3T_done x3T_hi_done x3T_lo_done feat_psum feat_read feat_cols_done featT_psum
            left_done right_done kern_lo_done
            conv1_psum h1_done h1_hi_done h1_lo_done msg_psum msg_done msg_hi_done msg_lo_done
            nmp_psum nmp_hi_done nmp_lo_done conv2_psum conv_sum_done xc_done xc_hi_done xc_lo_done
            x3_used result_done""".split()
        s = {n: sem(n) for n in names}
        rel_psum = [sem(f"rel_psum{t}") for t in range(T)]
        rel_read = [sem(f"rel_read{t}") for t in range(T)]
        gcn1_psum = [sem(f"gcn1_psum{k}") for k in range(2)]
        relu1_done = [sem(f"relu1_done{k}") for k in range(2)]
        hid_psum = [sem(f"hid_psum{k}") for k in range(2)]
        hid_done = [sem(f"hid_done{k}") for k in range(2)]
        dist_psum = [sem(f"dist_psum{t}") for t in range(T)]
        exp_done = [sem(f"exp_done{t}") for t in range(T)]
        kern_done = [sem(f"kern_done{t}") for t in range(T)]
        gru_psum = [sem(f"gru_psum{t}") for t in range(T)]
        gates_done = [sem(f"gates_done{t}") for t in range(T)]
        n_pre_done = [sem(f"n_pre_done{t}") for t in range(T)]
        cand_done = [sem(f"cand_done{t}") for t in range(T)]
        dve_step = sem("dve_step")
        act_setup, dve_setup = sem("act_setup"), sem("dve_setup")

        GRU_BANK = [3, 0, 1, 2]

        def W(name, lo=0, width=None):
            a, b = WCOLS[name]
            b = b if width is None else a + lo + width
            return w_hi[:, a + lo:b], w_lo[:, a + lo:b]

        def counts(eng, i):
            if isinstance(i, int):
                return i + 1, i, i, i - 1, i > 0, i > 1
            after, before = eng.snap(i + 1), eng.snap(i - 1)
            eng.to_reg(after)
            eng.to_reg(before)
            return after, i, i, before, True, True

        def run(eng, iteration):
            iteration(0, True, False)
            iteration(1, True, True)
            with eng.Fori(2, B) as i:
                iteration(i, True, True)
            iteration(B, False, True)

        block = ctx.enter_context(nc.Block())

        @block.sync
        def _(sp):
            for dst, src in ((w_raw, weights), (vec[:], vecs), (bn_eps_sb[:], bn_eps), (ident_f[:], ident),
                             (edge_w_sb, edge_w), (edge_f_sb, edge_f), (bias_sb, bias_rows),
                             (gin_b2_sb[:], gin_b2), (rel_b_sb[:], rel_b), (mask_sb[:], masks)):
                sp.dma_start(dst, src).then_inc(s["consts"], 16)

            def load(g, prev, again=True):
                if again:
                    sp.wait_ge(s["a_lo_done"], prev)
                sp.dma_start(a_in[:], adj[g].rearrange("(t p) m -> p t m", p=P)).then_inc(s["a_loaded"], 16)
                if again:
                    sp.wait_ge(s["at_lo_done"], prev)
                if again:
                    sp.wait_ge(s["at_kept"], prev)
                sp.dma_start(at_in[:], adjT[g].rearrange("(t p) m -> p t m", p=P)).then_inc(s["at_loaded"], 16)
                if again:
                    sp.wait_ge(s["xT_lo_done"], prev)
                sp.dma_start(x_in[:], x[g].rearrange("(t p) c -> p t c", p=P)).then_inc(s["x_loaded"], 16)
                sp.dma_start(xT_in[:], xT[g]).then_inc(s["xT_loaded"], 16)

            def store(g, n):
                sp.wait_ge(s["result_done"], n)
                sp.dma_start(out[g].rearrange("(t p) c -> p t c", p=P), result[:]).then_inc(s["stored"], 16)

            load(0, 0, again=False)
            load(1, 1)
            with sp.Fori(1, B - 1) as i:
                following = sp.snap(i + 1)
                load(following, following)
                store(sp.snap(i - 1), i)
            store(B - 2, B - 1)
            store(B - 1, B)
            sp.wait_ge(s["stored"], 16 * B)

        NCONST = 10 * 16

        @block.gpsimd
        def _(pool):
            pool.wait_ge(s["consts"], NCONST)
            nc.gpsimd.memset(feat_cols[:], 0.0).then_inc(s["consts_set"], 1)
            nc.gpsimd.tensor_copy(ident_h[:], ident_f[:]).then_inc(s["consts_set"], 1)
            nc.gpsimd.tensor_copy(ident_b[:], ident_f[:]).then_inc(s["consts_set"], 1)
            nc.gpsimd.memset(ones2[:], SX).then_inc(s["consts_set"], 1)
            nc.gpsimd.memset(h1_hi[:], 0.0).then_inc(s["consts_set"], 1)
            nc.gpsimd.memset(h1_lo[:], 0.0).then_inc(s["consts_set"], 1)
            nc.gpsimd.memset(sum_cols[:], SX).then_inc(s["consts_set"], 1)
            pool.wait_ge(s["consts_set"], 7)
            left_ones = feat_cols[:, :, 0:KD].rearrange("p t (a b d) -> p t a b d", a=3, b=3)
            nc.gpsimd.memset(left_ones[:, :, 0, :, 3], 1.0).then_inc(s["consts_set"], 1)

            def iteration(i, has_front, has_back):
                n, prev, bn, bprev, again, back_again = counts(pool, i)

                def lo_part(dst, src, hi):
                    return nc.gpsimd.tensor_tensor(dst, src, hi, ALU.subtract)

                if has_back:
                    pool.wait_ge(s["h1_hi_done"], bn)
                    lo_part(h1_lo[:, PAD:PAD + N], h1, h1_hi[:, PAD:PAD + N]).then_inc(s["h1_lo_done"], 1)
                    pool.wait_ge(s["msg_hi_done"], bn)
                    lo_part(msg_lo[:], msg[:], msg_hi[:]).then_inc(s["msg_lo_done"], 1)
                if has_front:
                    pool.wait_ge(s["ranks_done"], 1)
                    if again:
                        pool.wait_ge(s["kern_lo_done"], prev)
                    pool.wait_ge(s["at_hi_done"], n)
                    nc.gpsimd.tensor_copy(at_keep[:], at_in[:]).then_inc(s["at_kept"], 1)
                    pool.wait_ge(s["x1_hi_done"], n)
                    lo_part(x1_lo[:], x1[:], x1_hi[:]).then_inc(s["x1_lo_done"], 1)
                if has_back:
                    pool.wait_ge(s["xc_hi_done"], bn)
                    lo_part(xc_lo[:], xc, xc_hi[:]).then_inc(s["xc_lo_done"], 1)
                if has_front:
                    pool.wait_ge(s["g1_hi_done"], n)
                    lo_part(g1_lo[:], g1[:], g1_hi[:]).then_inc(s["g1_lo_done"], 1)
                    pool.wait_ge(s["gcn2_done"], n)
                    nc.gpsimd.tensor_tensor(y[:], gcn2_out[:], x1_skip[:], ALU.add).then_inc(s["y2_done"], 1)
                    pool.wait_ge(s["x2_hi_done"], n)
                    lo_part(x2_lo[:], x2[:], x2_hi[:]).then_inc(s["x2_lo_done"], 1)
                    nc.gpsimd.tensor_tensor(x2_bias[:], x2[:], gin_b2_sb[:].unsqueeze(1).to_broadcast([P, T, C]),
                                            ALU.add).then_inc(s["x2_bias_done"], 1)
                    for t in range(T):
                        pool.wait_ge(kern_done[t], n)
                        ins = nc.gpsimd.tensor_tensor(kern_lo[:, t], kern[:, t], kern_hi[:, t], ALU.subtract)
                    ins.then_inc(s["kern_lo_done"], 1)

            run(pool, iteration)

        @block.scalar
        def _(act):
            act.wait_ge(s["weights_folded"], 1)
            nc.scalar.activation(w_hi[:], w_raw, ACT.Copy, scale=SW).then_inc(s["w_hi_done"], 1)

            def iteration(i, has_front, has_back):
                n, prev, bn, bprev, again, back_again = counts(act, i)
                loaded = 16 * (i + 1) if isinstance(i, int) else act.snap(i * 16 + 16)

                def hi_from(dst, src, scale=DOWN):
                    return nc.scalar.activation(dst, src, ACT.Copy, scale=scale)

                def adjacency(src, hi, first):
                    for t in range(T):
                        ins = nc.scalar.activation(hi[:, t], src[:, t], ACT.Copy, scale=SW,
                                                   accum_out=sums[:, first + t:first + t + 1])
                    return ins

                def gru(t):
                    bank = back[:, GRU_BANK[t]]
                    act.wait_ge(gru_psum[t], bn)
                    nc.scalar.activation(gates[:, t], bank[:, C:3 * C], ACT.Tanh, scale=0.5 / (SX * SW))\
                        .then_inc(gates_done[t], 1)
                    act.wait_ge(n_pre_done[t], bn)
                    nc.scalar.activation(cand[:, t], n_pre[:, t % 2], ACT.Tanh, scale=1.0 / (SX * SW))\
                        .then_inc(cand_done[t], 1)

                if has_back:
                    act.wait_ge(s["conv1_psum"], bn)
                    nc.scalar.activation(h1, back[:, 0], ACT.Relu, scale=conv1_scale[:], bias=conv1_shift[:])\
                        .then_inc(s["h1_done"], 1)
                    act.wait_ge(s["msg_psum"], bn)
                    nc.scalar.activation(msg[:], tiles(back[:, 3]), ACT.Relu, scale=DOWN).then_inc(s["msg_done"], 1)
                if has_front:
                    if again:
                        act.wait_ge(s["atx_psum"], prev)
                    act.wait_ge(s["a_loaded"], loaded)
                    adjacency(a_in, a_hi, 0).then_inc(s["a_hi_done"], 1)
                    if again:
                        act.wait_ge(s["agg_psum"], prev)
                    act.wait_ge(s["at_loaded"], loaded)
                    adjacency(at_in, at_hi, T).then_inc(s["at_hi_done"], 1)
                    act.wait_ge(s["x_loaded"], loaded)
                    hi_from(x_hi[:], x_in[:], SX).then_inc(s["x_hi_done"], 1)
                    act.wait_ge(s["xT_loaded"], loaded)
                    hi_from(xT_hi[:], xT_in[:], SX).then_inc(s["xT_hi_done"], 1)
                    act.wait_ge(s["ax_psum"], n)
                    hi_from(ax_hi[:], front[:, 0]).then_inc(s["ax_hi_done"], 1)
                if has_back:
                    act.wait_ge(s["nmp_psum"], bn)
                    hi_from(nmp_hi[:], back[:, 2], 1.0 / SE).then_inc(s["nmp_hi_done"], 1)
                if has_front:
                    act.wait_ge(s["atx_psum"], n)
                    hi_from(atx_hi[:], front[:, 1]).then_inc(s["atx_hi_done"], 1)
                    act.wait_ge(s["sum_psum"], n)
                    hi_from(sum_rows[:], front[:, 2].bitcast(F16)[0:NROW, 0:P], 1.0).then_inc(s["sum_rows_done"], 1)
                    act.wait_ge(s["x1_done"], n)
                    hi_from(x1_hi[:], x1[:], 1.0).then_inc(s["x1_hi_done"], 1)
                if has_back:
                    act.wait_ge(s["conv_sum_done"], bn)
                    nc.scalar.activation(xc, conv_sum, ACT.Relu, bias=conv2_shift[:]).then_inc(s["xc_done"], 1)
                if has_front:
                    act.wait_ge(s["p1_psum"], n)
                    hi_from(p1_hi[:], front[:, 2]).then_inc(s["p1_hi_done"], 1)
                if has_back:
                    gru(0)
                if has_front:
                    for k in range(2):
                        bank = front[:, k].rearrange("p (t h c) -> p t h c", t=2, h=2)
                        act.wait_ge(gcn1_psum[k], n)
                        nc.scalar.activation(relu_part[:, 2 * k:2 * k + 2], bank[:, :, 0], ACT.Relu,
                                             scale=(1.0 - LRELU) * DOWN).then_inc(relu1_done[k], 1)
                    act.wait_ge(s["g1_done"], n)
                    hi_from(g1_hi[:], g1[:], 1.0).then_inc(s["g1_hi_done"], 1)
                if has_back:
                    gru(1)
                if has_front:
                    act.wait_ge(s["p2_psum"], n)
                    hi_from(p2_hi[:], front[:, 2]).then_inc(s["p2_hi_done"], 1)
                if has_back:
                    gru(2)
                if has_front:
                    act.wait_ge(s["gcn2_psum"], n)
                    nc.scalar.activation(relu_part[:], tiles(front[:, 3]), ACT.Relu,
                                         scale=(1.0 - LRELU) * DOWN).then_inc(s["relu2_done"], 1)
                if has_back:
                    gru(3)
                if has_front:
                    act.wait_ge(s["x2_done"], n)
                    hi_from(x2_hi[:], x2[:], 1.0).then_inc(s["x2_hi_done"], 1)
                    act.wait_ge(s["agg_psum"], n)
                    hi_from(agg_hi[:], front[:, 2]).then_inc(s["agg_hi_done"], 1)
                    for k in range(2):
                        act.wait_ge(hid_psum[k], n)
                        nc.scalar.activation(hid[:, k], front[:, k], ACT.Relu, scale=DOWN, bias=gin_b1[:, k:k + 1])\
                            .then_inc(hid_done[k], 1)
                    act.wait_ge(s["x3T_psum"], n)
                    hi_from(x3T[:], front[:, 2], 1.0).then_inc(s["x3T_done"], 1)
                    act.wait_ge(s["featT_psum"], n)
                    hi_from(left_rows[:], front[:, 2].bitcast(BF16)[0:KD, 0:N], 1.0).then_inc(s["left_done"], 1)
                    for t in range(T):
                        act.wait_ge(dist_psum[t], n)
                        nc.scalar.activation(expd[:, t], front[:, t], ACT.Exp, bias=feat[:, t, 3:4])\
                            .then_inc(exp_done[t], 1)

            run(act, iteration)

        @block.vector
        def _(dve):
            v = nc.vector
            steps = [0]

            def step(ins):
                steps[0] += 1
                ins.then_inc(dve_step, 1)
                return steps[0]

            def rsqrt(dst, src, tmp, gain):
                step(v.tensor_scalar(dst.bitcast(I32), src.bitcast(I32), -0.5, RSQRT_SEED, ALU.mult, ALU.add))
                for k in range(3):
                    dve.wait_ge(dve_step, steps[0])
                    step(v.scalar_tensor_tensor(out=tmp, in0=dst, scalar=-0.5, in1=dst, op0=ALU.mult, op1=ALU.mult))
                    dve.wait_ge(dve_step, steps[0])
                    step(v.tensor_tensor(tmp, tmp, src, ALU.mult))
                    dve.wait_ge(dve_step, steps[0])
                    step(v.scalar_tensor_tensor(out=dst, in0=tmp, scalar=1.5, in1=dst, op0=ALU.add, op1=ALU.mult))
                if gain != 1.0:
                    dve.wait_ge(dve_step, steps[0])
                    step(v.tensor_scalar(dst, dst, gain, None, ALU.mult))

            dve.wait_ge(s["consts"], NCONST)
            step(v.tensor_tensor(bn_tmp[:], vec[:, VEC_VAR:VEC_VAR + 4], bn_eps_sb[:], ALU.add))
            dve.wait_ge(dve_step, steps[0])
            step(v.tensor_copy(bn_shift[:], bn_tmp[:]))
            dve.wait_ge(dve_step, steps[0])
            rsqrt(bn_scale[:], bn_shift[:], bn_tmp[:], 1.0)
            dve.wait_ge(dve_step, steps[0])
            step(v.tensor_tensor(bn_scale[:], bn_scale[:], vec[:, VEC_GAMMA:VEC_GAMMA + 4], ALU.mult))
            dve.wait_ge(dve_step, steps[0])
            step(v.tensor_tensor(bn_tmp[:], bn_scale[:], vec[:, VEC_MEAN:VEC_MEAN + 4], ALU.mult))
            dve.wait_ge(dve_step, steps[0])
            step(v.tensor_tensor(bn_shift[:], vec[:, VEC_BETA:VEC_BETA + 4], bn_tmp[:], ALU.subtract))
            dve.wait_ge(dve_step, steps[0])
            for k in range(2):
                step(v.tensor_copy(shift_bc[:, k], bn_shift[:, k:k + 1].to_broadcast([P, NROW])))
            dve.wait_ge(dve_step, steps[0])
            dve_count_vectors = steps[0]
            step(v.tensor_scalar(conv1_scale[:], bn_scale[:, 2:3], DOWN, None, ALU.mult))
            step(v.tensor_scalar(conv2_scale[:], bn_scale[:, 3:4], DOWN, None, ALU.mult))
            step(v.tensor_scalar(conv1_shift[:], bn_shift[:, 2:3], SX, None, ALU.mult))
            step(v.tensor_scalar(conv2_shift[:], bn_shift[:, 3:4], SX, None, ALU.mult))
            step(v.tensor_scalar(gin_b1[:], vec[:, VEC_B1:VEC_B1 + 2], SX, None, ALU.mult))
            step(v.tensor_scalar(gin_b2_sb[:], gin_b2_sb[:], SX, None, ALU.mult))
            step(v.tensor_scalar(rel_b_sb[:], rel_b_sb[:], SX, None, ALU.mult))
            v.tensor_copy(bn_tmp[:, 0:1], bn_shift[:, 0:1]).then_inc(s["vectors_done"], 1)
            step(v.tensor_scalar(bn_tmp[:, 1:2], vec[:, VEC_EPS:VEC_EPS + 1], 1.0, None, ALU.add))
            dve.wait_ge(dve_step, steps[0])
            a, b = WCOLS["eye"]
            step(v.tensor_scalar(w_raw[:, a:b], ident_f[:], bn_tmp[:, 1:2], None, ALU.mult))
            dve.wait_ge(s["rank_psum"], 1)
            a, b = WCOLS["gcn1"]
            step(v.tensor_scalar(w_raw[:, a:b], w_raw[:, a:b], bn_scale[:, 0:1], None, ALU.mult))
            a, b = WCOLS["gcn2"]
            v.tensor_scalar(w_raw[:, a:b], w_raw[:, a:b], bn_scale[:, 1:2], None, ALU.mult)\
                .then_inc(s["weights_folded"], 1)

            def place(dst, cols, mask_hi, mask_lo, rows):
                step(v.tensor_scalar(dst, rows_hi[0:rows, cols], mask_sb[0:rows, mask_hi:mask_hi + 1], None, ALU.mult))
                dve.wait_ge(dve_step, steps[0])
                step(v.scalar_tensor_tensor(out=dst, in0=rows_lo[0:rows, cols],
                                            scalar=mask_sb[0:rows, mask_lo:mask_lo + 1], in1=dst,
                                            op0=ALU.mult, op1=ALU.add))

            def split_rows(width):
                dve.wait_ge(dve_step, steps[0])
                step(v.tensor_scalar(rows_hi[:, 0:width], rows_f[:, 0:width], SW, None, ALU.mult))
                dve.wait_ge(dve_step, steps[0])
                step(v.scalar_tensor_tensor(out=rows_lo[:, 0:width], in0=rows_f[:, 0:width], scalar=SW,
                                            in1=rows_hi[:, 0:width], op0=ALU.mult, op1=ALU.subtract))
                dve.wait_ge(dve_step, steps[0])

            def both(mask):
                return mask_sb[:, mask:mask + 1]

            step(v.tensor_copy(rows_f[:, 0:N], front[0:NROW, 0]))
            step(v.tensor_copy(rows_f[:, N:NREL * C], front[0:NROW, 1, 0:NREL * C - N]))
            split_rows(NREL * C)
            for t in range(T):
                place(rank_rel[:, t, 0:2 * C], slice(0, 2 * C), MASK_HI_ROW + t, MASK_LO_ROW + t, NROW)
                place(rank_rel[:, t, 2 * C:4 * C], slice(2 * C, 4 * C), MASK_HI_COL + t, MASK_LO_COL + t, NROW)
                place(rank_rel[:, t, 4 * C:], slice(4 * C, NREL * C), MASK_HI_ONE, MASK_LO_ONE, NROW)
            dve.wait_ge(dve_step, steps[0])
            step(v.tensor_scalar(rows_b[:, 0:3 * C], bias_sb[:, 0:3 * C], both(MASK_ONE), None, ALU.mult))
            dve.wait_ge(dve_step, steps[0])
            step(v.scalar_tensor_tensor(out=rows_f[:, 0:3 * C], in0=front[0:NROW, 2, 0:3 * C], scalar=both(MASK_ROW),
                                        in1=rows_b[:, 0:3 * C], op0=ALU.mult, op1=ALU.add))
            split_rows(3 * C)
            step(v.tensor_tensor(rows_b[:, 0:T], mask_sb[:, MASK_HI_ROW:MASK_HI_ROW + T],
                                 both(MASK_HI_ONE).to_broadcast([NROW, T]), ALU.add))
            step(v.tensor_tensor(rows_b[:, T:2 * T], mask_sb[:, MASK_LO_ROW:MASK_LO_ROW + T],
                                 both(MASK_LO_ONE).to_broadcast([NROW, T]), ALU.add))
            dve.wait_ge(dve_step, steps[0])
            for t in range(T):
                for dst, lo_c, hi_c in ((rank_gcn1, 0, 2 * C), (rank_gcn2, 2 * C, 3 * C)):
                    step(v.tensor_scalar(dst[:, t], rows_hi[:, lo_c:hi_c], rows_b[:, t:t + 1], None, ALU.mult))
                    dve.wait_ge(dve_step, steps[0])
                    step(v.scalar_tensor_tensor(out=dst[:, t], in0=rows_lo[:, lo_c:hi_c],
                                                scalar=rows_b[:, T + t:T + t + 1], in1=dst[:, t],
                                                op0=ALU.mult, op1=ALU.add))
            dve.wait_ge(dve_step, steps[0])
            ih, hh = BCOLS["ih"][0], BCOLS["hh"][0]
            step(v.tensor_copy(rows_f[:, 0:C], bias_sb[:, ih:ih + C]))
            step(v.tensor_tensor(rows_f[:, C:3 * C], bias_sb[:, ih + C:ih + 3 * C], bias_sb[:, hh:hh + 2 * C], ALU.add))
            step(v.tensor_copy(rows_f[:, 3 * C:4 * C], bias_sb[:, hh + 2 * C:hh + 3 * C]))
            step(v.tensor_copy(rows_f[:, 4 * C:5 * C + 4], bias_sb[:, BCOLS["msg"][0]:BCOLS["se"][1]]))
            split_rows(5 * C + 4)
            place(rank_gru[:], slice(0, 4 * C), MASK_FIRST, MASK_SECOND, 2)
            place(rank_msg[:], slice(4 * C, 5 * C + 4), MASK_FIRST, MASK_SECOND, 2)
            dve.wait_ge(dve_step, steps[0])
            v.tensor_copy(bn_tmp[:, 0:1], bn_shift[:, 0:1]).then_inc(s["ranks_done"], 1)
            dve.wait_ge(s["w_hi_done"], 1)
            v.scalar_tensor_tensor(out=w_lo[:], in0=w_raw, scalar=SW, in1=w_hi[:], op0=ALU.mult,
                                   op1=ALU.subtract).then_inc(s["w_lo_done"], 1)
            dve.wait_ge(s["w_lo_done"], 1)
            dve.wait_ge(s["ranks_done"], 1)
            dve.wait_ge(s["consts_set"], 8)
            dve.wait_ge(dve_step, steps[0])
            v.sem_clear(dve_step)
            steps[0] = 0

            def iteration(i, has_front, has_back):
                n, prev, bn, bprev, again, back_again = counts(dve, i)

                def lo_from(dst, src, hi, scale=DOWN):
                    return v.scalar_tensor_tensor(out=dst, in0=src, scalar=scale, in1=hi, op0=ALU.mult,
                                                  op1=ALU.subtract)

                def hi_copy(dst, src):
                    return v.tensor_copy(dst, src)

                def layernorm(src, dst, src_scale, dst_scale):
                    for t in range(T):
                        step(v.bn_stats(stats[:, t], src[:, t]))
                    dve.wait_ge(dve_step, steps[0])
                    for t in range(T):
                        step(v.bn_aggr(mean_var[:, t], stats[:, t]))
                    dve.wait_ge(dve_step, steps[0])
                    step(v.tensor_scalar(var_eps[:], mean_var[:, :, 1], LN_EPS * src_scale * src_scale, None, ALU.add))
                    dve.wait_ge(dve_step, steps[0])
                    rsqrt(rstd[:], var_eps[:], newton[:], dst_scale)
                    dve.wait_ge(dve_step, steps[0])
                    for t in range(T):
                        ins = v.tensor_scalar(dst[:, t], src[:, t], mean_var[:, t, 0:1], rstd[:, t:t + 1],
                                              ALU.subtract, ALU.mult)
                        if t < T - 1:
                            step(ins)
                    return ins

                def gru(t):
                    bank = back[:, GRU_BANK[t]]
                    dve.wait_ge(gates_done[t], bn)
                    step(v.scalar_tensor_tensor(out=reset_n[:, t % 2], in0=gates[:, t, 0:C], scalar=1.0,
                                                in1=bank[:, 3 * C:4 * C], op0=ALU.add, op1=ALU.mult))
                    dve.wait_ge(dve_step, steps[0])
                    v.scalar_tensor_tensor(out=n_pre[:, t % 2], in0=reset_n[:, t % 2], scalar=0.5,
                                           in1=bank[:, 0:C], op0=ALU.mult, op1=ALU.add).then_inc(n_pre_done[t], 1)

                if has_back:
                    dve.wait_ge(s["h1_done"], bn)
                    hi_copy(h1_hi[:, PAD:PAD + N], h1).then_inc(s["h1_hi_done"], 1)
                    dve.wait_ge(s["msg_done"], bn)
                    hi_copy(msg_hi[:], msg[:]).then_inc(s["msg_hi_done"], 1)
                if has_front:
                    dve.wait_ge(s["a_hi_done"], n)
                    lo_from(a_lo[:], a_in[:], a_hi[:], SW).then_inc(s["a_lo_done"], 1)
                    dve.wait_ge(s["at_hi_done"], n)
                    lo_from(at_lo[:], at_in[:], at_hi[:], SW).then_inc(s["at_lo_done"], 1)
                    cols = sum_cols[:, 0:8 * T].rearrange("p (g k j) -> p g k j", g=2 * T, k=2)
                    scaled = sums[:].unsqueeze(2).to_broadcast([P, 2 * T, 2])
                    c = step(v.tensor_scalar(cols[:, :, 0], scaled, SX / SW, None, ALU.mult))
                    dve.wait_ge(s["x_hi_done"], n)
                    lo_from(x_lo[:], x_in[:], x_hi[:], SX).then_inc(s["x_lo_done"], 1)
                    dve.wait_ge(dve_step, c)
                    v.scalar_tensor_tensor(out=cols[:, :, 1], in0=scaled, scalar=SX / SW, in1=cols[:, :, 0],
                                           op0=ALU.mult, op1=ALU.subtract).then_inc(s["sum_cols_done"], 1)
                    xb = step(v.scalar_tensor_tensor(out=x_bias[:], in0=x_in[:], scalar=SX, in1=rel_b_sb[:],
                                                     op0=ALU.mult, op1=ALU.add))
                    dve.wait_ge(s["xT_hi_done"], n)
                    lo_from(xT_lo[:], xT_in[:], xT_hi[:], SX).then_inc(s["xT_lo_done"], 1)
                    dve.wait_ge(s["ax_hi_done"], n)
                    lo_from(ax_lo[:], front[:, 0], ax_hi[:]).then_inc(s["ax_lo_done"], 1)
                if has_back:
                    dve.wait_ge(s["nmp_hi_done"], bn)
                    lo_from(nmp_lo[:], back[:, 2], nmp_hi[:], 1.0 / SE).then_inc(s["nmp_lo_done"], 1)
                if has_front:
                    dve.wait_ge(s["atx_hi_done"], n)
                    lo_from(atx_lo[:], front[:, 1], atx_hi[:]).then_inc(s["atx_lo_done"], 1)
                    for t in range(T):
                        f = 2 if t % 2 == 0 else 0
                        dve.wait_ge(rel_psum[t], n)
                        seven = front[:, f:f + 2].rearrange("p b n -> p (b n)")[:, 0:NREL * C]
                        v.tensor_reduce(rel_max[:, t], seven.rearrange("p (r c) -> p c r", r=NREL), AX_X, ALU.max)\
                            .then_inc(rel_read[t], 1)
                    dve.wait_ge(rel_read[T - 1], n)
                    step(v.scalar_tensor_tensor(out=y[:], in0=rel_max[:], scalar=DOWN, in1=x_bias[:],
                                                op0=ALU.mult, op1=ALU.add))
                    dve.wait_ge(dve_step, steps[0])
                    layernorm(y, x1, SX, SX).then_inc(s["x1_done"], 1)
                if has_back:
                    dve.wait_ge(s["conv2_psum"], bn)
                    v.scalar_tensor_tensor(out=conv_sum, in0=back[:, 1], scalar=conv2_scale[:], in1=x3T[:],
                                           op0=ALU.mult, op1=ALU.add).then_inc(s["conv_sum_done"], 1)
                    dve.wait_ge(s["xc_done"], bn)
                    hi_copy(xc_hi[:], xc).then_inc(s["xc_hi_done"], 1)
                if has_front:
                    dve.wait_ge(s["p1_hi_done"], n)
                    lo_from(p1_lo[:], front[:, 2], p1_hi[:]).then_inc(s["p1_lo_done"], 1)
                if has_back:
                    gru(0)
                if has_front:
                    for k in range(2):
                        bank = front[:, k].rearrange("p (t h c) -> p t h c", t=2, h=2)
                        pair = slice(2 * k, 2 * k + 2)
                        dve.wait_ge(relu1_done[k], n)
                        ins = v.scalar_tensor_tensor(out=g1[:, pair], in0=bank[:, :, 0], scalar=LRELU * DOWN,
                                                     in1=relu_part[:, pair], op0=ALU.mult, op1=ALU.add)
                        if k == 0:
                            step(ins)
                        else:
                            ins.then_inc(s["g1_done"], 1)
                    for k in range(2):
                        bank = front[:, k].rearrange("p (t h c) -> p t h c", t=2, h=2)
                        pair = slice(2 * k, 2 * k + 2)
                        ins = v.scalar_tensor_tensor(out=x1_skip[:, pair], in0=bank[:, :, 1], scalar=DOWN,
                                                     in1=x1[:, pair], op0=ALU.mult, op1=ALU.add)
                        if k == 0:
                            step(ins)
                        else:
                            ins.then_inc(s["gcn1_free"], 1)
                if has_back:
                    gru(1)
                if has_front:
                    dve.wait_ge(s["p2_hi_done"], n)
                    lo_from(p2_lo[:], front[:, 2], p2_hi[:]).then_inc(s["p2_lo_done"], 1)
                if has_back:
                    gru(2)
                if has_front:
                    dve.wait_ge(s["relu2_done"], n)
                    v.scalar_tensor_tensor(out=gcn2_out[:], in0=tiles(front[:, 3]), scalar=LRELU * DOWN,
                                           in1=relu_part[:], op0=ALU.mult, op1=ALU.add).then_inc(s["gcn2_done"], 1)
                if has_back:
                    gru(3)
                if has_front:
                    dve.wait_ge(s["y2_done"], n)
                    layernorm(y, x2, SX, SX).then_inc(s["x2_done"], 1)
                if has_back:
                    dve.wait_ge(cand_done[T - 1], bn)
                    step(v.scalar_tensor_tensor(out=x_minus, in0=x3[:], scalar=1.0 / SX, in1=cand[:],
                                                op0=ALU.mult, op1=ALU.subtract))
                    v.scalar_tensor_tensor(out=x_plus, in0=x3[:], scalar=1.0 / SX, in1=cand[:],
                                           op0=ALU.mult, op1=ALU.add).then_inc(s["x3_used"], 1)
                    dve.wait_ge(dve_step, steps[0])
                    step(v.scalar_tensor_tensor(out=x_minus, in0=gates[:, :, C:2 * C], scalar=1.0, in1=x_minus,
                                                op0=ALU.add, op1=ALU.mult))
                    dve.wait_ge(s["x3_used"], bn)
                    dve.wait_ge(dve_step, steps[0])
                    step(v.scalar_tensor_tensor(out=y4, in0=x_plus, scalar=2.0, in1=x_minus,
                                                op0=ALU.mult, op1=ALU.add))
                if has_front:
                    dve.wait_ge(s["agg_hi_done"], n)
                    lo_from(agg_lo[:], front[:, 2], agg_hi[:]).then_inc(s["agg_lo_done"], 1)
                if has_back:
                    if back_again:
                        dve.wait_ge(s["stored"], bn * 16 - 16)
                    dve.wait_ge(dve_step, steps[0])
                    layernorm(y4, result, 2.0, 1.0).then_inc(s["result_done"], 1)
                if has_front:
                    for k in range(2):
                        dve.wait_ge(hid_done[k], n)
                        c = step(v.tensor_copy(hid_hi[:, k], hid[:, k]))
                        dve.wait_ge(dve_step, c)
                        ins = v.tensor_tensor(hid_lo[:, k], hid[:, k], hid_hi[:, k], ALU.subtract)
                        if k == 0:
                            step(ins)
                        else:
                            ins.then_inc(s["hid_lo_done"], 1)
                    dve.wait_ge(s["x2_bias_done"], n)
                    dve.wait_ge(s["gin_psum"], n)
                    v.scalar_tensor_tensor(out=y[:], in0=tiles(front[:, 3]), scalar=DOWN, in1=x2_bias[:],
                                           op0=ALU.mult, op1=ALU.add).then_inc(s["y3_done"], 1)
                    dve.wait_ge(s["y3_done"], n)
                    layernorm(y, x3, SX, SX).then_inc(s["x3_done"], 1)
                    dve.wait_ge(s["x3T_done"], n)
                    hi_copy(x3T_hi[:], x3T[:]).then_inc(s["x3T_hi_done"], 1)
                    dve.wait_ge(s["x3T_hi_done"], n)
                    v.tensor_tensor(x3T_lo[:], x3T[:], x3T_hi[:], ALU.subtract).then_inc(s["x3T_lo_done"], 1)
                    dve.wait_ge(s["feat_psum"], n)
                    pf = front[:, 1, 0:4 * T].rearrange("p (t d) -> p t d", t=T)
                    v.tensor_scalar(feat[:, :, 0:3], pf[:, :, 0:3], 2.0 / (SX * SW), None, ALU.mult)\
                        .then_inc(s["feat_read"], 1)
                    dve.wait_ge(s["feat_read"], n)
                    step(v.scalar_tensor_tensor(out=feat_sq[:], in0=feat[:, :, 0:3], scalar=-0.25,
                                                in1=feat[:, :, 0:3], op0=ALU.mult, op1=ALU.mult))
                    dve.wait_ge(dve_step, steps[0])
                    step(v.tensor_reduce(feat[:, :, 3], feat_sq[:], AX_X, ALU.add))
                    dve.wait_ge(dve_step, steps[0])
                    step(v.tensor_copy(feat_parts[:, :, 0], feat[:]))
                    dve.wait_ge(dve_step, steps[0])
                    step(v.tensor_tensor(feat_rest[:], feat[:], feat_parts[:, :, 0], ALU.subtract))
                    dve.wait_ge(dve_step, steps[0])
                    step(v.tensor_copy(feat_parts[:, :, 1], feat_rest[:]))
                    dve.wait_ge(dve_step, steps[0])
                    step(v.tensor_tensor(feat_parts[:, :, 2], feat_rest[:], feat_parts[:, :, 1], ALU.subtract))
                    dve.wait_ge(dve_step, steps[0])
                    right = feat_cols[:, :, KD_RIGHT:KD_RIGHT + KD].rearrange("p t (a q) -> p t a q", a=3)
                    step(v.tensor_copy(right, feat_parts[:].rearrange("p t b d -> p t (b d)").unsqueeze(2)
                                       .to_broadcast([P, T, 3, 12])))
                    left = feat_cols[:, :, 0:KD].rearrange("p t (a b d) -> p t a b d", a=3, b=3)
                    for a in range(3):
                        ins = v.tensor_scalar(left[:, :, a, :, 0:3],
                                              feat_parts[:, :, a, 0:3].unsqueeze(2).to_broadcast([P, T, 3, 3]),
                                              0.5, None, ALU.mult)
                        if a < 2:
                            step(ins)
                    ins.then_inc(s["feat_cols_done"], 1)
                    dve.wait_ge(s["featT_psum"], n)
                    v.tensor_copy(right_rows[:], front[:, 2].bitcast(BF16)[KD_RIGHT:KD_RIGHT + KD, 0:N])\
                        .then_inc(s["right_done"], 1)
                    for t in range(T):
                        dve.wait_ge(exp_done[t], n)
                        c = step(v.scalar_tensor_tensor(out=kern[:, t], in0=expd[:, t], scalar=SE,
                                                        in1=at_keep[:, t], op0=ALU.mult, op1=ALU.mult))
                        dve.wait_ge(dve_step, c)
                        v.tensor_copy(kern_hi[:, t], kern[:, t]).then_inc(kern_done[t], 1)
                dve.wait_ge(dve_step, steps[0])
                dve.wait_ge(s["x3_done"] if has_front else s["result_done"], n if has_front else bn)
                v.sem_clear(dve_step)
                steps[0] = 0

            run(dve, iteration)

        @block.tensor
        def _(pe):
            def product(dst, left, right, start, stop, skip=False):
                (lh, ll), (rh, rl) = left, right
                nc.tensor.matmul(dst, lh, rh, start=start, stop=False, skip_group_check=skip)
                nc.tensor.matmul(dst, lh, rl, start=False, stop=False, skip_group_check=skip)
                return nc.tensor.matmul(dst, ll, rh, start=False, stop=stop, skip_group_check=skip)

            def over_nodes(dst, left, right, stop=True):
                for t in range(T):
                    last = product(dst, (left[0][:, t], left[1][:, t]), (right[0][:, t], right[1][:, t]),
                                   start=(t == 0), stop=stop and t == T - 1)
                return last

            def nodes(pair, t):
                return pair[0][:, t * P:(t + 1) * P], pair[1][:, t * P:(t + 1) * P]

            A, AT = (a_hi, a_lo), (at_hi, at_lo)

            pe.wait_ge(s["consts"], NCONST)
            for r in range(NREL):
                nc.tensor.matmul(front[0:NROW, r // 4, (r % 4) * C:(r % 4 + 1) * C], edge_f_sb[:, r],
                                 edge_w_sb[:, r], start=True, stop=True)
            pe.wait_ge(s["vectors_done"], 1)
            a, b = WCOLS["gcn1"]
            nc.tensor.matmul(front[0:NROW, 2, 0:2 * C], shift_bc[:, 0], w_raw[:, a:b], start=True, stop=True)
            a, b = WCOLS["gcn2"]
            nc.tensor.matmul(front[0:NROW, 2, 2 * C:3 * C], shift_bc[:, 1], w_raw[:, a:b], start=True, stop=True)\
                .then_inc(s["rank_psum"], 1)
            pe.wait_ge(s["w_lo_done"], 1)
            pe.wait_ge(s["ranks_done"], 1)
            pe.wait_ge(s["consts_set"], 8)

            def iteration(i, has_front, has_back):
                n, prev, bn, bprev, again, back_again = counts(pe, i)

                def conv1():
                    pe.wait_ge(s["x3T_lo_done"], bn)
                    if back_again:
                        pe.wait_ge(gates_done[1], bprev)
                    if back_again:
                        pe.wait_ge(n_pre_done[1], bprev)
                    product(back[:, 0], W("conv1"), (x3T_hi[:], x3T_lo[:]), True, True).then_inc(s["conv1_psum"], 1)

                def messages():
                    if back_again:
                        pe.wait_ge(n_pre_done[0], bprev)
                    for t in range(T):
                        dst = tiles(back[:, 3])[:, t]
                        nc.tensor.matmul(dst, ones2[:], rank_msg[:, 0:C], start=True, stop=False)
                        last = product(dst, nodes((x3T_hi, x3T_lo), t), W("msg"), False, True)
                    last.then_inc(s["msg_psum"], 1)

                def conv2(taps):
                    if taps[0] == 0:
                        pe.wait_ge(s["h1_lo_done"], bn)
                        if back_again:
                            pe.wait_ge(n_pre_done[2], bprev)
                    for k in taps:
                        last = product(back[:, 1], W("conv2", k * C, C), (h1_hi[:, k:k + N], h1_lo[:, k:k + N]),
                                       k == 0, k == TAPS - 1)
                    if taps[-1] == TAPS - 1:
                        last.then_inc(s["conv2_psum"], 1)

                def nmp():
                    pe.wait_ge(s["msg_lo_done"], bn)
                    pe.wait_ge(s["kern_lo_done"], bn)
                    if back_again:
                        pe.wait_ge(n_pre_done[3], bprev)
                    over_nodes(back[:, 2], (msg_hi, msg_lo), (kern_hi, kern_lo)).then_inc(s["nmp_psum"], 1)

                def gru(t):
                    if t == 0:
                        pe.wait_ge(s["xc_lo_done"], bn)
                        pe.wait_ge(s["nmp_lo_done"], bn)
                    bank = back[:, GRU_BANK[t]]
                    nc.tensor.matmul(bank, ones2[:], rank_gru[:], start=True, stop=False)
                    product(bank[:, C:4 * C], nodes((x3T_hi, x3T_lo), t), W("hh"), False, False)
                    product(bank[:, 0:3 * C], nodes((nmp_hi, nmp_lo), t), W("ih_nmp"), False, False)
                    product(bank[:, 0:3 * C], nodes((xc_hi, xc_lo), t), W("ih_conv"), False, True)\
                        .then_inc(gru_psum[t], 1)

                def adjacency_x():
                    pe.wait_ge(s["at_lo_done"], n)
                    pe.wait_ge(s["x_lo_done"], n)
                    if again:
                        pe.wait_ge(exp_done[T - 1], prev)
                    over_nodes(front[:, 0], (x_hi, x_lo), AT).then_inc(s["ax_psum"], 1)

                def adjacencyT_x():
                    pe.wait_ge(s["a_lo_done"], n)
                    over_nodes(front[:, 1], (x_hi, x_lo), A).then_inc(s["atx_psum"], 1)

                def sum_transpose():
                    pe.wait_ge(s["consts_set"], 8)
                    pe.wait_ge(s["sum_cols_done"], n)
                    nc.tensor.transpose(front[:, 2].bitcast(F16)[0:NROW, 0:P], sum_cols[:], ident_h[:])\
                        .then_inc(s["sum_psum"], 1)

                def relations(t):
                    f = 2 if t % 2 == 0 else 0
                    if t == 0:
                        pe.wait_ge(s["sum_rows_done"], n)
                        pe.wait_ge(s["xT_lo_done"], n)
                        pe.wait_ge(s["atx_lo_done"], n)
                    if t >= 2:
                        pe.wait_ge(rel_read[t - 2], n)
                    nc.tensor.matmul(front[:, f], sum_rows[:], rank_rel[:, t, 0:4 * C], start=True, stop=False)
                    product(front[:, f, 0:2 * C], nodes((ax_hi, ax_lo), t), W("rel", 0, 2 * C), False, False)
                    product(front[:, f, 2 * C:4 * C], nodes((atx_hi, atx_lo), t), W("rel", 2 * C, 2 * C), False, True)
                    nc.tensor.matmul(front[:, f + 1, 0:3 * C], sum_rows[:], rank_rel[:, t, 4 * C:], start=True,
                                     stop=False)
                    product(front[:, f + 1, 0:3 * C], nodes((xT_hi, xT_lo), t), W("rel", 4 * C, 3 * C), False, True)\
                        .then_inc(rel_psum[t], 1)

                def gcn_p1():
                    pe.wait_ge(s["x1_lo_done"], n)
                    over_nodes(front[:, 2], (x1_hi, x1_lo), AT).then_inc(s["p1_psum"], 1)

                def gcn_first():
                    pe.wait_ge(s["p1_lo_done"], n)
                    for t in range(T):
                        dst = front[:, t // 2, (t % 2) * 2 * C:(t % 2 + 1) * 2 * C]
                        nc.tensor.matmul(dst, sum_rows[:], rank_gcn1[:, t], start=True, stop=False)
                        last = product(dst, nodes((p1_hi, p1_lo), t), W("gcn1"), False, True)
                        if t % 2:
                            last.then_inc(gcn1_psum[t // 2], 1)

                def gcn_p2():
                    pe.wait_ge(s["g1_lo_done"], n)
                    over_nodes(front[:, 2], (g1_hi, g1_lo), AT).then_inc(s["p2_psum"], 1)

                def gcn_second():
                    pe.wait_ge(s["p2_lo_done"], n)
                    for t in range(T):
                        dst = tiles(front[:, 3])[:, t]
                        nc.tensor.matmul(dst, sum_rows[:], rank_gcn2[:, t], start=True, stop=False)
                        last = product(dst, nodes((p2_hi, p2_lo), t), W("gcn2"), False, True)
                    last.then_inc(s["gcn2_psum"], 1)

                def gin_aggregate():
                    pe.wait_ge(s["x2_lo_done"], n)
                    over_nodes(front[:, 2], (x2_hi, x2_lo), AT, stop=False)
                    for t in range(T):
                        last = product(front[:, 2, t * P:(t + 1) * P], (x2_hi[:, t], x2_lo[:, t]), W("eye"), False,
                                       t == T - 1)
                    last.then_inc(s["agg_psum"], 1)

                def gin_hidden():
                    pe.wait_ge(s["agg_lo_done"], n)
                    pe.wait_ge(s["gcn1_free"], n)
                    for k in range(2):
                        product(front[:, k], W("gin1", k * C, C), (agg_hi[:], agg_lo[:]), True, True)\
                            .then_inc(hid_psum[k], 1)

                def gin_out():
                    pe.wait_ge(s["hid_lo_done"], n)
                    pe.wait_ge(s["gcn2_done"], n)
                    for t in range(T):
                        dst = tiles(front[:, 3])[:, t]
                        product(dst, nodes((hid_hi[:, 0], hid_lo[:, 0]), t), W("gin2", 0, C), True, False)
                        last = product(dst, nodes((hid_hi[:, 1], hid_lo[:, 1]), t), W("gin2", C, C), False, True)
                    last.then_inc(s["gin_psum"], 1)

                def transpose_x3():
                    pe.wait_ge(s["x3_done"], n)
                    for t in range(T):
                        last = nc.tensor.transpose(front[:, 2, t * P:(t + 1) * P], x3[:, t], ident_f[:])
                    last.then_inc(s["x3T_psum"], 1)

                def features():
                    pe.wait_ge(s["x3T_lo_done"], n)
                    for t in range(T):
                        dst = front[:, 1, 4 * t:4 * t + 4]
                        nc.tensor.matmul(dst, ones2[:], rank_msg[:, C:C + 4], start=True, stop=False)
                        last = product(dst, nodes((x3T_hi, x3T_lo), t), W("se"), False, True)
                    last.then_inc(s["feat_psum"], 1)

                def feature_rows():
                    pe.wait_ge(s["feat_cols_done"], n)
                    for t in range(T):
                        last = nc.tensor.transpose(front[:, 2].bitcast(BF16)[:, t * P:(t + 1) * P], feat_cols[:, t],
                                                   ident_b[:])
                    last.then_inc(s["featT_psum"], 1)

                def distances():
                    pe.wait_ge(s["left_done"], n)
                    pe.wait_ge(s["right_done"], n)
                    pe.wait_ge(s["y3_done"], n)
                    for t in range(T):
                        nc.tensor.matmul(front[:, t], left_rows[:, t * P:(t + 1) * P], right_rows[:], start=True,
                                         stop=True).then_inc(dist_psum[t], 1)

                order = [(1, conv1), (1, messages), (1, conv2, range(0, 6)), (0, adjacency_x), (1, nmp),
                         (0, adjacencyT_x), (0, sum_transpose), (1, conv2, range(6, 10)),
                         (0, relations, 0), (0, relations, 1), (0, relations, 2), (0, relations, 3),
                         (1, conv2, range(10, TAPS)), (0, gcn_p1), (1, gru, 0), (0, gcn_first), (1, gru, 1),
                         (0, gcn_p2), (1, gru, 2), (0, gcn_second), (1, gru, 3), (0, gin_aggregate),
                         (0, gin_hidden), (0, gin_out), (0, transpose_x3), (0, features), (0, feature_rows),
                         (0, distances)]
                for is_back, stage, *args in order:
                    if has_back if is_back else has_front:
                        stage(*args)

            run(pe, iteration)


def kernel(**inputs):
    import numpy as _np
    import concourse.bacc as _bacc
    from concourse import mybir as _mybir
    from concourse.bass_utils import run_bass_kernel_spmd as _run

    a = {k: _np.ascontiguousarray(v) for k, v in inputs.items()}
    w_rel, w_ih, w_hh = a["L0_gnn_W"], a["L3_gnn_w_ih"], a["L3_gnn_w_hh"]
    ih_order = _np.concatenate([_np.arange(2 * C, 3 * C), _np.arange(0, 2 * C)])
    ih_t = w_ih[ih_order].T
    w_se = _np.concatenate([a["L3_gnn_w_se"].T, _np.zeros((C, 1), _np.float32)], axis=1)
    pieces = [w_rel[BLOCKS, :C].transpose(1, 0, 2).reshape(C, NREL * C),
              a["L1_gnn_w1"], a["L1_gnn_w_skip"], a["L1_gnn_w2"], a["L2_gnn_W1"],
              a["L2_gnn_W2"].reshape(2, C, C).transpose(1, 0, 2).reshape(C, 2 * C),
              a["L3_gnn_conv1_w"][:, :, 0].T,
              a["L3_gnn_conv2_w"].transpose(1, 2, 0).reshape(C, TAPS * C),
              a["L3_gnn_w_msg"].T, w_se, ih_t[:C], ih_t[C:], w_hh.T, _np.zeros((C, C), _np.float32)]
    weights = _np.ascontiguousarray(_np.concatenate(pieces, axis=1))
    bias = _np.concatenate([a["L1_gnn_b1"], a["L1_gnn_b_skip"], a["L1_gnn_b2"], a["L3_gnn_b_ih"][ih_order],
                            a["L3_gnn_b_hh"], a["L3_gnn_b_msg"], a["L3_gnn_b_se"], _np.zeros(1, _np.float32)])
    norms = ["L1_gnn_bn1_", "L1_gnn_bn2_", "L3_gnn_bn1_", "L3_gnn_bn2_"]
    vecs = [a[p + (q if "L1" in p else q[0])] for q in ("var", "gamma", "beta", "mean") for p in norms]
    vecs += [a["L2_gnn_b1"][:C], a["L2_gnn_b1"][C:], _np.broadcast_to(a["L2_gnn_eps"], (C,))]
    arrays = {
        "x": a["x"],
        "xT": _np.ascontiguousarray(a["x"].transpose(0, 2, 1)),
        "adj": a["adj"],
        "adjT": _np.ascontiguousarray(a["adj"].transpose(0, 2, 1)),
        "weights": weights,
        "edge_w": _np.ascontiguousarray(w_rel[BLOCKS, C:].transpose(1, 0, 2)),
        "edge_f": _np.ascontiguousarray(_np.broadcast_to(a["L0_gnn_W_edges"][BLOCKS].T[:, :, None], (REL, NREL, NROW))),
        "bias_rows": _np.ascontiguousarray(_np.broadcast_to(bias, (NROW, NB))),
        "vecs": _np.ascontiguousarray(_np.stack(vecs, axis=1)),
        "gin_b2": _np.ascontiguousarray(_np.broadcast_to(a["L2_gnn_b2"], (P, C))),
        "rel_b": _np.ascontiguousarray(a["L0_gnn_b"].reshape(T, P, C).transpose(1, 0, 2)),
        "ident": _np.eye(P, dtype=_np.float32),
        "masks": row_masks(),
        "bn_eps": _np.ascontiguousarray(_np.broadcast_to(_np.array([1e-3, 1e-3, 1e-5, 1e-5], _np.float32), (P, 4))),
    }
    nc = _bacc.Bacc("TRN2", target_bir_lowering=False, num_devices=1)
    feeds, args = {}, []
    for name, value in arrays.items():
        feeds[f"in_{name}_dram"] = value
        args.append(nc.dram_tensor(f"in_{name}_dram", value.shape, _mybir.dt.from_np(value.dtype),
                                   kind="ExternalInput").ap())
    args.append(nc.dram_tensor("out_dram", (B, N, C), _mybir.dt.float32, kind="ExternalOutput").ap())
    adj_resnorm(nc, *args)
    r = _run(nc, [feeds], core_ids=[0])
    return r.results[0]["out_dram"]
```

```python
from contextlib import ExitStack

import numpy as np

import concourse.bass as bass
from concourse import mybir

F32 = mybir.dt.float32
F16 = mybir.dt.float16
BF16 = mybir.dt.bfloat16
I32 = mybir.dt.int32
ALU = mybir.AluOpType
ACT = mybir.ActivationFunctionType
AX_X = mybir.AxisListType.X

P = 128
B, N, C = 16, 512, 128
T = N // P
NREL = 7
REL = 16
TAPS, PAD = 17, 8
SX = 16.0
SW = 256.0
SE = 1024.0
DOWN = 1.0 / SW
LRELU = 0.3
LN_EPS = 1e-5
RSQRT_SEED = 1597463007.0
HALF_SEED = RSQRT_SEED - 2 ** 22

NROW = 2 * 4 * T + 2
BLOCKS = [0, 1, 3, 4, 2, 5, 6]

WCOLS = {}
_at = 0
for _n, _w in (("rel", NREL * C), ("gcn1", 2 * C), ("gcn2", C), ("gin1", 2 * C), ("gin2", 2 * C),
               ("conv1", C), ("conv2", TAPS * C), ("msg", C), ("se", 4), ("ih_conv", 3 * C),
               ("ih_nmp", 3 * C), ("hh", 3 * C), ("eye", C)):
    WCOLS[_n] = (_at, _at + _w)
    _at += _w
NW = _at
BCOLS = {"gcn1": (0, 2 * C), "gcn2": (2 * C, 3 * C), "ih": (3 * C, 6 * C), "hh": (6 * C, 9 * C),
         "msg": (9 * C, 10 * C), "se": (10 * C, 10 * C + 4)}
NB = 10 * C + 4
VEC_VAR, VEC_GAMMA, VEC_BETA, VEC_MEAN, VEC_B1, VEC_EPS = 0, 4, 8, 12, 16, 18
NV = 19
MASK_HI_ROW, MASK_LO_ROW, MASK_HI_COL, MASK_LO_COL = 0, T, 2 * T, 3 * T
MASK_HI_ONE, MASK_LO_ONE, MASK_ROW, MASK_ONE, MASK_FIRST, MASK_SECOND = range(4 * T, 4 * T + 6)
NM = 4 * T + 6

KD = 36
KD_RIGHT = 64


def row_masks():
    m = np.zeros((NROW, NM), np.float32)
    for t in range(T):
        for j in range(4):
            m[4 * t + j, (MASK_LO_ROW if j % 2 else MASK_HI_ROW) + t] = 1.0
            m[4 * T + 4 * t + j, (MASK_LO_COL if j % 2 else MASK_HI_COL) + t] = 1.0
    m[NROW - 2, MASK_HI_ONE] = 1.0
    m[NROW - 1, MASK_LO_ONE] = 1.0
    m[0:4 * T, MASK_ROW] = 1.0
    m[NROW - 2:, MASK_ONE] = 1.0
    m[0, MASK_FIRST] = 1.0
    m[1, MASK_SECOND] = 1.0
    return m


def adj_resnorm(nc, x, xT, adj, adjT, weights, edge_w, edge_f, bias_rows, vecs, gin_b2, rel_b, ident, masks,
                bn_eps, out):
    ctx = ExitStack()
    with ctx:
        def sb(name, shape, dt=F32):
            return ctx.enter_context(nc.sbuf_tensor(name, shape, dt))

        def sem(name):
            return ctx.enter_context(nc.semaphore(name))

        shared = sb("shared", [P, 11 * N])
        w_raw = shared[:, 0:NW]
        w_hi = sb("w_hi", [P, NW], F16)
        w_lo = sb("w_lo", [P, NW], F16)
        at_keep = sb("at_keep", [P, T, N])
        setup_view = at_keep[:].rearrange("p t n -> p (t n)")
        rows_f = setup_view[0:NROW, 0:NREL * C]
        rows_b = setup_view[0:NROW, NREL * C:NREL * C + 4 * C]
        edge_f_sb = setup_view[0:REL, (NREL + 4) * C:(NREL + 4) * C + NREL * NROW]\
            .rearrange("p (r k) -> p r k", r=NREL)
        hid = sb("hid", [P, 2, N])
        edge_w_sb = hid[0:REL].rearrange("p k n -> p (k n)")[:, 0:NREL * C].rearrange("p (r c) -> p r c", r=NREL)
        gru_sums = sb("gru_sums", [P, 3, T * C])
        bias_sb = gru_sums[0:NROW].rearrange("p k n -> p (k n)")[:, 0:NB]
        vec = sb("vec", [P, NV])
        bn_eps_sb = sb("bn_eps_sb", [P, 4])
        bn_scale = sb("bn_scale", [P, 4])
        bn_shift = sb("bn_shift", [P, 4])
        bn_tmp = sb("bn_tmp", [P, 4])
        gin_b1 = sb("gin_b1", [P, 2])
        conv1_scale = sb("conv1_scale", [P, 1])
        conv1_shift = sb("conv1_shift", [P, 1])
        conv2_scale = sb("conv2_scale", [P, 1])
        conv2_shift = sb("conv2_shift", [P, 1])
        gin_b2_sb = sb("gin_b2_sb", [P, C])
        rel_b_sb = sb("rel_b_sb", [P, T, C])
        ident_f = sb("ident_f", [P, P])
        ident_h = sb("ident_h", [P, P], F16)
        ident_b = sb("ident_b", [P, P], BF16)
        mask_sb = sb("mask_sb", [NROW, NM])
        shift_bc = sb("shift_bc", [P, 2, NROW])
        kern_hi, kern_lo = sb("kern_hi", [P, T, N], F16), sb("kern_lo", [P, T, N], F16)
        rows_hi, rows_lo = (k[0:NROW].rearrange("p t n -> p (t n)")[:, 0:NREL * C] for k in (kern_hi, kern_lo))
        rank_rel = sb("rank_rel", [NROW, T, NREL * C], F16)
        rank_gcn1 = sb("rank_gcn1", [NROW, T, 2 * C], F16)
        rank_gcn2 = sb("rank_gcn2", [NROW, T, C], F16)
        rank_gru = sb("rank_gru", [2, 4 * C], F16)
        rank_msg = sb("rank_msg", [2, C + 4], F16)
        ones2 = sb("ones2", [2, P], F16)

        a_in = sb("a_in", [P, T, N])
        at_in = sb("at_in", [P, T, N])
        x_in = sb("x_in", [P, T, C])
        xT_in = sb("xT_in", [P, N])
        a_hi, a_lo = sb("a_hi", [P, T, N], F16), sb("a_lo", [P, T, N], F16)
        at_hi, at_lo = sb("at_hi", [P, T, N], F16), sb("at_lo", [P, T, N], F16)
        bt_hi, bt_lo = sb("bt_hi", [P, T, N], F16), sb("bt_lo", [P, T, N], F16)
        x_hi, x_lo = sb("x_hi", [P, T, C], F16), sb("x_lo", [P, T, C], F16)
        xT_hi, xT_lo = sb("xT_hi", [P, N], F16), sb("xT_lo", [P, N], F16)
        sums = sb("sums", [P, 2 * T])
        sum_cols = sb("sum_cols", [P, NROW], F16)
        sum_rows = sb("sum_rows", [NROW, P], F16)
        sum_rows_b = sb("sum_rows_b", [NROW, P], F16)
        x_bias = sb("x_bias", [P, T, C])
        ax_hi, ax_lo = sb("ax_hi", [P, N], F16), sb("ax_lo", [P, N], F16)
        atx_hi, atx_lo = sb("atx_hi", [P, N], F16), sb("atx_lo", [P, N], F16)
        rel_max = sb("rel_max", [P, T, C])
        y1, y2, y3 = (sb(f"y{k}", [P, T, C]) for k in (1, 2, 3))
        x1 = sb("x1", [P, T, C])
        x1_hi, x1_lo = sb("x1_hi", [P, T, C], F16), sb("x1_lo", [P, T, C], F16)
        p1_hi, p1_lo = sb("p1_hi", [P, N], F16), sb("p1_lo", [P, N], F16)
        relu_part = sb("relu_part", [P, T, C])
        g1_hi, g1_lo = sb("g1_hi", [P, T, C], F16), sb("g1_lo", [P, T, C], F16)
        x1_skip = sb("x1_skip", [P, T, C])
        p2_hi, p2_lo = sb("p2_hi", [P, N], F16), sb("p2_lo", [P, N], F16)
        gcn2_out = sb("gcn2_out", [P, T, C])
        x2 = sb("x2", [P, T, C])
        x2_hi, x2_lo = sb("x2_hi", [P, T, C], F16), sb("x2_lo", [P, T, C], F16)
        x2_bias = sb("x2_bias", [P, T, C])
        agg_hi, agg_lo = sb("agg_hi", [P, N], F16), sb("agg_lo", [P, N], F16)
        hid_hi, hid_lo = sb("hid_hi", [P, 2, N], F16), sb("hid_lo", [P, 2, N], F16)
        x3 = sb("x3", [P, T, C])
        x3_true = sb("x3_true", [P, T, C])
        x3T = sb("x3T", [P, N])
        x3T_hi, x3T_lo = sb("x3T_hi", [P, N], F16), sb("x3T_lo", [P, N], F16)
        feat = sb("feat", [P, T, 4])
        feat_rest = sb("feat_rest", [P, T, 4])
        feat_sq = sb("feat_sq", [P, T, 3])
        feat_parts = sb("feat_parts", [P, T, 3, 4], BF16)
        feat_cols = sb("feat_cols", [P, T, P], BF16)
        left_rows = sb("left_rows", [KD, N], BF16)
        right_rows = sb("right_rows", [KD, N], BF16)
        expd = shared[:, 0:2 * N].rearrange("p (t n) -> p t n", t=2)
        kern = shared[:, 2 * N:6 * N].rearrange("p (t n) -> p t n", t=T)
        h1, conv_sum, xc = (shared[:, k * N:(k + 1) * N] for k in (6, 7, 8))
        msg, g1 = (shared[:, k * N:(k + 1) * N].rearrange("p (t c) -> p t c", t=T) for k in (9, 10))
        stats = [sb(f"stats{k}", [P, T, 6]) for k in range(4)]
        mean_var = [sb(f"mean_var{k}", [P, T, 2]) for k in range(4)]
        rstd = [sb(f"rstd{k}", [P, T]) for k in range(4)]
        half_var = [sb(f"half_var{k}", [P, T]) for k in range(4)]
        newton = [sb(f"newton{k}", [P, T]) for k in range(4)]
        newton_t = [sb(f"newton_t{k}", [P, T]) for k in range(4)]
        minus_mean = [sb(f"minus_mean{k}", [P, T]) for k in range(4)]
        shift = [sb(f"shift{k}", [P, T]) for k in range(4)]

        msg_hi, msg_lo = sb("msg_hi", [P, T, C], F16), sb("msg_lo", [P, T, C], F16)
        h1_hi, h1_lo = sb("h1_hi", [P, N + 2 * PAD], F16), sb("h1_lo", [P, N + 2 * PAD], F16)
        nmp_hi, nmp_lo = sb("nmp_hi", [P, N], F16), sb("nmp_lo", [P, N], F16)
        xc_hi, xc_lo = sb("xc_hi", [P, N], F16), sb("xc_lo", [P, N], F16)
        gates = sb("gates", [P, T, 2 * C])
        reset_n = sb("reset_n", [P, 2, C])
        n_pre = sb("n_pre", [P, 2, C])
        cand = sb("cand", [P, T, C])
        x_minus, x_plus, y4 = (gru_sums[:, k].rearrange("p (t c) -> p t c", t=T) for k in range(3))
        result = sb("result", [P, T, C])

        pa = ctx.enter_context(nc.psum_tensor("pa", [P, 4, N], F32))
        pb = ctx.enter_context(nc.psum_tensor("pb", [P, 2, N], F32))
        pc = ctx.enter_context(nc.psum_tensor("pc", [P, 2, N], F32))
        dist_bank = [pc[:, 0], pb[:, 0], pc[:, 0], pb[:, 0]]
        gru_bank = [pc[:, 0], pc[:, 1], pc[:, 0], pc[:, 1]]

        def tiles(bank):
            return bank.rearrange("p (t c) -> p t c", t=T)

        names = """consts consts_set vectors_done weights_folded w_hi_done w_lo_done rank_psum ranks_done
            a_loaded at_loaded x_loaded stored
            a_hi_done a_lo_done at_hi_done at_lo_done x_hi_done x_lo_done xT_hi_done xT_lo_done x_bias_done
            sum_cols_done sum_psum sum_rows_done
            ax_psum ax_hi_done ax_lo_done atx_psum atx_hi_done atx_lo_done y1_done
            x1_done x1_hi_done x1_lo_done p1_psum p1_hi_done p1_lo_done
            g1_done g1_hi_done g1_lo_done gcn1_free bt_done at_kept p2_psum p2_hi_done p2_lo_done
            gcn2_psum relu2_done gcn2_done y2_done x2_done x2_hi_done x2_lo_done x2_bias_done
            agg_psum agg_hi_done agg_lo_done hid_lo_done gin_psum y3_done x3_done
            x3T_psum x3T_done x3T_hi_done x3T_lo_done feat_psum feat_read feat_cols_done featT_psum
            left_done right_done kern_lo_done x3_true_done
            conv1_psum h1_done h1_hi_done h1_lo_done msg_psum msg_done msg_hi_done msg_lo_done
            nmp_psum nmp_hi_done nmp_lo_done conv2_psum conv_sum_done xc_done xc_hi_done xc_lo_done
            mix_done y4_done result_done""".split()
        s = {n: sem(n) for n in names}
        rel_psum = [sem(f"rel_psum{t}") for t in range(T)]
        rel_read = [sem(f"rel_read{t}") for t in range(T)]
        gcn1_psum = [sem(f"gcn1_psum{k}") for k in range(2)]
        relu1_done = [sem(f"relu1_done{k}") for k in range(2)]
        hid_psum = [sem(f"hid_psum{k}") for k in range(2)]
        hid_done = [sem(f"hid_done{k}") for k in range(2)]
        hid_hi_done = [sem(f"hid_hi_done{k}") for k in range(2)]
        dist_psum = [sem(f"dist_psum{t}") for t in range(T)]
        exp_done = [sem(f"exp_done{t}") for t in range(T)]
        kern_done = [sem(f"kern_done{t}") for t in range(T)]
        kern_hi_done = [sem(f"kern_hi_done{t}") for t in range(T)]
        gru_psum = [sem(f"gru_psum{t}") for t in range(T)]
        gates_done = [sem(f"gates_done{t}") for t in range(T)]
        n_pre_done = [sem(f"n_pre_done{t}") for t in range(T)]
        cand_done = [sem(f"cand_done{t}") for t in range(T)]
        seed_done = [sem(f"seed_done{k}") for k in range(4)]
        norm_done = [sem(f"norm_done{k}") for k in range(4)]
        dve_step = sem("dve_step")
        pool_step = sem("pool_step")

        def W(name, lo=0, width=None):
            a, b = WCOLS[name]
            b = b if width is None else a + lo + width
            return w_hi[:, a + lo:b], w_lo[:, a + lo:b]

        class Counts:

            def __init__(self, eng, i):
                if isinstance(i, int):
                    at = {k: i + k for k in range(-3, 3)}
                    self.has_in, self.has_a, self.has_b, self.has_c, self.has_d = (
                        0 <= g < B for g in (i + 1, i, i - 1, i - 2, i - 3))
                    self.again_in, self.again_a, self.again_b, self.again_c, self.again_d = (
                        g > 0 for g in (i + 1, i, i - 1, i - 2, i - 3))
                else:
                    at = {k: eng.snap(i + k) for k in range(-3, 3)}
                    for value in at.values():
                        eng.to_reg(value)
                    self.has_in = self.has_a = self.has_b = self.has_c = self.has_d = True
                    self.again_in = self.again_a = self.again_b = self.again_c = self.again_d = True
                self.n_in, self.n_a, self.n_b, self.n_c, self.n_d = (at[k] for k in (2, 1, 0, -1, -2))
                self.prev_in, self.prev_a, self.prev_b, self.prev_c, self.prev_d = (at[k] for k in (1, 0, -1, -2, -3))

        def run(eng, iteration):
            for i in range(-1, 4):
                iteration(i)
            with eng.Fori(4, B - 1) as i:
                iteration(i)
            for i in range(B - 1, B + 3):
                iteration(i)

        block = ctx.enter_context(nc.Block())

        @block.sync
        def _(sp):
            for dst, src in ((w_raw, weights), (vec[:], vecs), (bn_eps_sb[:], bn_eps), (ident_f[:], ident),
                             (edge_w_sb, edge_w), (edge_f_sb, edge_f), (bias_sb, bias_rows),
                             (gin_b2_sb[:], gin_b2), (rel_b_sb[:], rel_b), (mask_sb[:], masks)):
                sp.dma_start(dst, src).then_inc(s["consts"], 16)

            def iteration(i):
                c = Counts(sp, i)
                if c.has_in:
                    g = i + 1
                    if c.again_in:
                        sp.wait_ge(s["a_lo_done"], c.prev_in)
                    sp.dma_start(a_in[:], adj[g].rearrange("(t p) m -> p t m", p=P)).then_inc(s["a_loaded"], 16)
                    if c.again_in:
                        sp.wait_ge(s["x_lo_done"], c.prev_in)
                        sp.wait_ge(s["xT_lo_done"], c.prev_in)
                        sp.wait_ge(s["x_bias_done"], c.prev_in)
                    sp.dma_start(x_in[:], x[g].rearrange("(t p) c -> p t c", p=P)).then_inc(s["x_loaded"], 16)
                    sp.dma_start(xT_in[:], xT[g]).then_inc(s["x_loaded"], 16)
                    if c.again_in:
                        sp.wait_ge(s["at_lo_done"], c.prev_in)
                    sp.dma_start(at_in[:], adjT[g].rearrange("(t p) m -> p t m", p=P)).then_inc(s["at_loaded"], 16)
                if c.has_b:
                    if c.again_b:
                        sp.wait_ge(kern_done[T - 1], c.prev_b)
                    else:
                        sp.wait_ge(s["ranks_done"], 1)
                    sp.dma_start(at_keep[:], adjT[i - 1].rearrange("(t p) m -> p t m", p=P))\
                        .then_inc(s["at_kept"], 16)
                if c.has_d:
                    sp.wait_ge(s["result_done"], c.n_d)
                    sp.dma_start(out[i - 3].rearrange("(t p) c -> p t c", p=P), result[:]).then_inc(s["stored"], 16)

            run(sp, iteration)
            sp.wait_ge(s["stored"], 16 * B)

        NCONST = 10 * 16

        @block.gpsimd
        def _(pool):
            pool.wait_ge(s["consts"], NCONST)
            nc.gpsimd.memset(feat_cols[:], 0.0).then_inc(s["consts_set"], 1)
            nc.gpsimd.tensor_copy(ident_h[:], ident_f[:]).then_inc(s["consts_set"], 1)
            nc.gpsimd.tensor_copy(ident_b[:], ident_f[:]).then_inc(s["consts_set"], 1)
            nc.gpsimd.memset(ones2[:], SX).then_inc(s["consts_set"], 1)
            nc.gpsimd.memset(h1_hi[:], 0.0).then_inc(s["consts_set"], 1)
            nc.gpsimd.memset(h1_lo[:], 0.0).then_inc(s["consts_set"], 1)
            nc.gpsimd.memset(sum_cols[:], SX).then_inc(s["consts_set"], 1)
            pool.wait_ge(s["consts_set"], 7)
            left_ones = feat_cols[:, :, 0:KD].rearrange("p t (a b d) -> p t a b d", a=3, b=3)
            nc.gpsimd.memset(left_ones[:, :, 0, :, 3], 1.0).then_inc(s["consts_set"], 1)

            steps = [0]

            def step(ins):
                steps[0] += 1
                return ins.then_inc(pool_step, 1)

            def lo_part(dst, src, hi):
                return nc.gpsimd.tensor_tensor(dst, src, hi, ALU.subtract)

            def newton_steps(k, gain):
                y_, a_, t_ = rstd[k][:], newton[k][:], newton_t[k][:]
                step(nc.gpsimd.tensor_tensor(a_, y_, y_, ALU.mult))
                pool.wait_ge(pool_step, steps[0])
                step(nc.gpsimd.tensor_tensor(a_, a_, half_var[k][:], ALU.mult))
                pool.wait_ge(pool_step, steps[0])
                step(nc.gpsimd.tensor_scalar(a_, a_, -1.0, 1.5, ALU.mult, ALU.add))
                pool.wait_ge(pool_step, steps[0])
                step(nc.gpsimd.tensor_tensor(y_, y_, a_, ALU.mult))
                pool.wait_ge(pool_step, steps[0])
                step(nc.gpsimd.tensor_tensor(a_, y_, y_, ALU.mult))
                pool.wait_ge(pool_step, steps[0])
                step(nc.gpsimd.tensor_tensor(a_, a_, half_var[k][:], ALU.mult))
                pool.wait_ge(pool_step, steps[0])
                step(nc.gpsimd.tensor_scalar(t_, a_, 1.5, -2.5, ALU.mult, ALU.add))
                pool.wait_ge(pool_step, steps[0])
                step(nc.gpsimd.tensor_tensor(t_, t_, a_, ALU.mult))
                pool.wait_ge(pool_step, steps[0])
                step(nc.gpsimd.tensor_scalar(t_, t_, 1.875, gain, ALU.add, ALU.mult))
                pool.wait_ge(pool_step, steps[0])
                step(nc.gpsimd.tensor_tensor(y_, y_, t_, ALU.mult))
                pool.wait_ge(pool_step, steps[0])
                return nc.gpsimd.tensor_tensor(shift[k][:], minus_mean[k][:], y_, ALU.mult)

            def iteration(i):
                c = Counts(pool, i)
                if c.has_d:
                    pool.wait_ge(cand_done[T - 1], c.n_d)
                    step(nc.gpsimd.tensor_tensor(x_minus, x3_true[:], cand[:], ALU.subtract))
                    nc.gpsimd.tensor_tensor(x_plus, x3_true[:], cand[:], ALU.add).then_inc(s["mix_done"], 1)
                if c.has_d:
                    pool.wait_ge(seed_done[3], c.n_d)
                    newton_steps(3, 1.0).then_inc(norm_done[3], 1)
                if c.has_c:
                    pool.wait_ge(s["h1_hi_done"], c.n_c)
                    lo_part(h1_lo[:, PAD:PAD + N], h1, h1_hi[:, PAD:PAD + N]).then_inc(s["h1_lo_done"], 1)
                if c.has_b:
                    pool.wait_ge(s["gcn2_done"], c.n_b)
                    nc.gpsimd.tensor_tensor(y2[:], gcn2_out[:], x1_skip[:], ALU.add).then_inc(s["y2_done"], 1)
                if c.has_c:
                    pool.wait_ge(kern_hi_done[0], c.n_c)
                    lo_part(kern_lo[:, 0], kern[:, 0], kern_hi[:, 0])
                if c.has_b:
                    pool.wait_ge(seed_done[1], c.n_b)
                    newton_steps(1, SX).then_inc(norm_done[1], 1)
                if c.has_c:
                    pool.wait_ge(kern_hi_done[1], c.n_c)
                    lo_part(kern_lo[:, 1], kern[:, 1], kern_hi[:, 1])
                if c.has_a:
                    pool.wait_ge(seed_done[0], c.n_a)
                    newton_steps(0, SX).then_inc(norm_done[0], 1)
                if c.has_c:
                    for t in range(2, T):
                        pool.wait_ge(kern_hi_done[t], c.n_c)
                        ins = lo_part(kern_lo[:, t], kern[:, t], kern_hi[:, t])
                    ins.then_inc(s["kern_lo_done"], 1)
                    pool.wait_ge(s["msg_hi_done"], c.n_c)
                    lo_part(msg_lo[:], msg, msg_hi[:]).then_inc(s["msg_lo_done"], 1)
                if c.has_b:
                    pool.wait_ge(s["x2_done"], c.n_b)
                    nc.gpsimd.tensor_tensor(x2_bias[:], x2[:], gin_b2_sb[:].unsqueeze(1).to_broadcast([P, T, C]),
                                            ALU.add).then_inc(s["x2_bias_done"], 1)
                if c.has_in:
                    if c.again_in:
                        pool.wait_ge(s["y1_done"], c.prev_in)
                    pool.wait_ge(s["x_hi_done"], c.n_in)
                    nc.gpsimd.tensor_tensor(x_bias[:], x_in[:], rel_b_sb[:], ALU.add).then_inc(s["x_bias_done"], 1)
                if c.has_c:
                    pool.wait_ge(s["xc_hi_done"], c.n_c)
                    lo_part(xc_lo[:], xc, xc_hi[:]).then_inc(s["xc_lo_done"], 1)
                if c.has_a:
                    pool.wait_ge(s["g1_hi_done"], c.n_a)
                    lo_part(g1_lo[:], g1, g1_hi[:]).then_inc(s["g1_lo_done"], 1)
                if c.has_b:
                    pool.wait_ge(seed_done[2], c.n_b)
                    newton_steps(2, SX).then_inc(norm_done[2], 1)
                if steps[0]:
                    pool.wait_ge(pool_step, steps[0])
                    pool.sem_clear(pool_step)
                    steps[0] = 0

            run(pool, iteration)

        @block.scalar
        def _(act):
            act.wait_ge(s["weights_folded"], 1)
            nc.scalar.activation(w_hi[:], w_raw, ACT.Copy, scale=SW).then_inc(s["w_hi_done"], 1)

            def hi_from(dst, src, scale=DOWN):
                return nc.scalar.activation(dst, src, ACT.Copy, scale=scale)

            def adjacency(src, hi, first, node_tiles):
                for t in node_tiles:
                    ins = nc.scalar.activation(hi[:, t], src[:, t], ACT.Copy, scale=SW,
                                               accum_out=sums[:, first + t:first + t + 1])
                return ins

            def normalize(k, src, dst):
                for t in range(T):
                    ins = nc.scalar.activation(dst[:, t], src[:, t], ACT.Identity, scale=rstd[k][:, t:t + 1],
                                               bias=shift[k][:, t:t + 1])
                return ins

            def distance_exp(t, c):
                act.wait_ge(dist_psum[t], c.n_c)
                if t >= 2:
                    act.wait_ge(kern_done[t - 2], c.n_c)
                nc.scalar.activation(expd[:, t % 2], dist_bank[t], ACT.Exp, bias=feat[:, t, 3:4])\
                    .then_inc(exp_done[t], 1)

            def kernel_hi(t, c):
                act.wait_ge(kern_done[t], c.n_c)
                hi_from(kern_hi[:, t], kern[:, t], 1.0).then_inc(kern_hi_done[t], 1)

            def iteration(i):
                c = Counts(act, i)
                loaded = 16 * c.n_in if isinstance(i, int) else act.snap(i * 16 + 32)
                loaded_x = 32 * c.n_in if isinstance(i, int) else act.snap(i * 32 + 64)

                def gru(t):
                    act.wait_ge(gru_psum[t], c.n_c)
                    nc.scalar.activation(gates[:, t], gru_bank[t][:, C:3 * C], ACT.Tanh, scale=0.5 / (SX * SW))\
                        .then_inc(gates_done[t], 1)
                    act.wait_ge(n_pre_done[t], c.n_c)
                    nc.scalar.activation(cand[:, t], n_pre[:, t % 2], ACT.Tanh, scale=1.0 / (SX * SW))\
                        .then_inc(cand_done[t], 1)

                if c.has_a:
                    act.wait_ge(s["ax_psum"], c.n_a)
                    hi_from(ax_hi[:], pa[:, 0]).then_inc(s["ax_hi_done"], 1)
                if c.has_c:
                    act.wait_ge(s["x3T_psum"], c.n_c)
                    hi_from(x3T[:], pb[:, 0], 1.0).then_inc(s["x3T_done"], 1)
                    hi_from(x3T_hi[:], pb[:, 0], 1.0).then_inc(s["x3T_hi_done"], 1)
                if c.has_a:
                    act.wait_ge(s["atx_psum"], c.n_a)
                    hi_from(atx_hi[:], pa[:, 1]).then_inc(s["atx_hi_done"], 1)
                    act.wait_ge(s["sum_psum"], c.n_a)
                    hi_from(sum_rows[:], pa[:, 2].bitcast(F16)[0:NROW, 0:P], 1.0).then_inc(s["sum_rows_done"], 1)
                if c.has_c:
                    act.wait_ge(s["conv1_psum"], c.n_c)
                    nc.scalar.activation(h1, pc[:, 0], ACT.Relu, scale=conv1_scale[:], bias=conv1_shift[:])\
                        .then_inc(s["h1_done"], 1)
                    act.wait_ge(s["h1_done"], c.n_c)
                    hi_from(h1_hi[:, PAD:PAD + N], h1, 1.0).then_inc(s["h1_hi_done"], 1)
                if c.has_in:
                    if c.again_in:
                        act.wait_ge(s["sum_psum"], c.prev_in)
                    act.wait_ge(s["a_loaded"], loaded)
                    adjacency(a_in, a_hi, 0, range(0, 2))
                if c.has_b:
                    act.wait_ge(s["p2_psum"], c.n_b)
                    hi_from(p2_hi[:], pb[:, 0]).then_inc(s["p2_hi_done"], 1)
                if c.has_in:
                    adjacency(a_in, a_hi, 0, range(2, T)).then_inc(s["a_hi_done"], 1)
                if c.has_c:
                    act.wait_ge(s["featT_psum"], c.n_c)
                    hi_from(left_rows[:], pc[:, 0].bitcast(BF16)[0:KD, 0:N], 1.0).then_inc(s["left_done"], 1)
                if c.has_d:
                    if c.again_d:
                        act.wait_ge(s["stored"], c.prev_d * 16)
                    act.wait_ge(norm_done[3], c.n_d)
                    normalize(3, y4, result).then_inc(s["result_done"], 1)
                if c.has_b:
                    act.wait_ge(s["gcn2_psum"], c.n_b)
                    nc.scalar.activation(relu_part[:], tiles(pb[:, 1]), ACT.Relu, scale=(1.0 - LRELU) * DOWN)\
                        .then_inc(s["relu2_done"], 1)
                if c.has_in:
                    act.wait_ge(s["x_loaded"], loaded_x)
                    hi_from(x_hi[:], x_in[:], SX).then_inc(s["x_hi_done"], 1)
                if c.has_c:
                    distance_exp(0, c)
                    distance_exp(1, c)
                    kernel_hi(0, c)
                if c.has_in:
                    if c.again_in:
                        act.wait_ge(rel_psum[T - 1], c.prev_in)
                    hi_from(xT_hi[:], xT_in[:], SX).then_inc(s["xT_hi_done"], 1)
                if c.has_c:
                    distance_exp(2, c)
                    kernel_hi(1, c)
                    distance_exp(3, c)
                    act.wait_ge(s["msg_psum"], c.n_c)
                    nc.scalar.activation(msg, tiles(pc[:, 0]), ACT.Relu, scale=DOWN).then_inc(s["msg_done"], 1)
                if c.has_b:
                    act.wait_ge(norm_done[1], c.n_b)
                    normalize(1, y2, x2).then_inc(s["x2_done"], 1)
                    act.wait_ge(s["x2_done"], c.n_b)
                    hi_from(x2_hi[:], x2[:], 1.0).then_inc(s["x2_hi_done"], 1)
                if c.has_c:
                    kernel_hi(2, c)
                    act.wait_ge(s["msg_done"], c.n_c)
                    hi_from(msg_hi[:], msg, 1.0).then_inc(s["msg_hi_done"], 1)
                if c.has_a:
                    act.wait_ge(norm_done[0], c.n_a)
                    normalize(0, y1, x1).then_inc(s["x1_done"], 1)
                    act.wait_ge(s["x1_done"], c.n_a)
                    hi_from(x1_hi[:], x1[:], 1.0).then_inc(s["x1_hi_done"], 1)
                if c.has_c:
                    kernel_hi(3, c)
                    if c.again_c:
                        act.wait_ge(s["mix_done"], c.prev_c)
                    hi_from(x3_true[:], x3[:], 1.0 / SX).then_inc(s["x3_true_done"], 1)
                if c.has_b:
                    act.wait_ge(s["agg_psum"], c.n_b)
                    hi_from(agg_hi[:], pb[:, 0]).then_inc(s["agg_hi_done"], 1)
                if c.has_a:
                    act.wait_ge(s["p1_psum"], c.n_a)
                    hi_from(p1_hi[:], pa[:, 2]).then_inc(s["p1_hi_done"], 1)
                if c.has_in:
                    if c.again_in:
                        act.wait_ge(s["bt_done"], c.prev_in)
                    act.wait_ge(s["at_loaded"], loaded)
                    adjacency(at_in, at_hi, T, range(T)).then_inc(s["at_hi_done"], 1)
                if c.has_b:
                    for k in range(2):
                        act.wait_ge(hid_psum[k], c.n_b)
                        nc.scalar.activation(hid[:, k], pb[:, 1 - k], ACT.Relu, scale=DOWN, bias=gin_b1[:, k:k + 1])\
                            .then_inc(hid_done[k], 1)
                    for k in range(2):
                        act.wait_ge(hid_done[k], c.n_b)
                        hi_from(hid_hi[:, k], hid[:, k], 1.0).then_inc(hid_hi_done[k], 1)
                if c.has_c:
                    act.wait_ge(s["conv_sum_done"], c.n_c)
                    nc.scalar.activation(xc, conv_sum, ACT.Relu, bias=conv2_shift[:]).then_inc(s["xc_done"], 1)
                    act.wait_ge(s["xc_done"], c.n_c)
                    hi_from(xc_hi[:], xc, 1.0).then_inc(s["xc_hi_done"], 1)
                if c.has_a:
                    for k in range(2):
                        bank = pa[:, k].rearrange("p (t h c) -> p t h c", t=2, h=2)
                        act.wait_ge(gcn1_psum[k], c.n_a)
                        nc.scalar.activation(relu_part[:, 2 * k:2 * k + 2], bank[:, :, 0], ACT.Relu,
                                             scale=(1.0 - LRELU) * DOWN).then_inc(relu1_done[k], 1)
                    act.wait_ge(s["g1_done"], c.n_a)
                    hi_from(g1_hi[:], g1, 1.0).then_inc(s["g1_hi_done"], 1)
                if c.has_c:
                    act.wait_ge(s["nmp_psum"], c.n_c)
                    hi_from(nmp_hi[:], pc[:, 0], 1.0 / SE).then_inc(s["nmp_hi_done"], 1)
                    gru(0)
                    gru(1)
                    gru(2)
                if c.has_b:
                    act.wait_ge(norm_done[2], c.n_b)
                    normalize(2, y3, x3).then_inc(s["x3_done"], 1)
                if c.has_c:
                    gru(3)

            run(act, iteration)

        @block.vector
        def _(dve):
            v = nc.vector
            steps = [0]

            def step(ins):
                steps[0] += 1
                ins.then_inc(dve_step, 1)
                return steps[0]

            def rsqrt(dst, src, tmp, gain):
                step(v.tensor_scalar(dst.bitcast(I32), src.bitcast(I32), -0.5, RSQRT_SEED, ALU.mult, ALU.add))
                for k in range(3):
                    dve.wait_ge(dve_step, steps[0])
                    step(v.scalar_tensor_tensor(out=tmp, in0=dst, scalar=-0.5, in1=dst, op0=ALU.mult, op1=ALU.mult))
                    dve.wait_ge(dve_step, steps[0])
                    step(v.tensor_tensor(tmp, tmp, src, ALU.mult))
                    dve.wait_ge(dve_step, steps[0])
                    step(v.scalar_tensor_tensor(out=dst, in0=tmp, scalar=1.5, in1=dst, op0=ALU.add, op1=ALU.mult))
                if gain != 1.0:
                    dve.wait_ge(dve_step, steps[0])
                    step(v.tensor_scalar(dst, dst, gain, None, ALU.mult))

            dve.wait_ge(s["consts"], NCONST)
            step(v.tensor_tensor(bn_tmp[:], vec[:, VEC_VAR:VEC_VAR + 4], bn_eps_sb[:], ALU.add))
            dve.wait_ge(dve_step, steps[0])
            step(v.tensor_copy(bn_shift[:], bn_tmp[:]))
            dve.wait_ge(dve_step, steps[0])
            rsqrt(bn_scale[:], bn_shift[:], bn_tmp[:], 1.0)
            dve.wait_ge(dve_step, steps[0])
            step(v.tensor_tensor(bn_scale[:], bn_scale[:], vec[:, VEC_GAMMA:VEC_GAMMA + 4], ALU.mult))
            dve.wait_ge(dve_step, steps[0])
            step(v.tensor_tensor(bn_tmp[:], bn_scale[:], vec[:, VEC_MEAN:VEC_MEAN + 4], ALU.mult))
            dve.wait_ge(dve_step, steps[0])
            step(v.tensor_tensor(bn_shift[:], vec[:, VEC_BETA:VEC_BETA + 4], bn_tmp[:], ALU.subtract))
            dve.wait_ge(dve_step, steps[0])
            for k in range(2):
                step(v.tensor_copy(shift_bc[:, k], bn_shift[:, k:k + 1].to_broadcast([P, NROW])))
            dve.wait_ge(dve_step, steps[0])
            dve_count_vectors = steps[0]
            step(v.tensor_scalar(conv1_scale[:], bn_scale[:, 2:3], DOWN, None, ALU.mult))
            step(v.tensor_scalar(conv2_scale[:], bn_scale[:, 3:4], DOWN, None, ALU.mult))
            step(v.tensor_scalar(conv1_shift[:], bn_shift[:, 2:3], SX, None, ALU.mult))
            step(v.tensor_scalar(conv2_shift[:], bn_shift[:, 3:4], SX, None, ALU.mult))
            step(v.tensor_scalar(gin_b1[:], vec[:, VEC_B1:VEC_B1 + 2], SX, None, ALU.mult))
            step(v.tensor_scalar(gin_b2_sb[:], gin_b2_sb[:], SX, None, ALU.mult))
            v.tensor_copy(bn_tmp[:, 0:1], bn_shift[:, 0:1]).then_inc(s["vectors_done"], 1)
            step(v.tensor_scalar(bn_tmp[:, 1:2], vec[:, VEC_EPS:VEC_EPS + 1], 1.0, None, ALU.add))
            dve.wait_ge(dve_step, steps[0])
            a, b = WCOLS["eye"]
            step(v.tensor_scalar(w_raw[:, a:b], ident_f[:], bn_tmp[:, 1:2], None, ALU.mult))
            dve.wait_ge(s["rank_psum"], 1)
            a, b = WCOLS["gcn1"]
            step(v.tensor_scalar(w_raw[:, a:b], w_raw[:, a:b], bn_scale[:, 0:1], None, ALU.mult))
            a, b = WCOLS["gcn2"]
            v.tensor_scalar(w_raw[:, a:b], w_raw[:, a:b], bn_scale[:, 1:2], None, ALU.mult)\
                .then_inc(s["weights_folded"], 1)

            def place(dst, cols, mask_hi, mask_lo, rows):
                step(v.tensor_scalar(dst, rows_hi[0:rows, cols], mask_sb[0:rows, mask_hi:mask_hi + 1], None, ALU.mult))
                dve.wait_ge(dve_step, steps[0])
                step(v.scalar_tensor_tensor(out=dst, in0=rows_lo[0:rows, cols],
                                            scalar=mask_sb[0:rows, mask_lo:mask_lo + 1], in1=dst,
                                            op0=ALU.mult, op1=ALU.add))

            def split_rows(width):
                dve.wait_ge(dve_step, steps[0])
                step(v.tensor_scalar(rows_hi[:, 0:width], rows_f[:, 0:width], SW, None, ALU.mult))
                dve.wait_ge(dve_step, steps[0])
                step(v.scalar_tensor_tensor(out=rows_lo[:, 0:width], in0=rows_f[:, 0:width], scalar=SW,
                                            in1=rows_hi[:, 0:width], op0=ALU.mult, op1=ALU.subtract))
                dve.wait_ge(dve_step, steps[0])

            def both(mask):
                return mask_sb[:, mask:mask + 1]

            step(v.tensor_copy(rows_f[:, 0:N], pa[0:NROW, 0]))
            step(v.tensor_copy(rows_f[:, N:NREL * C], pa[0:NROW, 1, 0:NREL * C - N]))
            split_rows(NREL * C)
            for t in range(T):
                place(rank_rel[:, t, 0:2 * C], slice(0, 2 * C), MASK_HI_ROW + t, MASK_LO_ROW + t, NROW)
                place(rank_rel[:, t, 2 * C:4 * C], slice(2 * C, 4 * C), MASK_HI_COL + t, MASK_LO_COL + t, NROW)
                place(rank_rel[:, t, 4 * C:], slice(4 * C, NREL * C), MASK_HI_ONE, MASK_LO_ONE, NROW)
            dve.wait_ge(dve_step, steps[0])
            step(v.tensor_scalar(rows_b[:, 0:3 * C], bias_sb[:, 0:3 * C], both(MASK_ONE), None, ALU.mult))
            dve.wait_ge(dve_step, steps[0])
            step(v.scalar_tensor_tensor(out=rows_f[:, 0:3 * C], in0=pa[0:NROW, 2, 0:3 * C], scalar=both(MASK_ROW),
                                        in1=rows_b[:, 0:3 * C], op0=ALU.mult, op1=ALU.add))
            split_rows(3 * C)
            step(v.tensor_tensor(rows_b[:, 0:T], mask_sb[:, MASK_HI_ROW:MASK_HI_ROW + T],
                                 both(MASK_HI_ONE).to_broadcast([NROW, T]), ALU.add))
            step(v.tensor_tensor(rows_b[:, T:2 * T], mask_sb[:, MASK_LO_ROW:MASK_LO_ROW + T],
                                 both(MASK_LO_ONE).to_broadcast([NROW, T]), ALU.add))
            dve.wait_ge(dve_step, steps[0])
            for t in range(T):
                for dst, lo_c, hi_c in ((rank_gcn1, 0, 2 * C), (rank_gcn2, 2 * C, 3 * C)):
                    step(v.tensor_scalar(dst[:, t], rows_hi[:, lo_c:hi_c], rows_b[:, t:t + 1], None, ALU.mult))
                    dve.wait_ge(dve_step, steps[0])
                    step(v.scalar_tensor_tensor(out=dst[:, t], in0=rows_lo[:, lo_c:hi_c],
                                                scalar=rows_b[:, T + t:T + t + 1], in1=dst[:, t],
                                                op0=ALU.mult, op1=ALU.add))
            dve.wait_ge(dve_step, steps[0])
            ih, hh = BCOLS["ih"][0], BCOLS["hh"][0]
            step(v.tensor_copy(rows_f[:, 0:C], bias_sb[:, ih:ih + C]))
            step(v.tensor_tensor(rows_f[:, C:3 * C], bias_sb[:, ih + C:ih + 3 * C], bias_sb[:, hh:hh + 2 * C], ALU.add))
            step(v.tensor_copy(rows_f[:, 3 * C:4 * C], bias_sb[:, hh + 2 * C:hh + 3 * C]))
            step(v.tensor_copy(rows_f[:, 4 * C:5 * C + 4], bias_sb[:, BCOLS["msg"][0]:BCOLS["se"][1]]))
            split_rows(5 * C + 4)
            place(rank_gru[:], slice(0, 4 * C), MASK_FIRST, MASK_SECOND, 2)
            place(rank_msg[:], slice(4 * C, 5 * C + 4), MASK_FIRST, MASK_SECOND, 2)
            dve.wait_ge(dve_step, steps[0])
            v.tensor_copy(bn_tmp[:, 0:1], bn_shift[:, 0:1]).then_inc(s["ranks_done"], 1)
            dve.wait_ge(s["w_hi_done"], 1)
            v.scalar_tensor_tensor(out=w_lo[:], in0=w_raw, scalar=SW, in1=w_hi[:], op0=ALU.mult,
                                   op1=ALU.subtract).then_inc(s["w_lo_done"], 1)
            dve.wait_ge(s["w_lo_done"], 1)
            dve.wait_ge(s["ranks_done"], 1)
            dve.wait_ge(s["consts_set"], 8)
            dve.wait_ge(dve_step, steps[0])
            v.sem_clear(dve_step)
            steps[0] = 0

            def lo_from(dst, src, hi, scale=DOWN):
                return v.scalar_tensor_tensor(out=dst, in0=src, scalar=scale, in1=hi, op0=ALU.mult,
                                              op1=ALU.subtract)

            def norm_stats(k, src, src_scale):
                for t in range(T):
                    step(v.bn_stats(stats[k][:, t], src[:, t]))
                dve.wait_ge(dve_step, steps[0])
                for t in range(T):
                    step(v.bn_aggr(mean_var[k][:, t], stats[k][:, t]))
                dve.wait_ge(dve_step, steps[0])
                halved = step(v.tensor_scalar(half_var[k][:], mean_var[k][:, :, 1], LN_EPS * src_scale * src_scale,
                                              0.5, ALU.add, ALU.mult))
                step(v.tensor_scalar(minus_mean[k][:], mean_var[k][:, :, 0], -1.0, None, ALU.mult))
                dve.wait_ge(dve_step, halved)
                return v.tensor_scalar(rstd[k][:].bitcast(I32), half_var[k][:].bitcast(I32), -0.5, HALF_SEED,
                                       ALU.mult, ALU.add)

            def iteration(i):
                c = Counts(dve, i)
                kept = 16 * c.n_c if isinstance(i, int) else dve.snap(i * 16 - 16)

                def relation_max(t):
                    f = 2 if t % 2 == 0 else 0
                    seven = pa[:, f:f + 2].rearrange("p b n -> p (b n)")[:, 0:NREL * C]
                    dve.wait_ge(rel_psum[t], c.n_a)
                    v.tensor_reduce(rel_max[:, t], seven.rearrange("p (r c) -> p c r", r=NREL), AX_X, ALU.max)\
                        .then_inc(rel_read[t], 1)

                def kernel_tile(t):
                    dve.wait_ge(exp_done[t], c.n_c)
                    if t == 0:
                        dve.wait_ge(s["at_kept"], kept)
                    v.scalar_tensor_tensor(out=kern[:, t], in0=expd[:, t % 2], scalar=SE, in1=at_keep[:, t],
                                           op0=ALU.mult, op1=ALU.mult).then_inc(kern_done[t], 1)

                def gru(t):
                    dve.wait_ge(gates_done[t], c.n_c)
                    step(v.scalar_tensor_tensor(out=reset_n[:, t % 2], in0=gates[:, t, 0:C], scalar=1.0,
                                                in1=gru_bank[t][:, 3 * C:4 * C], op0=ALU.add, op1=ALU.mult))
                    dve.wait_ge(dve_step, steps[0])
                    v.scalar_tensor_tensor(out=n_pre[:, t % 2], in0=reset_n[:, t % 2], scalar=0.5,
                                           in1=gru_bank[t][:, 0:C], op0=ALU.mult, op1=ALU.add)\
                        .then_inc(n_pre_done[t], 1)

                if c.has_a:
                    dve.wait_ge(s["ax_hi_done"], c.n_a)
                    lo_from(ax_lo[:], pa[:, 0], ax_hi[:]).then_inc(s["ax_lo_done"], 1)
                if c.has_c:
                    dve.wait_ge(s["x3T_hi_done"], c.n_c)
                    v.tensor_tensor(x3T_lo[:], x3T[:], x3T_hi[:], ALU.subtract).then_inc(s["x3T_lo_done"], 1)
                if c.has_d:
                    dve.wait_ge(s["mix_done"], c.n_d)
                    step(v.scalar_tensor_tensor(out=x_minus, in0=gates[:, :, C:2 * C], scalar=1.0, in1=x_minus,
                                                op0=ALU.add, op1=ALU.mult))
                    dve.wait_ge(dve_step, steps[0])
                    v.scalar_tensor_tensor(out=y4, in0=x_plus, scalar=2.0, in1=x_minus,
                                           op0=ALU.mult, op1=ALU.add).then_inc(s["y4_done"], 1)
                    dve.wait_ge(s["y4_done"], c.n_d)
                    norm_stats(3, y4, 2.0).then_inc(seed_done[3], 1)
                if c.has_a:
                    dve.wait_ge(s["atx_hi_done"], c.n_a)
                    lo_from(atx_lo[:], pa[:, 1], atx_hi[:]).then_inc(s["atx_lo_done"], 1)
                if c.has_c:
                    dve.wait_ge(s["feat_psum"], c.n_c)
                    pf = pb[:, 1, 0:4 * T].rearrange("p (t d) -> p t d", t=T)
                    v.tensor_scalar(feat[:, :, 0:3], pf[:, :, 0:3], 2.0 / (SX * SW), None, ALU.mult)\
                        .then_inc(s["feat_read"], 1)
                    dve.wait_ge(s["feat_read"], c.n_c)
                    step(v.scalar_tensor_tensor(out=feat_sq[:], in0=feat[:, :, 0:3], scalar=-0.25,
                                                in1=feat[:, :, 0:3], op0=ALU.mult, op1=ALU.mult))
                    dve.wait_ge(dve_step, steps[0])
                    step(v.tensor_reduce(feat[:, :, 3], feat_sq[:], AX_X, ALU.add))
                    dve.wait_ge(dve_step, steps[0])
                    step(v.tensor_copy(feat_parts[:, :, 0], feat[:]))
                    dve.wait_ge(dve_step, steps[0])
                    step(v.tensor_tensor(feat_rest[:], feat[:], feat_parts[:, :, 0], ALU.subtract))
                    dve.wait_ge(dve_step, steps[0])
                    step(v.tensor_copy(feat_parts[:, :, 1], feat_rest[:]))
                    dve.wait_ge(dve_step, steps[0])
                    step(v.tensor_tensor(feat_parts[:, :, 2], feat_rest[:], feat_parts[:, :, 1], ALU.subtract))
                    dve.wait_ge(dve_step, steps[0])
                    right = feat_cols[:, :, KD_RIGHT:KD_RIGHT + KD].rearrange("p t (a q) -> p t a q", a=3)
                    step(v.tensor_copy(right, feat_parts[:].rearrange("p t b d -> p t (b d)").unsqueeze(2)
                                       .to_broadcast([P, T, 3, 12])))
                    left = feat_cols[:, :, 0:KD].rearrange("p t (a b d) -> p t a b d", a=3, b=3)
                    for a in range(3):
                        ins = v.tensor_scalar(left[:, :, a, :, 0:3],
                                              feat_parts[:, :, a, 0:3].unsqueeze(2).to_broadcast([P, T, 3, 3]),
                                              0.5, None, ALU.mult)
                    ins.then_inc(s["feat_cols_done"], 1)
                if c.has_b:
                    dve.wait_ge(s["p2_hi_done"], c.n_b)
                    lo_from(p2_lo[:], pb[:, 0], p2_hi[:]).then_inc(s["p2_lo_done"], 1)
                if c.has_a:
                    relation_max(0)
                if c.has_c:
                    dve.wait_ge(s["featT_psum"], c.n_c)
                    v.tensor_copy(right_rows[:], pc[:, 0].bitcast(BF16)[KD_RIGHT:KD_RIGHT + KD, 0:N])\
                        .then_inc(s["right_done"], 1)
                if c.has_a:
                    relation_max(1)
                if c.has_b:
                    dve.wait_ge(s["relu2_done"], c.n_b)
                    v.scalar_tensor_tensor(out=gcn2_out[:], in0=tiles(pb[:, 1]), scalar=LRELU * DOWN,
                                           in1=relu_part[:], op0=ALU.mult, op1=ALU.add).then_inc(s["gcn2_done"], 1)
                if c.has_a:
                    relation_max(2)
                if c.has_c:
                    kernel_tile(0)
                if c.has_b:
                    dve.wait_ge(s["y2_done"], c.n_b)
                    norm_stats(1, y2, SX).then_inc(seed_done[1], 1)
                if c.has_a:
                    relation_max(3)
                if c.has_c:
                    kernel_tile(1)
                if c.has_a:
                    dve.wait_ge(s["x_bias_done"], c.n_a)
                    dve.wait_ge(rel_read[T - 1], c.n_a)
                    v.scalar_tensor_tensor(out=y1[:], in0=rel_max[:], scalar=1.0 / (SX * SW), in1=x_bias[:],
                                           op0=ALU.mult, op1=ALU.add).then_inc(s["y1_done"], 1)
                    dve.wait_ge(s["y1_done"], c.n_a)
                    norm_stats(0, y1, 1.0).then_inc(seed_done[0], 1)
                if c.has_c:
                    kernel_tile(2)
                    kernel_tile(3)
                if c.has_in:
                    dve.wait_ge(s["x_hi_done"], c.n_in)
                    lo_from(x_lo[:], x_in[:], x_hi[:], SX).then_inc(s["x_lo_done"], 1)
                if c.has_b:
                    dve.wait_ge(s["x2_hi_done"], c.n_b)
                    v.tensor_tensor(x2_lo[:], x2[:], x2_hi[:], ALU.subtract).then_inc(s["x2_lo_done"], 1)
                if c.has_in:
                    dve.wait_ge(s["a_hi_done"], c.n_in)
                    lo_from(a_lo[:], a_in[:], a_hi[:], SW).then_inc(s["a_lo_done"], 1)
                    dve.wait_ge(s["xT_hi_done"], c.n_in)
                    lo_from(xT_lo[:], xT_in[:], xT_hi[:], SX).then_inc(s["xT_lo_done"], 1)
                if c.has_a:
                    dve.wait_ge(s["x1_hi_done"], c.n_a)
                    v.tensor_tensor(x1_lo[:], x1[:], x1_hi[:], ALU.subtract).then_inc(s["x1_lo_done"], 1)
                if c.has_b:
                    dve.wait_ge(s["agg_hi_done"], c.n_b)
                    lo_from(agg_lo[:], pb[:, 0], agg_hi[:]).then_inc(s["agg_lo_done"], 1)
                if c.has_a:
                    if c.again_a:
                        dve.wait_ge(s["agg_psum"], c.prev_a)
                    step(v.tensor_copy(bt_hi[:], at_hi[:]))
                    step(v.tensor_copy(bt_lo[:], at_lo[:]))
                    v.tensor_copy(sum_rows_b[:], sum_rows[:]).then_inc(s["bt_done"], 1)
                    dve.wait_ge(s["p1_hi_done"], c.n_a)
                    lo_from(p1_lo[:], pa[:, 2], p1_hi[:]).then_inc(s["p1_lo_done"], 1)
                if c.has_in:
                    cols = sum_cols[:, 0:8 * T].rearrange("p (g k j) -> p g k j", g=2 * T, k=2)
                    scaled = sums[:].unsqueeze(2).to_broadcast([P, 2 * T, 2])
                    if c.again_in:
                        dve.wait_ge(s["sum_psum"], c.prev_in)
                    dve.wait_ge(s["at_hi_done"], c.n_in)
                    hi_cols = step(v.tensor_scalar(cols[:, :, 0], scaled, SX / SW, None, ALU.mult))
                    lo_from(at_lo[:], at_in[:], at_hi[:], SW).then_inc(s["at_lo_done"], 1)
                    dve.wait_ge(dve_step, hi_cols)
                    v.scalar_tensor_tensor(out=cols[:, :, 1], in0=scaled, scalar=SX / SW, in1=cols[:, :, 0],
                                           op0=ALU.mult, op1=ALU.subtract).then_inc(s["sum_cols_done"], 1)
                if c.has_c:
                    dve.wait_ge(s["conv2_psum"], c.n_c)
                    v.scalar_tensor_tensor(out=conv_sum, in0=pc[:, 1], scalar=conv2_scale[:], in1=x3T[:],
                                           op0=ALU.mult, op1=ALU.add).then_inc(s["conv_sum_done"], 1)
                if c.has_b:
                    for k in range(2):
                        dve.wait_ge(hid_hi_done[k], c.n_b)
                        ins = v.tensor_tensor(hid_lo[:, k], hid[:, k], hid_hi[:, k], ALU.subtract)
                    ins.then_inc(s["hid_lo_done"], 1)
                if c.has_a:
                    for k in range(2):
                        bank = pa[:, k].rearrange("p (t h c) -> p t h c", t=2, h=2)
                        pair = slice(2 * k, 2 * k + 2)
                        dve.wait_ge(relu1_done[k], c.n_a)
                        ins = v.scalar_tensor_tensor(out=g1[:, pair], in0=bank[:, :, 0], scalar=LRELU * DOWN,
                                                     in1=relu_part[:, pair], op0=ALU.mult, op1=ALU.add)
                    ins.then_inc(s["g1_done"], 1)
                    if c.again_a:
                        dve.wait_ge(s["y2_done"], c.prev_a)
                    for k in range(2):
                        bank = pa[:, k].rearrange("p (t h c) -> p t h c", t=2, h=2)
                        pair = slice(2 * k, 2 * k + 2)
                        ins = v.scalar_tensor_tensor(out=x1_skip[:, pair], in0=bank[:, :, 1], scalar=DOWN,
                                                     in1=x1[:, pair], op0=ALU.mult, op1=ALU.add)
                    ins.then_inc(s["gcn1_free"], 1)
                if c.has_c:
                    dve.wait_ge(s["nmp_hi_done"], c.n_c)
                    lo_from(nmp_lo[:], pc[:, 0], nmp_hi[:], 1.0 / SE).then_inc(s["nmp_lo_done"], 1)
                if c.has_b:
                    dve.wait_ge(s["x2_bias_done"], c.n_b)
                    dve.wait_ge(s["gin_psum"], c.n_b)
                    v.scalar_tensor_tensor(out=y3[:], in0=tiles(pb[:, 1]), scalar=DOWN, in1=x2_bias[:],
                                           op0=ALU.mult, op1=ALU.add).then_inc(s["y3_done"], 1)
                    dve.wait_ge(s["y3_done"], c.n_b)
                    norm_stats(2, y3, SX).then_inc(seed_done[2], 1)
                if c.has_c:
                    for t in range(T):
                        gru(t)
                if steps[0]:
                    dve.wait_ge(dve_step, steps[0])
                    v.sem_clear(dve_step)
                    steps[0] = 0

            run(dve, iteration)

        @block.tensor
        def _(pe):
            def product(dst, left, right, start, stop, skip=False):
                (lh, ll), (rh, rl) = left, right
                nc.tensor.matmul(dst, lh, rh, start=start, stop=False, skip_group_check=skip)
                nc.tensor.matmul(dst, lh, rl, start=False, stop=False, skip_group_check=skip)
                return nc.tensor.matmul(dst, ll, rh, start=False, stop=stop, skip_group_check=skip)

            def over_nodes(dst, left, right, stop=True):
                for t in range(T):
                    last = product(dst, (left[0][:, t], left[1][:, t]), (right[0][:, t], right[1][:, t]),
                                   start=(t == 0), stop=stop and t == T - 1)
                return last

            def nodes(pair, t):
                return pair[0][:, t * P:(t + 1) * P], pair[1][:, t * P:(t + 1) * P]

            A, AT, BT = (a_hi, a_lo), (at_hi, at_lo), (bt_hi, bt_lo)

            pe.wait_ge(s["consts"], NCONST)
            for r in range(NREL):
                nc.tensor.matmul(pa[0:NROW, r // 4, (r % 4) * C:(r % 4 + 1) * C], edge_f_sb[:, r],
                                 edge_w_sb[:, r], start=True, stop=True)
            pe.wait_ge(s["vectors_done"], 1)
            a, b = WCOLS["gcn1"]
            nc.tensor.matmul(pa[0:NROW, 2, 0:2 * C], shift_bc[:, 0], w_raw[:, a:b], start=True, stop=True)
            a, b = WCOLS["gcn2"]
            nc.tensor.matmul(pa[0:NROW, 2, 2 * C:3 * C], shift_bc[:, 1], w_raw[:, a:b], start=True, stop=True)\
                .then_inc(s["rank_psum"], 1)
            pe.wait_ge(s["w_lo_done"], 1)
            pe.wait_ge(s["ranks_done"], 1)
            pe.wait_ge(s["consts_set"], 8)

            def iteration(i):
                c = Counts(pe, i)

                def adjacency_x():
                    pe.wait_ge(s["at_lo_done"], c.n_a)
                    pe.wait_ge(s["x_lo_done"], c.n_a)
                    if c.again_a:
                        pe.wait_ge(s["gcn1_free"], c.prev_a)
                    over_nodes(pa[:, 0], (x_hi, x_lo), AT).then_inc(s["ax_psum"], 1)

                def adjacencyT_x():
                    pe.wait_ge(s["a_lo_done"], c.n_a)
                    over_nodes(pa[:, 1], (x_hi, x_lo), A).then_inc(s["atx_psum"], 1)
                    pe.wait_ge(s["consts_set"], 8)
                    pe.wait_ge(s["sum_cols_done"], c.n_a)
                    nc.tensor.transpose(pa[:, 2].bitcast(F16)[0:NROW, 0:P], sum_cols[:], ident_h[:])\
                        .then_inc(s["sum_psum"], 1)

                def relations(t):
                    f = 2 if t % 2 == 0 else 0
                    if t == 0:
                        pe.wait_ge(s["sum_rows_done"], c.n_a)
                        pe.wait_ge(s["xT_lo_done"], c.n_a)
                        pe.wait_ge(s["atx_lo_done"], c.n_a)
                    if t >= 2:
                        pe.wait_ge(rel_read[t - 2], c.n_a)
                    nc.tensor.matmul(pa[:, f], sum_rows[:], rank_rel[:, t, 0:4 * C], start=True, stop=False)
                    product(pa[:, f, 0:2 * C], nodes((ax_hi, ax_lo), t), W("rel", 0, 2 * C), False, False)
                    product(pa[:, f, 2 * C:4 * C], nodes((atx_hi, atx_lo), t), W("rel", 2 * C, 2 * C), False, True)
                    nc.tensor.matmul(pa[:, f + 1, 0:3 * C], sum_rows[:], rank_rel[:, t, 4 * C:], start=True,
                                     stop=False)
                    product(pa[:, f + 1, 0:3 * C], nodes((xT_hi, xT_lo), t), W("rel", 4 * C, 3 * C), False, True)\
                        .then_inc(rel_psum[t], 1)

                def gcn_p1():
                    pe.wait_ge(s["x1_lo_done"], c.n_a)
                    over_nodes(pa[:, 2], (x1_hi, x1_lo), AT).then_inc(s["p1_psum"], 1)

                def gcn_first():
                    pe.wait_ge(s["p1_lo_done"], c.n_a)
                    for t in range(T):
                        dst = pa[:, t // 2, (t % 2) * 2 * C:(t % 2 + 1) * 2 * C]
                        nc.tensor.matmul(dst, sum_rows[:], rank_gcn1[:, t], start=True, stop=False)
                        last = product(dst, nodes((p1_hi, p1_lo), t), W("gcn1"), False, True)
                        if t % 2:
                            last.then_inc(gcn1_psum[t // 2], 1)

                def gcn_p2():
                    pe.wait_ge(s["g1_lo_done"], c.n_b)
                    pe.wait_ge(s["bt_done"], c.n_b)
                    if c.has_c:
                        pe.wait_ge(s["x3T_hi_done"], c.n_c)
                    over_nodes(pb[:, 0], (g1_hi, g1_lo), BT).then_inc(s["p2_psum"], 1)

                def gcn_second():
                    pe.wait_ge(s["p2_lo_done"], c.n_b)
                    if c.has_c:
                        pe.wait_ge(s["feat_read"], c.n_c)
                    for t in range(T):
                        dst = tiles(pb[:, 1])[:, t]
                        nc.tensor.matmul(dst, sum_rows_b[:], rank_gcn2[:, t], start=True, stop=False)
                        last = product(dst, nodes((p2_hi, p2_lo), t), W("gcn2"), False, True)
                    last.then_inc(s["gcn2_psum"], 1)

                def gin_aggregate():
                    pe.wait_ge(s["x2_lo_done"], c.n_b)
                    if c.has_c:
                        pe.wait_ge(exp_done[T - 1], c.n_c)
                    over_nodes(pb[:, 0], (x2_hi, x2_lo), BT, stop=False)
                    for t in range(T):
                        last = product(pb[:, 0, t * P:(t + 1) * P], (x2_hi[:, t], x2_lo[:, t]), W("eye"), False,
                                       t == T - 1)
                    last.then_inc(s["agg_psum"], 1)

                def gin_hidden():
                    pe.wait_ge(s["agg_lo_done"], c.n_b)
                    for k in range(2):
                        product(pb[:, 1 - k], W("gin1", k * C, C), (agg_hi[:], agg_lo[:]), True, True)\
                            .then_inc(hid_psum[k], 1)

                def gin_out():
                    pe.wait_ge(s["hid_lo_done"], c.n_b)
                    for t in range(T):
                        dst = tiles(pb[:, 1])[:, t]
                        product(dst, nodes((hid_hi[:, 0], hid_lo[:, 0]), t), W("gin2", 0, C), True, False)
                        last = product(dst, nodes((hid_hi[:, 1], hid_lo[:, 1]), t), W("gin2", C, C), False, True)
                    last.then_inc(s["gin_psum"], 1)

                def transpose_x3():
                    pe.wait_ge(s["x3_done"], c.n_c)
                    for t in range(T):
                        last = nc.tensor.transpose(pb[:, 0, t * P:(t + 1) * P], x3[:, t], ident_f[:])
                    last.then_inc(s["x3T_psum"], 1)

                def conv1():
                    pe.wait_ge(s["x3T_lo_done"], c.n_c)
                    if c.again_c:
                        pe.wait_ge(n_pre_done[2], c.prev_c)
                    product(pc[:, 0], W("conv1"), (x3T_hi[:], x3T_lo[:]), True, True).then_inc(s["conv1_psum"], 1)

                def features():
                    for t in range(T):
                        dst = pb[:, 1, 4 * t:4 * t + 4]
                        nc.tensor.matmul(dst, ones2[:], rank_msg[:, C:C + 4], start=True, stop=False)
                        last = product(dst, nodes((x3T_hi, x3T_lo), t), W("se"), False, True)
                    last.then_inc(s["feat_psum"], 1)

                def feature_rows():
                    pe.wait_ge(s["feat_cols_done"], c.n_c)
                    pe.wait_ge(s["h1_done"], c.n_c)
                    for t in range(T):
                        last = nc.tensor.transpose(pc[:, 0].bitcast(BF16)[:, t * P:(t + 1) * P], feat_cols[:, t],
                                                   ident_b[:])
                    last.then_inc(s["featT_psum"], 1)

                def distances(t):
                    if t == 0:
                        pe.wait_ge(s["left_done"], c.n_c)
                        pe.wait_ge(s["right_done"], c.n_c)
                    if t == 1 and c.has_b:
                        pe.wait_ge(s["p2_lo_done"], c.n_b)
                    if t >= 2:
                        pe.wait_ge(exp_done[t - 2], c.n_c)
                    nc.tensor.matmul(dist_bank[t], left_rows[:, t * P:(t + 1) * P], right_rows[:], start=True,
                                     stop=True).then_inc(dist_psum[t], 1)

                def messages():
                    pe.wait_ge(exp_done[2], c.n_c)
                    for t in range(T):
                        dst = tiles(pc[:, 0])[:, t]
                        nc.tensor.matmul(dst, ones2[:], rank_msg[:, 0:C], start=True, stop=False)
                        last = product(dst, nodes((x3T_hi, x3T_lo), t), W("msg"), False, True)
                    last.then_inc(s["msg_psum"], 1)

                def conv2(taps):
                    if taps[0] == 0:
                        pe.wait_ge(s["h1_lo_done"], c.n_c)
                        if c.again_c:
                            pe.wait_ge(n_pre_done[3], c.prev_c)
                    for k in taps:
                        last = product(pc[:, 1], W("conv2", k * C, C), (h1_hi[:, k:k + N], h1_lo[:, k:k + N]),
                                       k == 0, k == TAPS - 1)
                    if taps[-1] == TAPS - 1:
                        last.then_inc(s["conv2_psum"], 1)

                def nmp():
                    pe.wait_ge(s["msg_lo_done"], c.n_c)
                    pe.wait_ge(s["kern_lo_done"], c.n_c)
                    over_nodes(pc[:, 0], (msg_hi, msg_lo), (kern_hi, kern_lo)).then_inc(s["nmp_psum"], 1)

                def gru(t):
                    if t == 0:
                        pe.wait_ge(s["nmp_lo_done"], c.n_c)
                        pe.wait_ge(s["xc_lo_done"], c.n_c)
                    else:
                        if t >= 2:
                            pe.wait_ge(n_pre_done[t - 2], c.n_c)
                    nc.tensor.matmul(gru_bank[t], ones2[:], rank_gru[:], start=True, stop=False)
                    product(gru_bank[t][:, C:4 * C], nodes((x3T_hi, x3T_lo), t), W("hh"), False, False)
                    product(gru_bank[t][:, 0:3 * C], nodes((nmp_hi, nmp_lo), t), W("ih_nmp"), False, False)
                    product(gru_bank[t][:, 0:3 * C], nodes((xc_hi, xc_lo), t), W("ih_conv"), False, True)\
                        .then_inc(gru_psum[t], 1)

                order = [("a", adjacency_x), ("c", transpose_x3), ("a", adjacencyT_x), ("c", conv1), ("c", features),
                         ("b", gcn_p2), ("a", relations, 0), ("c", feature_rows), ("a", relations, 1),
                         ("b", gcn_second), ("a", relations, 2), ("c", distances, 0), ("c", distances, 1),
                         ("a", relations, 3), ("c", conv2, range(0, 3)), ("c", distances, 2),
                         ("c", distances, 3), ("c", messages), ("c", conv2, range(3, 12)), ("b", gin_aggregate),
                         ("a", gcn_p1), ("b", gin_hidden), ("c", conv2, range(12, TAPS)), ("a", gcn_first),
                         ("c", nmp), ("b", gin_out), ("c", gru, 0), ("c", gru, 1), ("c", gru, 2), ("c", gru, 3)]
                present = {"a": c.has_a, "b": c.has_b, "c": c.has_c}
                for step_name, stage, *args in order:
                    if present[step_name]:
                        stage(*args)

            run(pe, iteration)


def kernel(**inputs):
    import numpy as _np
    import concourse.bacc as _bacc
    from concourse import mybir as _mybir
    from concourse.bass_utils import run_bass_kernel_spmd as _run

    a = {k: _np.ascontiguousarray(v) for k, v in inputs.items()}
    w_rel, w_ih, w_hh = a["L0_gnn_W"], a["L3_gnn_w_ih"], a["L3_gnn_w_hh"]
    ih_order = _np.concatenate([_np.arange(2 * C, 3 * C), _np.arange(0, 2 * C)])
    ih_t = w_ih[ih_order].T
    w_se = _np.concatenate([a["L3_gnn_w_se"].T, _np.zeros((C, 1), _np.float32)], axis=1)
    pieces = [w_rel[BLOCKS, :C].transpose(1, 0, 2).reshape(C, NREL * C),
              a["L1_gnn_w1"], a["L1_gnn_w_skip"], a["L1_gnn_w2"], a["L2_gnn_W1"],
              a["L2_gnn_W2"].reshape(2, C, C).transpose(1, 0, 2).reshape(C, 2 * C),
              a["L3_gnn_conv1_w"][:, :, 0].T,
              a["L3_gnn_conv2_w"].transpose(1, 2, 0).reshape(C, TAPS * C),
              a["L3_gnn_w_msg"].T, w_se, ih_t[:C], ih_t[C:], w_hh.T, _np.zeros((C, C), _np.float32)]
    weights = _np.ascontiguousarray(_np.concatenate(pieces, axis=1))
    bias = _np.concatenate([a["L1_gnn_b1"], a["L1_gnn_b_skip"], a["L1_gnn_b2"], a["L3_gnn_b_ih"][ih_order],
                            a["L3_gnn_b_hh"], a["L3_gnn_b_msg"], a["L3_gnn_b_se"], _np.zeros(1, _np.float32)])
    norms = ["L1_gnn_bn1_", "L1_gnn_bn2_", "L3_gnn_bn1_", "L3_gnn_bn2_"]
    vecs = [a[p + (q if "L1" in p else q[0])] for q in ("var", "gamma", "beta", "mean") for p in norms]
    vecs += [a["L2_gnn_b1"][:C], a["L2_gnn_b1"][C:], _np.broadcast_to(a["L2_gnn_eps"], (C,))]
    arrays = {
        "x": a["x"],
        "xT": _np.ascontiguousarray(a["x"].transpose(0, 2, 1)),
        "adj": a["adj"],
        "adjT": _np.ascontiguousarray(a["adj"].transpose(0, 2, 1)),
        "weights": weights,
        "edge_w": _np.ascontiguousarray(w_rel[BLOCKS, C:].transpose(1, 0, 2)),
        "edge_f": _np.ascontiguousarray(_np.broadcast_to(a["L0_gnn_W_edges"][BLOCKS].T[:, :, None], (REL, NREL, NROW))),
        "bias_rows": _np.ascontiguousarray(_np.broadcast_to(bias, (NROW, NB))),
        "vecs": _np.ascontiguousarray(_np.stack(vecs, axis=1)),
        "gin_b2": _np.ascontiguousarray(_np.broadcast_to(a["L2_gnn_b2"], (P, C))),
        "rel_b": _np.ascontiguousarray(a["L0_gnn_b"].reshape(T, P, C).transpose(1, 0, 2)),
        "ident": _np.eye(P, dtype=_np.float32),
        "masks": row_masks(),
        "bn_eps": _np.ascontiguousarray(_np.broadcast_to(_np.array([1e-3, 1e-3, 1e-5, 1e-5], _np.float32), (P, 4))),
    }
    nc = _bacc.Bacc("TRN2", target_bir_lowering=False, num_devices=1)
    feeds, args = {}, []
    for name, value in arrays.items():
        feeds[f"in_{name}_dram"] = value
        args.append(nc.dram_tensor(f"in_{name}_dram", value.shape, _mybir.dt.from_np(value.dtype),
                                   kind="ExternalInput").ap())
    args.append(nc.dram_tensor("out_dram", (B, N, C), _mybir.dt.float32, kind="ExternalOutput").ap())
    adj_resnorm(nc, *args)
    r = _run(nc, [feeds], core_ids=[0])
    return r.results[0]["out_dram"]
```

```python
from contextlib import ExitStack

import numpy as np

import concourse.bass as bass
from concourse import mybir

F32 = mybir.dt.float32
F16 = mybir.dt.float16
BF16 = mybir.dt.bfloat16
I32 = mybir.dt.int32
ALU = mybir.AluOpType
ACT = mybir.ActivationFunctionType
AX_X = mybir.AxisListType.X

P = 128
B, N, C = 16, 512, 128
T = N // P
NREL = 7
REL = 16
TAPS, PAD = 17, 8
HALF = N // 2
HPAD = HALF + PAD
SX = 16.0
SW = 256.0
SE = 1024.0
DOWN = 1.0 / SW
LRELU = 0.3
LN_EPS = 1e-5
RSQRT_SEED = 1597463007.0
HALF_SEED = RSQRT_SEED - 2 ** 22

QUAD, ROW_AT, COL_AT, ONE_AT = 32, 0, 16, 20
BLOCKS = [0, 1, 3, 4, 2, 5, 6]

WCOLS = {}
_at = 0
for _n, _w in (("rel", NREL * C), ("gcn1", 2 * C), ("gcn2", C), ("gin1", 2 * C), ("gin2", 2 * C),
               ("conv1", C), ("conv2", TAPS * C), ("msg", C), ("se", 4), ("ih_conv", 3 * C),
               ("ih_nmp", 3 * C), ("hh", 3 * C),
               ("tap_sums", TAPS // 2 * C)):
    WCOLS[_n] = (_at, _at + _w)
    _at += _w
NW = _at
NRAW = WCOLS["tap_sums"][0]
NFRONT = WCOLS["gcn2"][1]
BCOLS = {"gcn1": (0, 2 * C), "gcn2": (2 * C, 3 * C), "msg": (3 * C, 4 * C), "se": (4 * C, 4 * C + 4)}
NB = 4 * C + 4
VEC_VAR, VEC_GAMMA, VEC_BETA, VEC_MEAN, VEC_B1, VEC_EPS, VEC_IH, VEC_HH = 0, 4, 8, 12, 16, 18, 19, 22
NV = 25
MASK_ROW, LESS_ROW, MASK_COL, LESS_COL, MASK_ONE, LESS_ONE, LESS_BOTH, LESS_SECOND = range(8)
NM = 8

KD = 36
KD_RIGHT = 64


def row_masks():
    m = np.zeros((P, NM), np.float32)
    for t in range(T):
        for first, count, mask, less in ((ROW_AT, 4, MASK_ROW, LESS_ROW), (COL_AT, 4, MASK_COL, LESS_COL),
                                         (ONE_AT, 2, MASK_ONE, LESS_ONE)):
            for j in range(count):
                m[QUAD * t + first + j, mask] = SW
                m[QUAD * t + first + j, less] = -1.0 if j % 2 else 0.0
    m[:, LESS_BOTH] = m[:, LESS_ROW] + m[:, LESS_ONE]
    m[1, LESS_SECOND] = -1.0
    return m


def adj_resnorm(nc, x, xT, adj, adjT, weights, edge_w, edge_f, bias_rows, vecs, gin_b2, rel_b, ident, masks,
                bn_eps, out):
    ctx = ExitStack()
    with ctx:
        def sb(name, shape, dt=F32):
            return ctx.enter_context(nc.sbuf_tensor(name, shape, dt))

        def sem(name):
            return ctx.enter_context(nc.semaphore(name))

        shared = sb("shared", [P, NRAW + N])
        w_raw = shared[:, 0:NRAW]
        w_hi = sb("w_hi", [P, NW], F16)
        w_lo = sb("w_lo", [P, NW], F16)
        at_keep = sb("at_keep", [P, T, N])
        setup_view = at_keep[:].rearrange("p t n -> p (t n)")
        rows_f = setup_view[:, 0:NREL * C]
        rows_b = setup_view[:, NREL * C:NREL * C + 3 * C]
        gru_sums = sb("gru_sums", [P, 3, T * C])
        bias_sb = gru_sums[:].rearrange("p k n -> p (k n)")[:, 0:NB]
        vec = sb("vec", [P, NV])
        bn_eps_sb = sb("bn_eps_sb", [P, 4])
        bn_scale = sb("bn_scale", [P, 4])
        bn_shift = sb("bn_shift", [P, 4])
        bn_tmp = sb("bn_tmp", [P, 4])
        gin_b1 = sb("gin_b1", [P, 2])
        conv1_scale = sb("conv1_scale", [P, 1])
        conv1_shift = sb("conv1_shift", [P, 1])
        conv2_scale = sb("conv2_scale", [P, 1])
        conv2_shift = sb("conv2_shift", [P, 1])
        conv2_minus = sb("conv2_minus", [P, 1])
        gin_b2_sb = sb("gin_b2_sb", [P, C])
        rel_b_sb = sb("rel_b_sb", [P, T, C])
        ident_f = sb("ident_f", [P, P])
        ident_h = sb("ident_h", [P, P], F16)
        ident_b = sb("ident_b", [P, P], BF16)
        diagonal = sb("diagonal", [P, P])
        mask_sb = sb("mask_sb", [P, NM])
        kern_hi, kern_lo = sb("kern_hi", [P, T, N], F16), sb("kern_lo", [P, T, N], F16)
        rows_hi = kern_hi[:].rearrange("p t n -> p (t n)")[:, 0:NREL * C]
        rank_rel = sb("rank_rel", [P, T, NREL * C], F16)
        rank_gcn = sb("rank_gcn", [P, T, 3 * C], F16)
        gate_bias = sb("gate_bias", [P, 2])
        hidden_bias = sb("hidden_bias", [P, 1])
        rank_se = sb("rank_se", [2, 4], F16)
        msg_bias = sb("msg_bias", [P, C])
        ones2 = sb("ones2", [2, P], F16)

        a_in = sb("a_in", [P, T, N])
        at_in = sb("at_in", [P, T, N])
        x_in = sb("x_in", [P, T, C])
        xT_in = sb("xT_in", [P, N])
        a_hi, a_lo = sb("a_hi", [P, T, N], F16), sb("a_lo", [P, T, N], F16)
        at_hi, at_lo = sb("at_hi", [P, T, N], F16), sb("at_lo", [P, T, N], F16)
        bt_hi, bt_lo = sb("bt_hi", [P, T, N], F16), sb("bt_lo", [P, T, N], F16)
        edge_w_sb = bt_hi[0:REL].rearrange("p t n -> p (t n)").bitcast(F32)[:, 0:NREL * C]\
            .rearrange("p (r c) -> p r c", r=NREL)
        tap_sums = bt_lo[:].rearrange("p t n -> p (t n)").bitcast(F32)
        x_hi, x_lo = sb("x_hi", [P, T, C], F16), sb("x_lo", [P, T, C], F16)
        xT_hi, xT_lo = sb("xT_hi", [P, N], F16), sb("xT_lo", [P, N], F16)
        sums = sb("sums", [P, 2 * T])
        sum_cols = sb("sum_cols", [P, P], F16)
        sum_rows = sb("sum_rows", [P, P], F16)
        sum_rows_b = sb("sum_rows_b", [P, P], F16)
        x_bias = sb("x_bias", [P, T, C])
        ax_hi, ax_lo = sb("ax_hi", [P, N], F16), sb("ax_lo", [P, N], F16)
        atx_hi, atx_lo = sb("atx_hi", [P, N], F16), sb("atx_lo", [P, N], F16)
        y1, y2, y3 = (sb(f"y{k}", [P, T, C]) for k in (1, 2, 3))
        rel_max, gcn2_out, x2_bias = y1, y2, y3
        x1 = sb("x1", [P, T, C])
        x1_hi, x1_lo = sb("x1_hi", [P, T, C], F16), sb("x1_lo", [P, T, C], F16)
        p1_hi, p1_lo = sb("p1_hi", [P, N], F16), sb("p1_lo", [P, N], F16)
        diag_hi, diag_lo = ([b[:].rearrange("p t n -> p (t n)")[:, 0:2 * (N + P)]
                             .rearrange("p (k q) -> p k q", k=2)[:, :, 0:P],
                             b[:].rearrange("p t n -> p (t n)")[:, T * N - 2 * (N + P):]
                             .rearrange("p (k q) -> p k q", k=2)[:, :, N:]] for b in (bt_hi, bt_lo))
        diag_sum = y3
        relu_part = sb("relu_part", [P, T, C])
        g1_hi, g1_lo = sb("g1_hi", [P, T, C], F16), sb("g1_lo", [P, T, C], F16)
        x1_skip = sb("x1_skip", [P, T, C])
        p2_hi, p2_lo = sb("p2_hi", [P, N], F16), sb("p2_lo", [P, N], F16)
        x2 = sb("x2", [P, T, C])
        x2_hi, x2_lo = sb("x2_hi", [P, T, C], F16), sb("x2_lo", [P, T, C], F16)
        agg_hi, agg_lo = sb("agg_hi", [P, N], F16), sb("agg_lo", [P, N], F16)
        hid_hi, hid_lo = sb("hid_hi", [P, 2, N], F16), sb("hid_lo", [P, 2, N], F16)
        x3 = sb("x3", [P, T, C])
        x3_true = sb("x3_true", [P, N])
        rank_all = x3_true[:].bitcast(F16)[:, 0:NREL * C]
        x3T = sb("x3T", [P, N])
        x3T_hi, x3T_lo = sb("x3T_hi", [P, N], F16), sb("x3T_lo", [P, N], F16)
        feat = sb("feat", [P, T, 4])
        feat_rest = sb("feat_rest", [P, T, 4])
        feat_sq = sb("feat_sq", [P, T, 3])
        feat_parts = sb("feat_parts", [P, T, 3, 4], BF16)
        feat_cols = sb("feat_cols", [P, T, P], BF16)
        left_rows = sb("left_rows", [KD, N], BF16)
        right_rows = sb("right_rows", [KD, N], BF16)
        expd = shared[:, 0:2 * N].rearrange("p (t n) -> p t n", t=2)
        kern = shared[:, 2 * N:6 * N].rearrange("p (t n) -> p t n", t=T)
        hid = expd
        at = 6 * N
        h1 = shared[:, at:at + 3 * HALF].rearrange("p (e u) -> p e u", e=3)
        at += 3 * HALF
        conv_sum = shared[:, at:at + N].rearrange("p (e u) -> p e u", e=2)
        xc = shared[:, at + N:at + 2 * N]
        msg = shared[:, at + 2 * N:at + 3 * N].rearrange("p (t c) -> p t c", t=T)
        assert at + 3 * N <= NRAW
        g1 = shared[:, NRAW:NRAW + N].rearrange("p (t c) -> p t c", t=T)
        stats = [sb(f"stats{k}", [P, T, 6]) for k in range(4)]
        mean_var = [sb(f"mean_var{k}", [P, T, 2]) for k in range(4)]
        rstd = [sb(f"rstd{k}", [P, T]) for k in range(4)]
        half_var = [sb(f"half_var{k}", [P, T]) for k in range(4)]
        newton = [sb(f"newton{k}", [P, T]) for k in range(4)]
        newton_t = [sb(f"newton_t{k}", [P, T]) for k in range(4)]
        minus_mean = [sb(f"minus_mean{k}", [P, T]) for k in range(4)]
        shift = [sb(f"shift{k}", [P, T]) for k in range(4)]

        msg_hi, msg_lo = sb("msg_hi", [P, T, C], F16), sb("msg_lo", [P, T, C], F16)
        h1_hi, h1_lo = sb("h1_hi", [P, 3, HPAD], F16), sb("h1_lo", [P, 3, HPAD], F16)
        nmp_hi, nmp_lo = sb("nmp_hi", [P, N], F16), sb("nmp_lo", [P, N], F16)
        xc_hi, xc_lo = sb("xc_hi", [P, N], F16), sb("xc_lo", [P, N], F16)
        gates = sb("gates", [P, 2, N])
        edge_f_sb = gates[0:REL].rearrange("p k n -> p (k n)")[:, 0:NREL * P].rearrange("p (r k) -> p r k", r=NREL)
        hidden_n = sb("hidden_n", [P, N])
        cand = sb("cand", [P, N])
        shift_bc = cand[:, 0:2 * P].rearrange("p (k q) -> p k q", k=2)
        x_minus, x_plus, y4 = (gru_sums[:, k] for k in range(3))
        result = sb("result", [P, T, C])

        pa = ctx.enter_context(nc.psum_tensor("pa", [P, 4, N], F32))
        pb = ctx.enter_context(nc.psum_tensor("pb", [P, 2, N], F32))
        pc = ctx.enter_context(nc.psum_tensor("pc", [P, 2, N], F32))
        dist_bank = [pc[:, 0], pb[:, 0], pc[:, 0], pb[:, 0]]
        hidden_bank, input_bank, reset_bank, update_bank = pc[:, 1], pc[:, 0], pb[:, 0], pb[:, 1]

        def tiles(bank):
            return bank.rearrange("p (t c) -> p t c", t=T)

        names = """vecs_loaded edges_loaded w_front_loaded biases_loaded w_back_loaded
            consts_set vectors_done weights_folded tap_sums_done w_hi_done w_lo_done edge_psum rank_psum ranks_done
            a_loaded at_loaded x_loaded stored
            a_hi_done a_lo_done at_lo_done x_hi_done x_lo_done xT_hi_done xT_lo_done x_bias_done
            sum_cols_done sum_psum sum_rows_done
            ax_psum ax_hi_done ax_lo_done atx_psum atx_hi_done atx_lo_done y1_done
            x1_done x1_hi_done x1_lo_done p1_psum p1_hi_done p1_lo_done
            g1_done g1_hi_done g1_lo_done gcn1_free bt_done diag_sum_done
            diag_hi_done diag_done at_kept p2_psum p2_hi_done p2_lo_done
            gcn2_psum relu2_done gcn2_done y2_done x2_done x2_hi_done x2_lo_done x2_bias_done
            agg_psum agg_hi_done agg_lo_done hid_lo_done gin_psum y3_done x3_done
            x3T_psum x3T_done x3T_hi_done x3T_lo_done feat_psum feat_read feat_cols_done featT_psum
            left_done right_done kern_lo_done
            conv1_psum h1_done h1_sum_done h1_hi_done h1_lo_done msg_psum msg_sum_done msg_done msg_hi_done msg_lo_done
            nmp_psum nmp_hi_done nmp_lo_done conv2_psum conv2_odd_psum conv_sum_done xc_done xc_hi_done xc_lo_done
            hidden_psum reset_psum input_psum update_psum hidden_done reset_done update_done n_pre_done cand_done
            x3_true_done y4_done y4T_psum result_done""".split()
        s = {n: sem(n) for n in names}
        at_hi_done = [sem(f"at_hi_done{k}") for k in range(2)]
        rel_psum = [sem(f"rel_psum{t}") for t in range(T)]
        rel_read = [sem(f"rel_read{t}") for t in range(T)]
        gcn1_psum = [sem(f"gcn1_psum{k}") for k in range(2)]
        relu1_done = [sem(f"relu1_done{k}") for k in range(2)]
        hid_psum = [sem(f"hid_psum{k}") for k in range(2)]
        hid_done = [sem(f"hid_done{k}") for k in range(2)]
        hid_hi_done = sem("hid_hi_done")
        dist_psum = [sem(f"dist_psum{t}") for t in range(T)]
        exp_done = [sem(f"exp_done{t}") for t in range(T)]
        kern_done = [sem(f"kern_done{t}") for t in range(T)]
        kern_hi_done = [sem(f"kern_hi_done{t}") for t in range(T)]
        seed_done = [sem(f"seed_done{k}") for k in range(4)]
        norm_done = [sem(f"norm_done{k}") for k in range(4)]
        dve_step = sem("dve_step")
        pool_step = sem("pool_step")

        def W(name, lo=0, width=None):
            a, b = WCOLS[name]
            b = b if width is None else a + lo + width
            return w_hi[:, a + lo:b], w_lo[:, a + lo:b]

        class Counts:

            def __init__(self, eng, i):
                if isinstance(i, int):
                    at = {k: i + k for k in range(-3, 3)}
                    self.has_in, self.has_a, self.has_b, self.has_c, self.has_d = (
                        0 <= g < B for g in (i + 1, i, i - 1, i - 2, i - 3))
                    self.again_in, self.again_a, self.again_b, self.again_c, self.again_d = (
                        g > 0 for g in (i + 1, i, i - 1, i - 2, i - 3))
                else:
                    at = {k: eng.snap(i + k) for k in range(-3, 3)}
                    for value in at.values():
                        eng.to_reg(value)
                    self.has_in = self.has_a = self.has_b = self.has_c = self.has_d = True
                    self.again_in = self.again_a = self.again_b = self.again_c = self.again_d = True
                self.filling = isinstance(i, int) and i in (0, 1)
                self.early = isinstance(i, int) and i == 0
                self.made_early = isinstance(i, int) and i == 1
                self.n_in, self.n_a, self.n_b, self.n_c, self.n_d = (at[k] for k in (2, 1, 0, -1, -2))
                self.prev_in, self.prev_a, self.prev_b, self.prev_c, self.prev_d = (at[k] for k in (1, 0, -1, -2, -3))

        def run(iteration, eng, prologue=None):
            if prologue is not None:
                prologue()
            for i in range(4):
                iteration(i)
            with eng.Fori(4, B - 1) as i:
                iteration(i)
            for i in range(B - 1, B + 3):
                iteration(i)

        block = ctx.enter_context(nc.Block())

        @block.sync
        def _(sp):
            for dst, src in ((vec[:], vecs), (bn_eps_sb[:], bn_eps), (mask_sb[:], masks), (ident_f[:], ident)):
                sp.dma_start(dst, src).then_inc(s["vecs_loaded"], 16)
            sp.dma_start(edge_w_sb, edge_w).then_inc(s["edges_loaded"], 16)
            sp.dma_start(edge_f_sb, edge_f).then_inc(s["edges_loaded"], 16)

            def prologue():
                sp.dma_start(at_in[:], adjT[0].rearrange("(t p) m -> p t m", p=P)).then_inc(s["at_loaded"], 16)
                sp.dma_start(x_in[:], x[0].rearrange("(t p) c -> p t c", p=P)).then_inc(s["x_loaded"], 16)
                sp.dma_start(xT_in[:], xT[0]).then_inc(s["x_loaded"], 16)
                sp.dma_start(a_in[:], adj[0].rearrange("(t p) m -> p t m", p=P)).then_inc(s["a_loaded"], 16)
                sp.dma_start(w_raw[:, 0:NFRONT], weights[:, 0:NFRONT]).then_inc(s["w_front_loaded"], 16)
                sp.dma_start(bias_sb, bias_rows).then_inc(s["biases_loaded"], 16)
                sp.dma_start(rel_b_sb[:], rel_b).then_inc(s["biases_loaded"], 16)
                sp.dma_start(gin_b2_sb[:], gin_b2).then_inc(s["biases_loaded"], 16)
                sp.dma_start(w_raw[:, NFRONT:], weights[:, NFRONT:]).then_inc(s["w_back_loaded"], 16)

            def iteration(i):
                c = Counts(sp, i)
                if c.has_in:
                    g = i + 1
                    sp.wait_ge(s["a_lo_done"], c.prev_in)
                    sp.dma_start(a_in[:], adj[g].rearrange("(t p) m -> p t m", p=P)).then_inc(s["a_loaded"], 16)
                    sp.wait_ge(s["x_lo_done"], c.prev_in)
                    sp.wait_ge(s["xT_lo_done"], c.prev_in)
                    sp.wait_ge(s["x_bias_done"], c.prev_in)
                    sp.dma_start(x_in[:], x[g].rearrange("(t p) c -> p t c", p=P)).then_inc(s["x_loaded"], 16)
                    sp.dma_start(xT_in[:], xT[g]).then_inc(s["x_loaded"], 16)
                    sp.wait_ge(s["at_lo_done"], c.prev_in)
                    sp.dma_start(at_in[:], adjT[g].rearrange("(t p) m -> p t m", p=P)).then_inc(s["at_loaded"], 16)
                if c.has_b:
                    if c.again_b:
                        sp.wait_ge(kern_done[T - 1], c.prev_b)
                    else:
                        sp.wait_ge(s["ranks_done"], 3)
                    sp.dma_start(at_keep[:], adjT[i - 1].rearrange("(t p) m -> p t m", p=P))\
                        .then_inc(s["at_kept"], 16)
                if c.has_d:
                    sp.wait_ge(s["result_done"], c.n_d)
                    sp.dma_start(out[i - 3].rearrange("(t p) c -> p t c", p=P), result[:]).then_inc(s["stored"], 16)

            run(iteration, sp, prologue)
            sp.wait_ge(s["stored"], 16 * B)


        @block.gpsimd
        def _(pool):
            nc.gpsimd.memset(feat_cols[:], 0.0).then_inc(s["consts_set"], 1)
            nc.gpsimd.memset(ones2[:], SX).then_inc(s["consts_set"], 1)
            nc.gpsimd.memset(h1_hi[:], 0.0).then_inc(s["consts_set"], 1)
            nc.gpsimd.memset(h1_lo[:], 0.0).then_inc(s["consts_set"], 1)
            nc.gpsimd.memset(sum_cols[:], SX).then_inc(s["consts_set"], 1)
            nc.gpsimd.memset(rank_rel[:], 0.0).then_inc(s["consts_set"], 1)
            nc.gpsimd.memset(rank_gcn[:], 0.0).then_inc(s["consts_set"], 1)
            pool.wait_ge(s["consts_set"], 7)
            left_ones = feat_cols[:, :, 0:KD].rearrange("p t (a b d) -> p t a b d", a=3, b=3)
            nc.gpsimd.memset(left_ones[:, :, 0, :, 3], 1.0).then_inc(s["consts_set"], 1)
            pool.wait_ge(s["vecs_loaded"], 4 * 16)
            nc.gpsimd.tensor_copy(ident_h[:], ident_f[:]).then_inc(s["consts_set"], 1)
            nc.gpsimd.tensor_copy(ident_b[:], ident_f[:]).then_inc(s["consts_set"], 1)
            pool.wait_ge(s["biases_loaded"], 3 * 16)
            steps = [0]

            def step(ins):
                steps[0] += 1
                return ins.then_inc(pool_step, 1)

            def lo_part(dst, src, hi):
                return nc.gpsimd.tensor_tensor(dst, src, hi, ALU.subtract)

            def newton_steps(k, gain):
                y_, a_, t_ = rstd[k][:], newton[k][:], newton_t[k][:]
                step(nc.gpsimd.tensor_tensor(a_, y_, y_, ALU.mult))
                pool.wait_ge(pool_step, steps[0])
                step(nc.gpsimd.tensor_tensor(a_, a_, half_var[k][:], ALU.mult))
                pool.wait_ge(pool_step, steps[0])
                step(nc.gpsimd.tensor_scalar(a_, a_, -1.0, 1.5, ALU.mult, ALU.add))
                pool.wait_ge(pool_step, steps[0])
                step(nc.gpsimd.tensor_tensor(y_, y_, a_, ALU.mult))
                pool.wait_ge(pool_step, steps[0])
                step(nc.gpsimd.tensor_tensor(a_, y_, y_, ALU.mult))
                pool.wait_ge(pool_step, steps[0])
                step(nc.gpsimd.tensor_tensor(a_, a_, half_var[k][:], ALU.mult))
                pool.wait_ge(pool_step, steps[0])
                step(nc.gpsimd.tensor_scalar(t_, a_, 1.5, -2.5, ALU.mult, ALU.add))
                pool.wait_ge(pool_step, steps[0])
                step(nc.gpsimd.tensor_tensor(t_, t_, a_, ALU.mult))
                pool.wait_ge(pool_step, steps[0])
                step(nc.gpsimd.tensor_scalar(t_, t_, 1.875, gain, ALU.add, ALU.mult))
                pool.wait_ge(pool_step, steps[0])
                step(nc.gpsimd.tensor_tensor(y_, y_, t_, ALU.mult))
                pool.wait_ge(pool_step, steps[0])
                return nc.gpsimd.tensor_tensor(shift[k][:], minus_mean[k][:], y_, ALU.mult)

            def iteration(i):
                c = Counts(pool, i)
                if c.has_b:
                    if c.again_b:
                        pool.wait_ge(s["x3_done"], c.prev_b)
                    pool.wait_ge(s["bt_done"], c.n_b)
                    for k in range(2):
                        step(nc.gpsimd.tensor_tensor(diag_sum[:, 2 * k:2 * k + 2], diag_hi[k], diag_lo[k], ALU.add))
                    pool.wait_ge(pool_step, steps[0])
                    nc.gpsimd.tensor_tensor(diag_sum[:], diag_sum[:], diagonal[:].unsqueeze(1).to_broadcast([P, T, P]),
                                            ALU.add).then_inc(s["diag_sum_done"], 1)
                if c.has_c:
                    pool.wait_ge(s["h1_done"], c.n_c)
                    nc.gpsimd.tensor_tensor(h1[:, 2], h1[:, 0], h1[:, 1], ALU.add).then_inc(s["h1_sum_done"], 1)
                    pool.wait_ge(s["h1_hi_done"], c.n_c)
                    lo_part(h1_lo[:, :, PAD // 2:PAD // 2 + HALF], h1, h1_hi[:, :, PAD // 2:PAD // 2 + HALF])\
                        .then_inc(s["h1_lo_done"], 1)
                if c.has_b:
                    pool.wait_ge(s["gcn2_done"], c.n_b)
                    nc.gpsimd.tensor_tensor(y2[:], gcn2_out[:], x1_skip[:], ALU.add).then_inc(s["y2_done"], 1)
                    pool.wait_ge(s["diag_hi_done"], c.n_b)
                    for k in range(2):
                        ins = lo_part(diag_lo[k], diag_sum[:, 2 * k:2 * k + 2], diag_hi[k])
                    ins.then_inc(s["diag_done"], 1)
                if c.has_c:
                    pool.wait_ge(kern_hi_done[0], c.n_c)
                    lo_part(kern_lo[:, 0], kern[:, 0], kern_hi[:, 0])
                if c.has_b:
                    pool.wait_ge(seed_done[1], c.n_b)
                    newton_steps(1, SX).then_inc(norm_done[1], 1)
                if c.has_c:
                    pool.wait_ge(kern_hi_done[1], c.n_c)
                    lo_part(kern_lo[:, 1], kern[:, 1], kern_hi[:, 1])
                if c.has_a:
                    pool.wait_ge(seed_done[0], c.n_a)
                    newton_steps(0, SX).then_inc(norm_done[0], 1)
                if c.has_c:
                    for t in range(2, T):
                        pool.wait_ge(kern_hi_done[t], c.n_c)
                        ins = lo_part(kern_lo[:, t], kern[:, t], kern_hi[:, t])
                    ins.then_inc(s["kern_lo_done"], 1)
                    pool.wait_ge(s["msg_hi_done"], c.n_c)
                    lo_part(msg_lo[:], msg, msg_hi[:]).then_inc(s["msg_lo_done"], 1)
                if c.has_b:
                    pool.wait_ge(s["x2_done"], c.n_b)
                    nc.gpsimd.tensor_tensor(x2_bias[:], x2[:], gin_b2_sb[:].unsqueeze(1).to_broadcast([P, T, C]),
                                            ALU.add).then_inc(s["x2_bias_done"], 1)
                if c.has_in:
                    pool.wait_ge(s["y1_done"], c.prev_in)
                    pool.wait_ge(s["x_hi_done"], c.n_in)
                    nc.gpsimd.tensor_tensor(x_bias[:], x_in[:], rel_b_sb[:], ALU.add).then_inc(s["x_bias_done"], 1)
                if c.has_c:
                    pool.wait_ge(s["xc_hi_done"], c.n_c)
                    lo_part(xc_lo[:], xc, xc_hi[:]).then_inc(s["xc_lo_done"], 1)
                if c.has_d:
                    pool.wait_ge(seed_done[3], c.n_d)
                    newton_steps(3, 1.0).then_inc(norm_done[3], 1)
                if c.has_a:
                    pool.wait_ge(s["g1_hi_done"], c.n_a)
                    lo_part(g1_lo[:], g1, g1_hi[:]).then_inc(s["g1_lo_done"], 1)
                if c.has_b:
                    pool.wait_ge(seed_done[2], c.n_b)
                    newton_steps(2, SX).then_inc(norm_done[2], 1)
                if steps[0]:
                    pool.wait_ge(pool_step, steps[0])
                    pool.sem_clear(pool_step)
                    steps[0] = 0

            def prologue():
                pool.wait_ge(s["x_hi_done"], 1)
                nc.gpsimd.tensor_tensor(x_bias[:], x_in[:], rel_b_sb[:], ALU.add).then_inc(s["x_bias_done"], 1)
                a, b = WCOLS["conv2"]
                taps = w_raw[:, a + C:b].rearrange("p (j e c) -> p j e c", e=2, c=C)
                pool.wait_ge(s["w_back_loaded"], 16)
                pool.wait_ge(s["edge_psum"], NREL)
                nc.gpsimd.tensor_tensor(tap_sums.rearrange("p (j c) -> p j c", c=C), taps[:, :, 1], taps[:, :, 0],
                                        ALU.add).then_inc(s["tap_sums_done"], 1)

            run(iteration, pool, prologue)

        @block.scalar
        def _(act):
            def weights_hi_rest():
                act.wait_ge(s["w_back_loaded"], 16)
                nc.scalar.activation(w_hi[:, NFRONT:NRAW], w_raw[:, NFRONT:], ACT.Copy, scale=SW)
                act.wait_ge(s["tap_sums_done"], 1)
                nc.scalar.activation(w_hi[:, NRAW:], tap_sums, ACT.Copy, scale=SW).then_inc(s["w_hi_done"], 1)

            def hi_from(dst, src, scale=DOWN):
                return nc.scalar.activation(dst, src, ACT.Copy, scale=scale)

            def adjacency(src, hi, way, node_tiles):
                for t in node_tiles:
                    ins = nc.scalar.activation(hi[:, t], src[:, t], ACT.Copy, scale=SW,
                                               accum_out=sums[:, 2 * t + way:2 * t + way + 1])
                return ins

            def normalize(k, src, dst):
                for t in range(T):
                    ins = nc.scalar.activation(dst[:, t], src[:, t], ACT.Identity, scale=rstd[k][:, t:t + 1],
                                               bias=shift[k][:, t:t + 1])
                return ins

            def distance_exp(t, c):
                act.wait_ge(dist_psum[t], c.n_c)
                if t >= 2:
                    act.wait_ge(kern_done[t - 2], c.n_c)
                nc.scalar.activation(expd[:, t % 2], dist_bank[t], ACT.Exp, bias=feat[:, t, 3:4])\
                    .then_inc(exp_done[t], 1)

            def kernel_hi(t, c):
                act.wait_ge(kern_done[t], c.n_c)
                hi_from(kern_hi[:, t], kern[:, t], 1.0).then_inc(kern_hi_done[t], 1)

            def iteration(i):
                c = Counts(act, i)
                loaded = 16 * c.n_in if isinstance(i, int) else act.snap(i * 16 + 32)
                loaded_x = 32 * c.n_in if isinstance(i, int) else act.snap(i * 32 + 64)

                if c.has_a:
                    act.wait_ge(s["ax_psum"], c.n_a)
                    hi_from(ax_hi[:], pa[:, 0]).then_inc(s["ax_hi_done"], 1)
                if c.has_c:
                    act.wait_ge(s["x3T_psum"], c.n_c)
                    hi_from(x3T_hi[:], pb[:, 0], 1.0).then_inc(s["x3T_hi_done"], 1)
                    act.wait_ge(s["x3T_lo_done"], c.n_c)
                    hi_from(x3T[:], pb[:, 0], 1.0).then_inc(s["x3T_done"], 1)
                if c.has_a:
                    if not c.made_early:
                        act.wait_ge(s["atx_psum"], c.n_a)
                        hi_from(atx_hi[:], pa[:, 1]).then_inc(s["atx_hi_done"], 1)
                    act.wait_ge(s["sum_psum"], c.n_a)
                    hi_from(sum_rows[:], pa[:, 2].bitcast(F16)[:, 0:P], 1.0).then_inc(s["sum_rows_done"], 1)
                if c.has_c:
                    act.wait_ge(s["conv1_psum"], c.n_c)
                    nc.scalar.activation(h1[:, 0:2].rearrange("p e u -> p u e"),
                                         pc[:, 0].rearrange("p (u e) -> p u e", e=2), ACT.Relu,
                                         scale=conv1_scale[:], bias=conv1_shift[:]).then_inc(s["h1_done"], 1)
                if c.has_in:
                    act.wait_ge(s["sum_psum"], c.prev_in)
                    act.wait_ge(s["a_loaded"], loaded)
                    adjacency(a_in, a_hi, 0, range(0, 2))
                if c.has_b:
                    act.wait_ge(s["p2_psum"], c.n_b)
                    hi_from(p2_hi[:], pb[:, 0]).then_inc(s["p2_hi_done"], 1)
                    act.wait_ge(s["diag_sum_done"], c.n_b)
                    for k in range(2):
                        ins = hi_from(diag_hi[k], diag_sum[:, 2 * k:2 * k + 2], 1.0)
                    ins.then_inc(s["diag_hi_done"], 1)
                if c.has_c:
                    act.wait_ge(s["h1_sum_done"], c.n_c)
                    hi_from(h1_hi[:, :, PAD // 2:PAD // 2 + HALF], h1, 1.0).then_inc(s["h1_hi_done"], 1)
                if c.has_in:
                    adjacency(a_in, a_hi, 0, range(2, T)).then_inc(s["a_hi_done"], 1)
                if c.has_c:
                    act.wait_ge(s["featT_psum"], c.n_c)
                    hi_from(left_rows[:], pc[:, 0].bitcast(BF16)[0:KD, 0:N], 1.0).then_inc(s["left_done"], 1)
                if c.has_b:
                    act.wait_ge(s["gcn2_psum"], c.n_b)
                    nc.scalar.activation(relu_part[:], tiles(pb[:, 1]), ACT.Relu, scale=(1.0 - LRELU) * DOWN)\
                        .then_inc(s["relu2_done"], 1)
                if c.has_in:
                    act.wait_ge(s["x_loaded"], loaded_x)
                    hi_from(x_hi[:], x_in[:], SX).then_inc(s["x_hi_done"], 1)
                if c.has_c:
                    distance_exp(0, c)
                    distance_exp(1, c)
                    kernel_hi(0, c)
                if c.has_a and not c.again_a:
                    weights_hi_rest()
                if c.has_in:
                    act.wait_ge(rel_psum[T - 1], c.prev_in)
                    hi_from(xT_hi[:], xT_in[:], SX).then_inc(s["xT_hi_done"], 1)
                if c.has_c:
                    distance_exp(2, c)
                    kernel_hi(1, c)
                    distance_exp(3, c)
                if c.has_b:
                    act.wait_ge(norm_done[1], c.n_b)
                    normalize(1, y2, x2).then_inc(s["x2_done"], 1)
                    act.wait_ge(s["x2_done"], c.n_b)
                    hi_from(x2_hi[:], x2[:], 1.0).then_inc(s["x2_hi_done"], 1)
                if c.has_c:
                    kernel_hi(2, c)
                    act.wait_ge(s["msg_sum_done"], c.n_c)
                    nc.scalar.activation(msg, msg, ACT.Relu).then_inc(s["msg_done"], 1)
                    act.wait_ge(s["msg_done"], c.n_c)
                    hi_from(msg_hi[:], msg, 1.0).then_inc(s["msg_hi_done"], 1)
                if c.has_a:
                    act.wait_ge(norm_done[0], c.n_a)
                    normalize(0, y1, x1).then_inc(s["x1_done"], 1)
                    act.wait_ge(s["x1_done"], c.n_a)
                    hi_from(x1_hi[:], x1[:], 1.0).then_inc(s["x1_hi_done"], 1)
                if c.early:
                    act.wait_ge(s["atx_psum"], c.n_in)
                    hi_from(atx_hi[:], pa[:, 1]).then_inc(s["atx_hi_done"], 1)
                if c.has_c:
                    kernel_hi(3, c)
                    if c.again_c:
                        act.wait_ge(s["y4_done"], c.prev_c)
                    hi_from(x3_true[:], x3T[:], 1.0 / SX).then_inc(s["x3_true_done"], 1)
                if c.has_c:
                    act.wait_ge(s["conv_sum_done"], c.n_c)
                    nc.scalar.activation(xc.rearrange("p (u e) -> p e u", e=2), conv_sum, ACT.Relu,
                                         bias=conv2_shift[:]).then_inc(s["xc_done"], 1)
                    act.wait_ge(s["xc_done"], c.n_c)
                    hi_from(xc_hi[:], xc, 1.0).then_inc(s["xc_hi_done"], 1)
                if c.has_b:
                    act.wait_ge(s["agg_psum"], c.n_b)
                    hi_from(agg_hi[:], pb[:, 0]).then_inc(s["agg_hi_done"], 1)
                if c.has_a:
                    act.wait_ge(s["p1_psum"], c.n_a)
                    hi_from(p1_hi[:], pa[:, 2]).then_inc(s["p1_hi_done"], 1)
                if c.has_in:
                    act.wait_ge(s["bt_done"], c.prev_in)
                    act.wait_ge(s["at_loaded"], loaded)
                    adjacency(at_in, at_hi, 1, range(0, 2)).then_inc(at_hi_done[0], 1)
                if c.has_b:
                    for k in range(2):
                        act.wait_ge(hid_psum[k], c.n_b)
                        nc.scalar.activation(hid[:, k], pb[:, 1 - k], ACT.Relu, scale=DOWN, bias=gin_b1[:, k:k + 1])\
                            .then_inc(hid_done[k], 1)
                    for k in range(2):
                        act.wait_ge(hid_done[k], c.n_b)
                        ins = hi_from(hid_hi[:, k], hid[:, k], 1.0)
                    ins.then_inc(hid_hi_done, 1)
                if c.has_c:
                    act.wait_ge(s["nmp_psum"], c.n_c)
                    hi_from(nmp_hi[:], pc[:, 0], 1.0 / SE).then_inc(s["nmp_hi_done"], 1)
                if c.has_in and not c.has_b:
                    adjacency(at_in, at_hi, 1, range(2, T)).then_inc(at_hi_done[1], 1)
                if c.has_a:
                    for k in range(2):
                        bank = pa[:, k].rearrange("p (t h c) -> p t h c", t=2, h=2)
                        act.wait_ge(gcn1_psum[k], c.n_a)
                        nc.scalar.activation(relu_part[:, 2 * k:2 * k + 2], bank[:, :, 0], ACT.Relu,
                                             scale=(1.0 - LRELU) * DOWN).then_inc(relu1_done[k], 1)
                if c.has_in and c.has_b:
                    adjacency(at_in, at_hi, 1, range(2, T)).then_inc(at_hi_done[1], 1)
                if c.has_a:
                    act.wait_ge(s["g1_done"], c.n_a)
                    hi_from(g1_hi[:], g1, 1.0).then_inc(s["g1_hi_done"], 1)
                if c.has_c:
                    act.wait_ge(s["hidden_psum"], c.n_c)
                    nc.scalar.activation(hidden_n[:], hidden_bank, ACT.Identity, bias=hidden_bias[:])\
                        .then_inc(s["hidden_done"], 1)
                    act.wait_ge(s["reset_psum"], c.n_c)
                    nc.scalar.activation(gates[:, 0], reset_bank, ACT.Tanh, scale=0.5 / (SX * SW),
                                         bias=gate_bias[:, 0:1]).then_inc(s["reset_done"], 1)
                if c.has_d:
                    if c.again_d:
                        act.wait_ge(s["stored"], c.prev_d * 16)
                    act.wait_ge(norm_done[3], c.n_d)
                    normalize(3, tiles(pa[:, 3]), result).then_inc(s["result_done"], 1)
                if c.has_c:
                    act.wait_ge(s["n_pre_done"], c.n_c)
                    nc.scalar.activation(cand[:], hidden_n[:], ACT.Tanh, scale=1.0 / (SX * SW),
                                         bias=vec[:, VEC_IH + 2:VEC_IH + 3]).then_inc(s["cand_done"], 1)
                if c.has_b:
                    act.wait_ge(norm_done[2], c.n_b)
                    normalize(2, y3, x3).then_inc(s["x3_done"], 1)
                if c.has_c:
                    act.wait_ge(s["update_psum"], c.n_c)
                    nc.scalar.activation(gates[:, 1], update_bank, ACT.Tanh, scale=0.5 / (SX * SW),
                                         bias=gate_bias[:, 1:2]).then_inc(s["update_done"], 1)
            def prologue():
                act.wait_ge(s["at_loaded"], 16)
                for k in range(2):
                    adjacency(at_in, at_hi, 1, range(2 * k, 2 * k + 2)).then_inc(at_hi_done[k], 1)
                act.wait_ge(s["x_loaded"], 2 * 16)
                hi_from(x_hi[:], x_in[:], SX).then_inc(s["x_hi_done"], 1)
                hi_from(xT_hi[:], xT_in[:], SX).then_inc(s["xT_hi_done"], 1)
                act.wait_ge(s["a_loaded"], 16)
                adjacency(a_in, a_hi, 0, range(T)).then_inc(s["a_hi_done"], 1)
                act.wait_ge(s["weights_folded"], 1)
                nc.scalar.activation(w_hi[:, 0:NFRONT], w_raw[:, 0:NFRONT], ACT.Copy, scale=SW)\
                    .then_inc(s["w_hi_done"], 1)

            run(iteration, act, prologue)

        @block.vector
        def _(dve):
            v = nc.vector
            steps = [0]

            def step(ins):
                steps[0] += 1
                ins.then_inc(dve_step, 1)
                return steps[0]

            def rsqrt(dst, src, tmp, gain):
                step(v.tensor_scalar(dst.bitcast(I32), src.bitcast(I32), -0.5, RSQRT_SEED, ALU.mult, ALU.add))
                for k in range(3):
                    dve.wait_ge(dve_step, steps[0])
                    step(v.scalar_tensor_tensor(out=tmp, in0=dst, scalar=-0.5, in1=dst, op0=ALU.mult, op1=ALU.mult))
                    dve.wait_ge(dve_step, steps[0])
                    step(v.tensor_tensor(tmp, tmp, src, ALU.mult))
                    dve.wait_ge(dve_step, steps[0])
                    step(v.scalar_tensor_tensor(out=dst, in0=tmp, scalar=1.5, in1=dst, op0=ALU.add, op1=ALU.mult))
                if gain != 1.0:
                    dve.wait_ge(dve_step, steps[0])
                    step(v.tensor_scalar(dst, dst, gain, None, ALU.mult))

            dve.wait_ge(s["vecs_loaded"], 4 * 16)
            step(v.tensor_tensor(bn_tmp[:], vec[:, VEC_VAR:VEC_VAR + 4], bn_eps_sb[:], ALU.add))
            dve.wait_ge(dve_step, steps[0])
            step(v.tensor_copy(bn_shift[:], bn_tmp[:]))
            dve.wait_ge(dve_step, steps[0])
            rsqrt(bn_scale[:], bn_shift[:], bn_tmp[:], 1.0)
            dve.wait_ge(dve_step, steps[0])
            step(v.tensor_tensor(bn_scale[:], bn_scale[:], vec[:, VEC_GAMMA:VEC_GAMMA + 4], ALU.mult))
            dve.wait_ge(dve_step, steps[0])
            step(v.tensor_tensor(bn_tmp[:], bn_scale[:], vec[:, VEC_MEAN:VEC_MEAN + 4], ALU.mult))
            dve.wait_ge(dve_step, steps[0])
            step(v.tensor_tensor(bn_shift[:], vec[:, VEC_BETA:VEC_BETA + 4], bn_tmp[:], ALU.subtract))
            dve.wait_ge(dve_step, steps[0])
            for k in range(2):
                step(v.tensor_copy(shift_bc[:, k], bn_shift[:, k:k + 1].to_broadcast([P, P])))
            dve.wait_ge(dve_step, steps[0])
            step(v.tensor_scalar(conv1_scale[:], bn_scale[:, 2:3], DOWN, None, ALU.mult))
            step(v.tensor_scalar(conv2_scale[:], bn_scale[:, 3:4], DOWN, None, ALU.mult))
            step(v.tensor_scalar(conv2_minus[:], bn_scale[:, 3:4], -DOWN, None, ALU.mult))
            step(v.tensor_scalar(conv1_shift[:], bn_shift[:, 2:3], SX, None, ALU.mult))
            step(v.tensor_scalar(conv2_shift[:], bn_shift[:, 3:4], SX, None, ALU.mult))
            step(v.tensor_tensor(gate_bias[:], vec[:, VEC_IH:VEC_IH + 2], vec[:, VEC_HH:VEC_HH + 2], ALU.add))
            dve.wait_ge(dve_step, steps[0])
            step(v.tensor_scalar(gate_bias[:], gate_bias[:], 0.5, None, ALU.mult))
            step(v.tensor_scalar(hidden_bias[:], vec[:, VEC_HH + 2:VEC_HH + 3], SX * SW, None, ALU.mult))
            step(v.tensor_scalar(gin_b1[:], vec[:, VEC_B1:VEC_B1 + 2], SX, None, ALU.mult))
            v.tensor_copy(bn_tmp[:, 0:1], bn_shift[:, 0:1]).then_inc(s["vectors_done"], 1)
            dve.wait_ge(s["consts_set"], 8)

            def place(dst, cols, less, rows=P):
                step(v.scalar_tensor_tensor(out=dst, in0=rows_hi[0:rows, cols], scalar=mask_sb[0:rows, less:less + 1],
                                            in1=rows_f[0:rows, cols], op0=ALU.mult, op1=ALU.add))

            def round_rows(width):
                dve.wait_ge(dve_step, steps[0])
                step(v.tensor_copy(rows_hi[:, 0:width], rows_f[:, 0:width]))
                dve.wait_ge(dve_step, steps[0])

            def mask(k):
                return mask_sb[:, k:k + 1]

            def to_own_partitions(dst, width):
                dve.wait_ge(dve_step, steps[0])
                for t in range(T):
                    own = slice(QUAD * t, QUAD * (t + 1))
                    step(v.tensor_copy(dst[own, t], rank_all[own, 0:width]))
                dve.wait_ge(dve_step, steps[0])

            def relation_rows():
                dve.wait_ge(s["edge_psum"], NREL)
                step(v.tensor_scalar(rows_f[:, 0:2 * C], pc[:, 0, 0:2 * C], mask(MASK_ROW), None, ALU.mult))
                step(v.tensor_scalar(rows_f[:, 2 * C:4 * C], pc[:, 0, 2 * C:4 * C], mask(MASK_COL), None, ALU.mult))
                step(v.tensor_scalar(rows_f[:, 4 * C:NREL * C], pc[:, 1, 0:3 * C], mask(MASK_ONE), None, ALU.mult))
                round_rows(NREL * C)

            def prepare_weights():
                dve.wait_ge(s["rank_psum"], 1)
                a, b = WCOLS["gcn1"]
                step(v.tensor_scalar(w_raw[:, a:b], w_raw[:, a:b], bn_scale[:, 0:1], None, ALU.mult))
                a, b = WCOLS["gcn2"]
                v.tensor_scalar(w_raw[:, a:b], w_raw[:, a:b], bn_scale[:, 1:2], None, ALU.mult)\
                    .then_inc(s["weights_folded"], 1)
                place(rank_all[:, 0:2 * C], slice(0, 2 * C), LESS_ROW)
                place(rank_all[:, 2 * C:4 * C], slice(2 * C, 4 * C), LESS_COL)
                place(rank_all[:, 4 * C:], slice(4 * C, NREL * C), LESS_ONE)
                to_own_partitions(rank_rel, NREL * C)
                dve.wait_ge(s["w_hi_done"], 1)
                step(v.scalar_tensor_tensor(out=w_lo[:, 0:NFRONT], in0=w_raw[:, 0:NFRONT], scalar=SW,
                                            in1=w_hi[:, 0:NFRONT], op0=ALU.mult, op1=ALU.subtract))
                dve.wait_ge(dve_step, steps[0])
                v.tensor_copy(bn_tmp[:, 1:2], bn_shift[:, 0:1]).then_inc(s["ranks_done"], 1)

            def gcn_rows():
                dve.wait_ge(s["biases_loaded"], 3 * 16)
                step(v.tensor_scalar(gin_b2_sb[:], gin_b2_sb[:], SX, None, ALU.mult))
                step(v.tensor_scalar(rows_b[:], bias_sb[:, 0:3 * C], mask(MASK_ONE), None, ALU.mult))
                dve.wait_ge(dve_step, steps[0])
                step(v.scalar_tensor_tensor(out=rows_f[:, 0:3 * C], in0=pb[:, 0, 0:3 * C], scalar=mask(MASK_ROW),
                                            in1=rows_b[:], op0=ALU.mult, op1=ALU.add))
                round_rows(3 * C)
                place(rank_all[:, 0:3 * C], slice(0, 3 * C), LESS_BOTH)
                to_own_partitions(rank_gcn, 3 * C)
                step(v.tensor_scalar(bn_tmp[:, 3:4], vec[:, VEC_EPS:VEC_EPS + 1], SW, SW, ALU.mult, ALU.add))
                dve.wait_ge(dve_step, steps[0])
                step(v.tensor_scalar(diagonal[:], ident_f[:], bn_tmp[:, 3:4], None, ALU.mult))
                dve.wait_ge(dve_step, steps[0])
                v.tensor_copy(bn_tmp[:, 0:1], bn_shift[:, 0:1]).then_inc(s["ranks_done"], 1)

            def layer3_biases():
                step(v.tensor_scalar(msg_bias[:], bias_sb[:, slice(*BCOLS["msg"])], SX, None, ALU.mult))
                step(v.tensor_scalar(rows_f[:, 0:4], bias_sb[:, slice(*BCOLS["se"])], SW, None, ALU.mult))
                round_rows(4)
                place(rank_se[:], slice(0, 4), LESS_SECOND, 2)
                dve.wait_ge(dve_step, steps[0])
                v.tensor_copy(bn_tmp[:, 2:3], bn_shift[:, 0:1]).then_inc(s["ranks_done"], 1)

            def tap_sums_lo():
                dve.wait_ge(s["w_hi_done"], 2)
                step(v.scalar_tensor_tensor(out=w_lo[:, NRAW:], in0=tap_sums, scalar=SW, in1=w_hi[:, NRAW:],
                                            op0=ALU.mult, op1=ALU.subtract))
                dve.wait_ge(dve_step, steps[0])

            def weights_lo():
                dve.wait_ge(s["w_hi_done"], 2)
                step(v.scalar_tensor_tensor(out=w_lo[:, NFRONT:NRAW], in0=w_raw[:, NFRONT:], scalar=SW,
                                            in1=w_hi[:, NFRONT:NRAW], op0=ALU.mult, op1=ALU.subtract))
                dve.wait_ge(dve_step, steps[0])
                dve.wait_ge(s["consts_set"], 10)
                v.tensor_copy(bn_tmp[:, 0:1], bn_shift[:, 0:1]).then_inc(s["w_lo_done"], 1)

            def lo_from(dst, src, hi, scale=DOWN):
                return v.scalar_tensor_tensor(out=dst, in0=src, scalar=scale, in1=hi, op0=ALU.mult,
                                              op1=ALU.subtract)

            def norm_stats(k, src, src_scale):
                for t in range(T):
                    step(v.bn_stats(stats[k][:, t], src[:, t]))
                dve.wait_ge(dve_step, steps[0])
                for t in range(T):
                    step(v.bn_aggr(mean_var[k][:, t], stats[k][:, t]))
                dve.wait_ge(dve_step, steps[0])
                halved = step(v.tensor_scalar(half_var[k][:], mean_var[k][:, :, 1], LN_EPS * src_scale * src_scale,
                                              0.5, ALU.add, ALU.mult))
                step(v.tensor_scalar(minus_mean[k][:], mean_var[k][:, :, 0], -1.0, None, ALU.mult))
                dve.wait_ge(dve_step, halved)
                return v.tensor_scalar(rstd[k][:].bitcast(I32), half_var[k][:].bitcast(I32), -0.5, HALF_SEED,
                                       ALU.mult, ALU.add)

            def x_lo_part(n):
                dve.wait_ge(s["x_hi_done"], n)
                lo_from(x_lo[:], x_in[:], x_hi[:], SX).then_inc(s["x_lo_done"], 1)

            def xT_lo_part(n):
                dve.wait_ge(s["xT_hi_done"], n)
                lo_from(xT_lo[:], xT_in[:], xT_hi[:], SX).then_inc(s["xT_lo_done"], 1)

            def adjacency_lo(n):
                dve.wait_ge(s["a_hi_done"], n)
                lo_from(a_lo[:], a_in[:], a_hi[:], SW).then_inc(s["a_lo_done"], 1)

            def adjacencyT_lo(k, n):
                half = slice(2 * k, 2 * k + 2)
                dve.wait_ge(at_hi_done[k], n)
                ins = lo_from(at_lo[:, half], at_in[:, half], at_hi[:, half], SW)
                if k == 0:
                    step(ins)
                else:
                    ins.then_inc(s["at_lo_done"], 1)

            sum_parts = sum_cols[:].rearrange("p (g q) -> p g q", q=COL_AT)[:, :, 0:4]\
                .rearrange("p g (k j) -> p g k j", k=2)
            sums_twice = sums[:].unsqueeze(2).to_broadcast([P, 2 * T, 2])

            def sums_hi():
                return step(v.tensor_scalar(sum_parts[:, :, 0], sums_twice, SX / SW, None, ALU.mult))

            def sums_lo():
                return v.scalar_tensor_tensor(out=sum_parts[:, :, 1], in0=sums_twice, scalar=SX / SW,
                                              in1=sum_parts[:, :, 0], op0=ALU.mult, op1=ALU.subtract)

            def prologue():
                adjacencyT_lo(0, 1)
                adjacencyT_lo(1, 1)
                x_lo_part(1)
                relation_rows()
                xT_lo_part(1)
                adjacency_lo(1)
                sums_hi()
                dve.wait_ge(dve_step, steps[0])
                sums_lo().then_inc(s["sum_cols_done"], 1)
                prepare_weights()
                dve.wait_ge(dve_step, steps[0])
                v.sem_clear(dve_step)
                steps[0] = 0

            def iteration(i):
                c = Counts(dve, i)
                kept = 16 * c.n_c if isinstance(i, int) else dve.snap(i * 16 - 16)

                def x2_lo_part():
                    dve.wait_ge(s["x2_hi_done"], c.n_b)
                    v.tensor_tensor(x2_lo[:], x2[:], x2_hi[:], ALU.subtract).then_inc(s["x2_lo_done"], 1)

                def hand_on():
                    if c.again_a:
                        dve.wait_ge(s["agg_psum"], c.prev_a)
                    step(v.tensor_copy(bt_hi[:], at_hi[:]))
                    step(v.tensor_copy(bt_lo[:], at_lo[:]))
                    v.tensor_copy(sum_rows_b[:], sum_rows[:]).then_inc(s["bt_done"], 1)

                def skip_sum():
                    if c.again_a:
                        dve.wait_ge(s["y2_done"], c.prev_a)
                    for k in range(2):
                        bank = pa[:, k].rearrange("p (t h c) -> p t h c", t=2, h=2)
                        pair = slice(2 * k, 2 * k + 2)
                        ins = v.scalar_tensor_tensor(out=x1_skip[:, pair], in0=bank[:, :, 1], scalar=DOWN,
                                                     in1=x1[:, pair], op0=ALU.mult, op1=ALU.add)
                    ins.then_inc(s["gcn1_free"], 1)

                def rest_of_adjacencyT():
                    dve.wait_ge(at_hi_done[1], c.n_in)
                    dve.wait_ge(s["sum_psum"], c.prev_in)
                    hi_cols = sums_hi()
                    if c.has_b:
                        adjacencyT_lo(1, c.n_in)
                    dve.wait_ge(dve_step, hi_cols)
                    sums_lo().then_inc(s["sum_cols_done"], 1)

                def relation_max(t):
                    f = 2 if t % 2 == 0 else 0
                    seven = pa[:, f:f + 2].rearrange("p b n -> p (b n)")[:, 0:NREL * C]
                    dve.wait_ge(rel_psum[t], c.n_a)
                    v.tensor_reduce(rel_max[:, t], seven.rearrange("p (r c) -> p c r", r=NREL), AX_X, ALU.max)\
                        .then_inc(rel_read[t], 1)

                def kernel_tile(t):
                    dve.wait_ge(exp_done[t], c.n_c)
                    if t == 0:
                        dve.wait_ge(s["at_kept"], kept)
                    v.scalar_tensor_tensor(out=kern[:, t], in0=expd[:, t % 2], scalar=SE, in1=at_keep[:, t],
                                           op0=ALU.mult, op1=ALU.mult).then_inc(kern_done[t], 1)

                if c.has_b and not c.again_b:
                    layer3_biases()
                    weights_lo()
                if c.has_c:
                    dve.wait_ge(s["x3T_hi_done"], c.n_c)
                    v.tensor_tensor(x3T_lo[:], pb[:, 0], x3T_hi[:], ALU.subtract).then_inc(s["x3T_lo_done"], 1)
                if c.has_a:
                    dve.wait_ge(s["ax_hi_done"], c.n_a)
                    lo_from(ax_lo[:], pa[:, 0], ax_hi[:]).then_inc(s["ax_lo_done"], 1)
                if c.has_a and not c.made_early:
                    dve.wait_ge(s["atx_hi_done"], c.n_a)
                    lo_from(atx_lo[:], pa[:, 1], atx_hi[:]).then_inc(s["atx_lo_done"], 1)
                if c.has_a and not c.again_a:
                    gcn_rows()
                if c.has_c:
                    dve.wait_ge(s["feat_psum"], c.n_c)
                    pf = pb[:, 1, 0:4 * T].rearrange("p (t d) -> p t d", t=T)
                    v.tensor_scalar(feat[:, :, 0:3], pf[:, :, 0:3], 2.0 / (SX * SW), None, ALU.mult)\
                        .then_inc(s["feat_read"], 1)
                    dve.wait_ge(s["feat_read"], c.n_c)
                    step(v.scalar_tensor_tensor(out=feat_sq[:], in0=feat[:, :, 0:3], scalar=-0.25,
                                                in1=feat[:, :, 0:3], op0=ALU.mult, op1=ALU.mult))
                    dve.wait_ge(dve_step, steps[0])
                    step(v.tensor_reduce(feat[:, :, 3], feat_sq[:], AX_X, ALU.add))
                    dve.wait_ge(dve_step, steps[0])
                    step(v.tensor_copy(feat_parts[:, :, 0], feat[:]))
                    dve.wait_ge(dve_step, steps[0])
                    step(v.tensor_tensor(feat_rest[:], feat[:], feat_parts[:, :, 0], ALU.subtract))
                    dve.wait_ge(dve_step, steps[0])
                    step(v.tensor_copy(feat_parts[:, :, 1], feat_rest[:]))
                    dve.wait_ge(dve_step, steps[0])
                    step(v.tensor_tensor(feat_parts[:, :, 2], feat_rest[:], feat_parts[:, :, 1], ALU.subtract))
                    dve.wait_ge(dve_step, steps[0])
                    right = feat_cols[:, :, KD_RIGHT:KD_RIGHT + KD].rearrange("p t (a q) -> p t a q", a=3)
                    step(v.tensor_copy(right, feat_parts[:].rearrange("p t b d -> p t (b d)").unsqueeze(2)
                                       .to_broadcast([P, T, 3, 12])))
                    left = feat_cols[:, :, 0:KD].rearrange("p t (a b d) -> p t a b d", a=3, b=3)
                    for a in range(3):
                        ins = v.tensor_scalar(left[:, :, a, :, 0:3],
                                              feat_parts[:, :, a, 0:3].unsqueeze(2).to_broadcast([P, T, 3, 3]),
                                              0.5, None, ALU.mult)
                    ins.then_inc(s["feat_cols_done"], 1)
                if c.has_b:
                    dve.wait_ge(s["p2_hi_done"], c.n_b)
                    lo_from(p2_lo[:], pb[:, 0], p2_hi[:]).then_inc(s["p2_lo_done"], 1)
                if c.has_a:
                    relation_max(0)
                if c.has_c:
                    dve.wait_ge(s["featT_psum"], c.n_c)
                    v.tensor_copy(right_rows[:], pc[:, 0].bitcast(BF16)[KD_RIGHT:KD_RIGHT + KD, 0:N])\
                        .then_inc(s["right_done"], 1)
                if c.has_a:
                    relation_max(1)
                if c.has_b:
                    dve.wait_ge(s["relu2_done"], c.n_b)
                    v.scalar_tensor_tensor(out=gcn2_out[:], in0=tiles(pb[:, 1]), scalar=LRELU * DOWN,
                                           in1=relu_part[:], op0=ALU.mult, op1=ALU.add).then_inc(s["gcn2_done"], 1)
                if c.has_a:
                    relation_max(2)
                if c.has_c:
                    kernel_tile(0)
                if c.has_b:
                    dve.wait_ge(s["y2_done"], c.n_b)
                    norm_stats(1, y2, SX).then_inc(seed_done[1], 1)
                if c.has_a:
                    relation_max(3)
                if c.has_c:
                    kernel_tile(1)
                if c.has_a:
                    dve.wait_ge(s["x_bias_done"], c.n_a)
                    dve.wait_ge(rel_read[T - 1], c.n_a)
                    v.scalar_tensor_tensor(out=y1[:], in0=rel_max[:], scalar=1.0 / (SX * SW), in1=x_bias[:],
                                           op0=ALU.mult, op1=ALU.add).then_inc(s["y1_done"], 1)
                    dve.wait_ge(s["y1_done"], c.n_a)
                    norm_stats(0, y1, 1.0).then_inc(seed_done[0], 1)
                if c.filling:
                    x_lo_part(c.n_in)
                if c.filling and not c.early:
                    xT_lo_part(c.n_in)
                    x2_lo_part()
                    adjacency_lo(c.n_in)
                if c.early:
                    adjacency_lo(c.n_in)
                    tap_sums_lo()
                    xT_lo_part(c.n_in)
                if c.has_c:
                    kernel_tile(2)
                    kernel_tile(3)
                    dve.wait_ge(s["msg_psum"], c.n_c)
                    v.scalar_tensor_tensor(out=msg, in0=tiles(pc[:, 0]), scalar=DOWN,
                                           in1=msg_bias[:].unsqueeze(1).to_broadcast([P, T, C]),
                                           op0=ALU.mult, op1=ALU.add).then_inc(s["msg_sum_done"], 1)
                if c.has_b and not c.filling:
                    x2_lo_part()
                if c.has_c:
                    dve.wait_ge(s["x3T_done"], c.n_c)
                    even_psum, sum_psum, odd_psum = pc[:, 1, 0:HALF], pc[:, 1, HALF:N], pa[:, 3]
                    x3_parity = x3T[:].rearrange("p (u e) -> p e u", e=2)
                    dve.wait_ge(s["conv2_psum"], c.n_c)
                    even_first = step(v.scalar_tensor_tensor(out=conv_sum[:, 0], in0=even_psum, scalar=conv2_scale[:],
                                                             in1=x3_parity[:, 0], op0=ALU.mult, op1=ALU.add))
                    step(v.scalar_tensor_tensor(out=conv_sum[:, 1], in0=sum_psum, scalar=conv2_scale[:],
                                                in1=x3_parity[:, 1], op0=ALU.mult, op1=ALU.add))
                    dve.wait_ge(dve_step, steps[0])
                    step(v.scalar_tensor_tensor(out=conv_sum[:, 1], in0=even_psum, scalar=conv2_minus[:],
                                                in1=conv_sum[:, 1], op0=ALU.mult, op1=ALU.add))
                if c.has_in and c.has_c:
                    x_lo_part(c.n_in)
                    xT_lo_part(c.n_in)
                if c.has_c:
                    dve.wait_ge(s["conv2_odd_psum"], c.n_c)
                    dve.wait_ge(dve_step, even_first)
                    step(v.scalar_tensor_tensor(out=conv_sum[:, 0], in0=odd_psum[:, 0:HALF], scalar=conv2_scale[:],
                                                in1=conv_sum[:, 0], op0=ALU.mult, op1=ALU.add))
                    dve.wait_ge(dve_step, steps[0] - 1)
                    v.scalar_tensor_tensor(out=conv_sum[:, 1], in0=odd_psum[:, 1:HALF + 1], scalar=conv2_minus[:],
                                           in1=conv_sum[:, 1], op0=ALU.mult, op1=ALU.add)\
                        .then_inc(s["conv_sum_done"], 1)
                if c.has_a:
                    dve.wait_ge(s["x1_hi_done"], c.n_a)
                    v.tensor_tensor(x1_lo[:], x1[:], x1_hi[:], ALU.subtract).then_inc(s["x1_lo_done"], 1)
                if c.early:
                    dve.wait_ge(s["atx_hi_done"], c.n_in)
                    lo_from(atx_lo[:], pa[:, 1], atx_hi[:]).then_inc(s["atx_lo_done"], 1)
                if c.has_in and not c.filling:
                    adjacency_lo(c.n_in)
                if c.has_b:
                    dve.wait_ge(s["agg_hi_done"], c.n_b)
                    lo_from(agg_lo[:], pb[:, 0], agg_hi[:]).then_inc(s["agg_lo_done"], 1)
                if c.has_a:
                    hand_on()
                    dve.wait_ge(s["p1_hi_done"], c.n_a)
                    lo_from(p1_lo[:], pa[:, 2], p1_hi[:]).then_inc(s["p1_lo_done"], 1)
                if c.has_d:
                    dve.wait_ge(s["y4T_psum"], c.n_d)
                    norm_stats(3, tiles(pa[:, 3]), 2.0).then_inc(seed_done[3], 1)
                if c.has_in:
                    adjacencyT_lo(0, c.n_in)
                if c.has_in and not c.has_b:
                    adjacencyT_lo(1, c.n_in)
                if c.has_b:
                    dve.wait_ge(hid_hi_done, c.n_b)
                    for k in range(2):
                        ins = v.tensor_tensor(hid_lo[:, k], hid[:, k], hid_hi[:, k], ALU.subtract)
                    ins.then_inc(s["hid_lo_done"], 1)
                if c.has_c:
                    dve.wait_ge(s["nmp_hi_done"], c.n_c)
                    lo_from(nmp_lo[:], pc[:, 0], nmp_hi[:], 1.0 / SE).then_inc(s["nmp_lo_done"], 1)
                if c.has_a:
                    for k in range(2):
                        bank = pa[:, k].rearrange("p (t h c) -> p t h c", t=2, h=2)
                        pair = slice(2 * k, 2 * k + 2)
                        dve.wait_ge(relu1_done[k], c.n_a)
                        ins = v.scalar_tensor_tensor(out=g1[:, pair], in0=bank[:, :, 0], scalar=LRELU * DOWN,
                                                     in1=relu_part[:, pair], op0=ALU.mult, op1=ALU.add)
                    ins.then_inc(s["g1_done"], 1)
                if c.filling:
                    skip_sum()
                if c.has_in and not c.has_c:
                    rest_of_adjacencyT()
                if c.has_b:
                    dve.wait_ge(s["x2_bias_done"], c.n_b)
                    dve.wait_ge(s["gin_psum"], c.n_b)
                    v.scalar_tensor_tensor(out=y3[:], in0=tiles(pb[:, 1]), scalar=DOWN, in1=x2_bias[:],
                                           op0=ALU.mult, op1=ALU.add).then_inc(s["y3_done"], 1)
                if c.has_b:
                    dve.wait_ge(s["y3_done"], c.n_b)
                    norm_stats(2, y3, SX).then_inc(seed_done[2], 1)
                if c.has_in and c.has_c:
                    rest_of_adjacencyT()
                if c.has_c:
                    dve.wait_ge(s["hidden_done"], c.n_c)
                    dve.wait_ge(s["reset_done"], c.n_c)
                    step(v.scalar_tensor_tensor(out=hidden_n[:], in0=gates[:, 0], scalar=1.0, in1=hidden_n[:],
                                                op0=ALU.add, op1=ALU.mult))
                if c.has_a and not c.filling:
                    skip_sum()
                if c.has_c:
                    dve.wait_ge(s["input_psum"], c.n_c)
                    dve.wait_ge(dve_step, steps[0])
                    v.scalar_tensor_tensor(out=hidden_n[:], in0=hidden_n[:], scalar=0.5, in1=input_bank,
                                           op0=ALU.mult, op1=ALU.add).then_inc(s["n_pre_done"], 1)
                    dve.wait_ge(s["cand_done"], c.n_c)
                    dve.wait_ge(s["x3_true_done"], c.n_c)
                    step(v.tensor_tensor(x_minus, x3_true[:], cand[:], ALU.subtract))
                    step(v.tensor_tensor(x_plus, x3_true[:], cand[:], ALU.add))
                    dve.wait_ge(s["update_done"], c.n_c)
                    dve.wait_ge(dve_step, steps[0])
                    step(v.scalar_tensor_tensor(out=x_minus, in0=gates[:, 1], scalar=1.0, in1=x_minus,
                                                op0=ALU.add, op1=ALU.mult))
                    dve.wait_ge(dve_step, steps[0])
                    v.scalar_tensor_tensor(out=y4, in0=x_plus, scalar=2.0, in1=x_minus,
                                           op0=ALU.mult, op1=ALU.add).then_inc(s["y4_done"], 1)
                if steps[0]:
                    dve.wait_ge(dve_step, steps[0])
                    v.sem_clear(dve_step)
                    steps[0] = 0

            run(iteration, dve, prologue)

        @block.tensor
        def _(pe):
            def product(dst, left, right, start, stop):
                (lh, ll), (rh, rl) = left, right
                nc.tensor.matmul(dst, lh, rh, start=start, stop=False)
                nc.tensor.matmul(dst, lh, rl, start=False, stop=False)
                return nc.tensor.matmul(dst, ll, rh, start=False, stop=stop)

            def over_nodes(dst, left, right):
                for t in range(T):
                    last = product(dst, (left[0][:, t], left[1][:, t]), (right[0][:, t], right[1][:, t]),
                                   start=(t == 0), stop=t == T - 1)
                return last

            def nodes(pair, t):
                return pair[0][:, t * P:(t + 1) * P], pair[1][:, t * P:(t + 1) * P]

            A, AT, BT = (a_hi, a_lo), (at_hi, at_lo), (bt_hi, bt_lo)

            pe.wait_ge(s["edges_loaded"], 2 * 16)
            for r in range(NREL):
                nc.tensor.matmul(pc[:, r // 4, (r % 4) * C:(r % 4 + 1) * C], edge_f_sb[:, r],
                                 edge_w_sb[:, r], start=True, stop=True)\
                    .then_inc(s["edge_psum"], 1)
            def shift_products():
                pe.wait_ge(s["vectors_done"], 1)
                pe.wait_ge(s["w_front_loaded"], 16)
                a, b = WCOLS["gcn1"]
                nc.tensor.matmul(pb[:, 0, 0:2 * C], shift_bc[:, 0], w_raw[:, a:b], start=True, stop=True)
                a, b = WCOLS["gcn2"]
                nc.tensor.matmul(pb[:, 0, 2 * C:3 * C], shift_bc[:, 1], w_raw[:, a:b], start=True, stop=True)\
                    .then_inc(s["rank_psum"], 1)

            def iteration(i):
                c = Counts(pe, i)

                def adjacency_x():
                    pe.wait_ge(s["at_lo_done"], c.n_a)
                    pe.wait_ge(s["x_lo_done"], c.n_a)
                    if c.again_a:
                        pe.wait_ge(s["gcn1_free"], c.prev_a)
                    over_nodes(pa[:, 0], (x_hi, x_lo), AT).then_inc(s["ax_psum"], 1)
                    if not c.again_a:
                        shift_products()

                def adjacencyT_x():
                    if not c.made_early:
                        pe.wait_ge(s["a_lo_done"], c.n_a)
                        over_nodes(pa[:, 1], (x_hi, x_lo), A).then_inc(s["atx_psum"], 1)
                    pe.wait_ge(s["consts_set"], 10)
                    pe.wait_ge(s["sum_cols_done"], c.n_a)
                    nc.tensor.transpose(pa[:, 2].bitcast(F16)[:, 0:P], sum_cols[:], ident_h[:])\
                        .then_inc(s["sum_psum"], 1)

                def relations(t):
                    f = 2 if t % 2 == 0 else 0
                    if t == 0:
                        if c.again_c:
                            pe.wait_ge(s["conv_sum_done"], c.prev_c)
                        if c.again_d:
                            pe.wait_ge(s["result_done"], c.prev_d)
                        pe.wait_ge(s["sum_rows_done"], c.n_a)
                        pe.wait_ge(s["xT_lo_done"], c.n_a)
                        pe.wait_ge(s["ax_lo_done"], c.n_a)
                        pe.wait_ge(s["atx_lo_done"], c.n_a)
                    if t >= 2:
                        pe.wait_ge(rel_read[t - 2], c.n_a)
                    if t == 0 and not c.again_a:
                        pe.wait_ge(s["w_hi_done"], 1)
                        pe.wait_ge(s["ranks_done"], 1)
                    nc.tensor.matmul(pa[:, f], sum_rows[:], rank_rel[:, t, 0:4 * C], start=True, stop=False)
                    product(pa[:, f, 0:2 * C], nodes((ax_hi, ax_lo), t), W("rel", 0, 2 * C), False, False)
                    product(pa[:, f, 2 * C:4 * C], nodes((atx_hi, atx_lo), t), W("rel", 2 * C, 2 * C), False, True)
                    nc.tensor.matmul(pa[:, f + 1, 0:3 * C], sum_rows[:], rank_rel[:, t, 4 * C:], start=True,
                                     stop=False)
                    product(pa[:, f + 1, 0:3 * C], nodes((xT_hi, xT_lo), t), W("rel", 4 * C, 3 * C), False, True)\
                        .then_inc(rel_psum[t], 1)

                def next_adjacencyT_x():
                    pe.wait_ge(s["a_lo_done"], c.n_in)
                    pe.wait_ge(s["x_lo_done"], c.n_in)
                    pe.wait_ge(rel_read[T - 1], c.n_a)
                    over_nodes(pa[:, 1], (x_hi, x_lo), A).then_inc(s["atx_psum"], 1)

                def gcn_p1():
                    pe.wait_ge(s["x1_lo_done"], c.n_a)
                    over_nodes(pa[:, 2], (x1_hi, x1_lo), AT).then_inc(s["p1_psum"], 1)

                def gcn_first():
                    pe.wait_ge(s["p1_lo_done"], c.n_a)
                    if not c.again_a:
                        pe.wait_ge(s["ranks_done"], 2)
                    if c.early:
                        pe.wait_ge(s["atx_lo_done"], c.n_in)
                    for t in range(T):
                        dst = pa[:, t // 2, (t % 2) * 2 * C:(t % 2 + 1) * 2 * C]
                        nc.tensor.matmul(dst, sum_rows[:], rank_gcn[:, t, 0:2 * C], start=True, stop=False)
                        last = product(dst, nodes((p1_hi, p1_lo), t), W("gcn1"), False, True)
                        if t % 2:
                            last.then_inc(gcn1_psum[t // 2], 1)

                def gcn_p2():
                    pe.wait_ge(s["g1_lo_done"], c.n_b)
                    pe.wait_ge(s["bt_done"], c.n_b)
                    if c.has_c:
                        pe.wait_ge(s["x3T_done"], c.n_c)
                    over_nodes(pb[:, 0], (g1_hi, g1_lo), BT).then_inc(s["p2_psum"], 1)

                def gcn_second():
                    pe.wait_ge(s["p2_lo_done"], c.n_b)
                    if c.has_c:
                        pe.wait_ge(s["feat_read"], c.n_c)
                    for t in range(T):
                        dst = tiles(pb[:, 1])[:, t]
                        nc.tensor.matmul(dst, sum_rows_b[:], rank_gcn[:, t, 2 * C:], start=True, stop=False)
                        last = product(dst, nodes((p2_hi, p2_lo), t), W("gcn2"), False, True)
                    last.then_inc(s["gcn2_psum"], 1)

                def gin_aggregate():
                    pe.wait_ge(s["x2_lo_done"], c.n_b)
                    if c.has_c:
                        pe.wait_ge(exp_done[T - 1], c.n_c)
                    pe.wait_ge(s["diag_done"], c.n_b)
                    over_nodes(pb[:, 0], (x2_hi, x2_lo), BT).then_inc(s["agg_psum"], 1)

                def gin_hidden():
                    pe.wait_ge(s["agg_lo_done"], c.n_b)
                    if not c.again_b:
                        pe.wait_ge(s["ranks_done"], 3)
                        pe.wait_ge(s["w_lo_done"], 1)
                    for k in range(2):
                        product(pb[:, 1 - k], W("gin1", k * C, C), (agg_hi[:], agg_lo[:]), True, True)\
                            .then_inc(hid_psum[k], 1)

                def gin_out():
                    pe.wait_ge(s["hid_lo_done"], c.n_b)
                    for t in range(T):
                        dst = tiles(pb[:, 1])[:, t]
                        product(dst, nodes((hid_hi[:, 0], hid_lo[:, 0]), t), W("gin2", 0, C), True, False)
                        last = product(dst, nodes((hid_hi[:, 1], hid_lo[:, 1]), t), W("gin2", C, C), False, True)
                    last.then_inc(s["gin_psum"], 1)

                def transpose_x3():
                    pe.wait_ge(s["x3_done"], c.n_c)
                    if c.again_c:
                        pe.wait_ge(s["reset_done"], c.prev_c)
                    for t in range(T):
                        last = nc.tensor.transpose(pb[:, 0, t * P:(t + 1) * P], x3[:, t], ident_f[:])
                    last.then_inc(s["x3T_psum"], 1)

                def conv1():
                    pe.wait_ge(s["x3T_lo_done"], c.n_c)
                    if c.again_c:
                        pe.wait_ge(s["n_pre_done"], c.prev_c)
                    product(pc[:, 0], W("conv1"), (x3T_hi[:], x3T_lo[:]), True, True).then_inc(s["conv1_psum"], 1)

                def features():
                    if c.again_c:
                        pe.wait_ge(s["update_done"], c.prev_c)
                    for t in range(T):
                        dst = pb[:, 1, 4 * t:4 * t + 4]
                        nc.tensor.matmul(dst, ones2[:], rank_se[:], start=True, stop=False)
                        last = product(dst, nodes((x3T_hi, x3T_lo), t), W("se"), False, True)
                    last.then_inc(s["feat_psum"], 1)

                def feature_rows():
                    pe.wait_ge(s["feat_cols_done"], c.n_c)
                    pe.wait_ge(s["h1_done"], c.n_c)
                    for t in range(T):
                        last = nc.tensor.transpose(pc[:, 0].bitcast(BF16)[:, t * P:(t + 1) * P], feat_cols[:, t],
                                                   ident_b[:])
                    last.then_inc(s["featT_psum"], 1)

                def distances(t):
                    if t == 0:
                        pe.wait_ge(s["left_done"], c.n_c)
                        pe.wait_ge(s["right_done"], c.n_c)
                    if t == 1 and c.has_b:
                        pe.wait_ge(s["p2_lo_done"], c.n_b)
                    if t >= 2:
                        pe.wait_ge(exp_done[t - 2], c.n_c)
                    nc.tensor.matmul(dist_bank[t], left_rows[:, t * P:(t + 1) * P], right_rows[:], start=True,
                                     stop=True).then_inc(dist_psum[t], 1)

                def messages():
                    pe.wait_ge(exp_done[2], c.n_c)
                    for t in range(T):
                        dst = tiles(pc[:, 0])[:, t]
                        last = product(dst, nodes((x3T_hi, x3T_lo), t), W("msg"), True, True)
                    last.then_inc(s["msg_psum"], 1)

                def conv2_even(taps):
                    if taps[0] == 0:
                        pe.wait_ge(s["h1_lo_done"], c.n_c)
                    for j in taps:
                        product(pc[:, 1, 0:HALF], W("conv2", 2 * j * C, C),
                                (h1_hi[:, 0, j:j + HALF], h1_lo[:, 0, j:j + HALF]), j == 0, j == TAPS // 2)

                def conv2_sum(taps):
                    for j in taps:
                        weights_j = W("tap_sums", (j - 1) * C, C) if j else W("conv2", 0, C)
                        last = product(pc[:, 1, HALF:N], weights_j, (h1_hi[:, 2, j:j + HALF], h1_lo[:, 2, j:j + HALF]),
                                       j == 0, j == TAPS // 2)
                    if taps[-1] == TAPS // 2:
                        last.then_inc(s["conv2_psum"], 1)

                def conv2_odd(taps):
                    if taps[0] == 1 and c.has_a:
                        pe.wait_ge(rel_read[2], c.n_a)
                    for j in taps:
                        last = product(pa[:, 3, 0:HALF + 1], W("conv2", (2 * j - 1) * C, C),
                                       (h1_hi[:, 1, j - 1:j + HALF], h1_lo[:, 1, j - 1:j + HALF]),
                                       j == 1, j == TAPS // 2)
                    if taps[-1] == TAPS // 2:
                        last.then_inc(s["conv2_odd_psum"], 1)

                def nmp():
                    pe.wait_ge(s["msg_lo_done"], c.n_c)
                    pe.wait_ge(s["kern_lo_done"], c.n_c)
                    over_nodes(pc[:, 0], (msg_hi, msg_lo), (kern_hi, kern_lo)).then_inc(s["nmp_psum"], 1)

                x3_pair, xc_pair, nmp_pair = (x3T_hi[:], x3T_lo[:]), (xc_hi[:], xc_lo[:]), (nmp_hi[:], nmp_lo[:])

                def gru_hidden():
                    pe.wait_ge(s["conv_sum_done"], c.n_c)
                    product(hidden_bank, W("hh", 2 * C, C), x3_pair, True, True).then_inc(s["hidden_psum"], 1)

                def gru_gates():
                    if c.has_b:
                        pe.wait_ge(hid_done[1], c.n_b)
                    product(reset_bank, W("hh", 0, C), x3_pair, True, False)
                    pe.wait_ge(s["xc_lo_done"], c.n_c)
                    product(reset_bank, W("ih_conv", 0, C), xc_pair, False, False)
                    pe.wait_ge(s["nmp_lo_done"], c.n_c)
                    product(reset_bank, W("ih_nmp", 0, C), nmp_pair, False, True).then_inc(s["reset_psum"], 1)
                    product(input_bank, W("ih_conv", 2 * C, C), xc_pair, True, False)
                    product(input_bank, W("ih_nmp", 2 * C, C), nmp_pair, False, True).then_inc(s["input_psum"], 1)
                    if c.has_b:
                        pe.wait_ge(s["y3_done"], c.n_b)
                    product(update_bank, W("hh", C, C), x3_pair, True, False)
                    product(update_bank, W("ih_conv", C, C), xc_pair, False, False)
                    product(update_bank, W("ih_nmp", C, C), nmp_pair, False, True).then_inc(s["update_psum"], 1)

                def transpose_y4():
                    pe.wait_ge(s["y4_done"], c.n_d)
                    if c.has_c:
                        pe.wait_ge(s["conv_sum_done"], c.n_c)
                    if c.again_d:
                        pe.wait_ge(s["result_done"], c.prev_d)
                    for t in range(T):
                        last = nc.tensor.transpose(pa[:, 3, t * P:(t + 1) * P], y4[:, t * P:(t + 1) * P], ident_f[:])
                    last.then_inc(s["y4T_psum"], 1)

                order = [("a", adjacency_x), ("c", transpose_x3), ("a", adjacencyT_x), ("c", conv1), ("c", features),
                         ("b", gcn_p2), ("a", relations, 0), ("c", feature_rows), ("a", relations, 1),
                         ("b", gcn_second), ("a", relations, 2), ("c", distances, 0), ("c", distances, 1),
                         ("a", relations, 3), ("c", conv2_even, range(0, 6)), ("c", distances, 2),
                         ("c", distances, 3), ("c", conv2_even, range(6, 9)), ("c", messages),
                         ("c", conv2_sum, range(0, 9)), ("c", conv2_odd, range(1, 9)), ("b", gin_aggregate),
                         ("a", gcn_p1), ("d", transpose_y4), ("b", gin_hidden), ("c", nmp), ("a", gcn_first),
                         ("b", gin_out), ("c", gru_hidden), ("c", gru_gates)]
                if c.early:
                    order.insert(order.index(("a", relations, 3)) + 1, ("a", next_adjacencyT_x))
                present = {"a": c.has_a, "b": c.has_b, "c": c.has_c, "d": c.has_d}
                for step_name, stage, *args in order:
                    if present[step_name]:
                        stage(*args)

            run(iteration, pe)


def kernel(**inputs):
    import numpy as _np
    import concourse.bacc as _bacc
    from concourse import mybir as _mybir
    from concourse.bass_utils import run_bass_kernel_spmd as _run

    a = {k: _np.ascontiguousarray(v) for k, v in inputs.items()}
    w_rel, w_ih, w_hh = a["L0_gnn_W"], a["L3_gnn_w_ih"], a["L3_gnn_w_hh"]
    ih_t = w_ih.T
    w_se = _np.concatenate([a["L3_gnn_w_se"].T, _np.zeros((C, 1), _np.float32)], axis=1)
    pieces = [w_rel[BLOCKS, :C].transpose(1, 0, 2).reshape(C, NREL * C),
              a["L1_gnn_w1"], a["L1_gnn_w_skip"], a["L1_gnn_w2"], a["L2_gnn_W1"],
              a["L2_gnn_W2"].reshape(2, C, C).transpose(1, 0, 2).reshape(C, 2 * C),
              a["L3_gnn_conv1_w"][:, :, 0].T,
              a["L3_gnn_conv2_w"].transpose(1, 2, 0).reshape(C, TAPS * C),
              a["L3_gnn_w_msg"].T, w_se, ih_t[:C], ih_t[C:], w_hh.T]
    weights = _np.ascontiguousarray(_np.concatenate(pieces, axis=1))
    bias = _np.concatenate([a["L1_gnn_b1"], a["L1_gnn_b_skip"], a["L1_gnn_b2"],
                            a["L3_gnn_b_msg"], a["L3_gnn_b_se"], _np.zeros(1, _np.float32)])
    norms = ["L1_gnn_bn1_", "L1_gnn_bn2_", "L3_gnn_bn1_", "L3_gnn_bn2_"]
    vecs = [a[p + (q if "L1" in p else q[0])] for q in ("var", "gamma", "beta", "mean") for p in norms]
    vecs += [a["L2_gnn_b1"][:C], a["L2_gnn_b1"][C:], _np.broadcast_to(a["L2_gnn_eps"], (C,))]
    vecs += [a["L3_gnn_b_ih"][k * C:(k + 1) * C] for k in range(3)]
    vecs += [a["L3_gnn_b_hh"][k * C:(k + 1) * C] for k in range(3)]
    arrays = {
        "x": a["x"],
        "xT": _np.ascontiguousarray(a["x"].transpose(0, 2, 1)),
        "adj": a["adj"],
        "adjT": _np.ascontiguousarray(a["adj"].transpose(0, 2, 1)),
        "weights": weights,
        "edge_w": _np.ascontiguousarray(w_rel[BLOCKS, C:].transpose(1, 0, 2)),
        "edge_f": _np.ascontiguousarray(_np.broadcast_to(a["L0_gnn_W_edges"][BLOCKS].T[:, :, None], (REL, NREL, P))),
        "bias_rows": _np.ascontiguousarray(_np.broadcast_to(bias, (P, NB))),
        "vecs": _np.ascontiguousarray(_np.stack(vecs, axis=1)),
        "gin_b2": _np.ascontiguousarray(_np.broadcast_to(a["L2_gnn_b2"], (P, C))),
        "rel_b": _np.ascontiguousarray(a["L0_gnn_b"].reshape(T, P, C).transpose(1, 0, 2)),
        "ident": _np.eye(P, dtype=_np.float32),
        "masks": row_masks(),
        "bn_eps": _np.ascontiguousarray(_np.broadcast_to(_np.array([1e-3, 1e-3, 1e-5, 1e-5], _np.float32), (P, 4))),
    }
    nc = _bacc.Bacc("TRN2", target_bir_lowering=False, num_devices=1)
    feeds, args = {}, []
    for name, value in arrays.items():
        feeds[f"in_{name}_dram"] = value
        args.append(nc.dram_tensor(f"in_{name}_dram", value.shape, _mybir.dt.from_np(value.dtype),
                                   kind="ExternalInput").ap())
    args.append(nc.dram_tensor("out_dram", (B, N, C), _mybir.dt.float32, kind="ExternalOutput").ap())
    adj_resnorm(nc, *args)
    r = _run(nc, [feeds], core_ids=[0])
    return r.results[0]["out_dram"]
```
